# Optimizing a Trainium2 kernel written in Bass

```python
import numpy as np
import jax
import jax.numpy as jnp

def _softmax(x, axis=-1):
    return jax.nn.softmax(x, axis=axis)

def _gelu(x):
    return jax.nn.gelu(x, approximate=True)

def _silu(x):
    return jax.nn.silu(x)

def _sigmoid(x):
    return jax.nn.sigmoid(x)

def _layernorm(x, axis=-1, eps=1e-05):
    m = jnp.mean(x, axis=axis, keepdims=True)
    v = jnp.var(x, axis=axis, keepdims=True)
    return (x - m) / jnp.sqrt(v + eps)

def _scatter_add(tgt, idx, src, axis=0):
    return tgt.at[idx].add(src)

def _segment_sum(src, seg, n):
    return jax.ops.segment_sum(src, seg, n)
kernel_name = 'mk_conv_attn_hybrid_d2_conv_nhwc512_r4_eab28d'

def setup_inputs(seed: int=0):
    np.random.seed(seed)
    _w = jnp.asarray

    def _rec_inputs():
        import jax
        import jax.numpy as jnp
        _gk = jax.random.key(seed)
        x = -0.0003929 + 0.9999 * jax.random.normal(jax.random.fold_in(_gk, 1), (8, 16, 16, 128), jnp.float32)
        return x
    x = _rec_inputs()

    def _L0_conv_setup():
        import jax, jax.numpy as jnp
        import numpy as np
        HEAD = 8
        AGENT = 16
        DIM = 128

        def _heads(t, head=HEAD):
            b, n, c = t.shape
            return t.reshape(b, n, head, c // head).transpose(0, 2, 1, 3)

        def _attn(q, k, v, pe, scale):
            s = jax.nn.softmax(jnp.einsum('bhnd,bhmd->bhnm', q, k) * scale, axis=-1) + pe
            o = jnp.einsum('bhnm,bhmd->bhnd', s, v)
            b, h, n, d = o.shape
            return o.transpose(0, 2, 1, 3).reshape(b, n, h * d)

        def _mlp(x, w1, b1, w2, b2):
            return jax.nn.silu(x @ w1 + b1) @ w2 + b2
        key = jax.random.key(seed)
        ks = jax.random.split(key, 32)
        d = DIM
        inp = {'x': jax.random.normal(ks[0], (8, 16, 16, d), jnp.float32), 'learnable_q': jax.random.normal(ks[1], (1, AGENT, d), jnp.float32) * 0.02, 'learnable_kv': jax.random.normal(ks[2], (1, AGENT, d), jnp.float32) * 0.02, 'pe1': jax.random.normal(ks[3], (1, HEAD, 1, AGENT), jnp.float32) * 0.02, 'pe2': jax.random.normal(ks[4], (1, HEAD, AGENT, 1), jnp.float32) * 0.02, 'w_q': jax.random.normal(ks[5], (d, d), jnp.float32) * d ** (-0.5), 'b_q': jax.random.normal(ks[6], (d,), jnp.float32) * 0.02, 'w_kvx': jax.random.normal(ks[7], (d, 2 * d), jnp.float32) * d ** (-0.5), 'b_kvx': jax.random.normal(ks[8], (2 * d,), jnp.float32) * 0.02, 'w_kvy': jax.random.normal(ks[9], (d, 2 * d), jnp.float32) * d ** (-0.5), 'b_kvy': jax.random.normal(ks[10], (2 * d,), jnp.float32) * 0.02, 'w_q2': jax.random.normal(ks[11], (d, d), jnp.float32) * d ** (-0.5), 'b_q2': jax.random.normal(ks[12], (d,), jnp.float32) * 0.02, 'f1w1': jax.random.normal(ks[13], (d, d), jnp.float32) * d ** (-0.5), 'f1b1': jax.random.normal(ks[14], (d,), jnp.float32) * 0.02, 'f1w2': jax.random.normal(ks[15], (d, d), jnp.float32) * d ** (-0.5), 'f1b2': jax.random.normal(ks[16], (d,), jnp.float32) * 0.02, 'f2w1': jax.random.normal(ks[17], (d, d), jnp.float32) * d ** (-0.5), 'f2b1': jax.random.normal(ks[18], (d,), jnp.float32) * 0.02, 'f2w2': jax.random.normal(ks[19], (d, d), jnp.float32) * d ** (-0.5), 'f2b2': jax.random.normal(ks[20], (d,), jnp.float32) * 0.02}
        return inp
    _L0_conv_all = _L0_conv_setup()
    _L0_conv_in = {k: v for k, v in _L0_conv_all.items() if k in ('learnable_q', 'learnable_kv', 'pe1', 'pe2', 'w_q', 'b_q', 'w_kvx', 'b_kvx', 'w_kvy', 'b_kvy', 'w_q2', 'b_q2', 'f1w1', 'f1b1', 'f1w2', 'f1b2', 'f2w1', 'f2b1', 'f2w2', 'f2b2')}
    del _L0_conv_all

    def _L1_attn_setup():
        import jax, jax.numpy as jnp
        import numpy as np
        N_HEADS = 8
        D_K = 16
        NEG = 1000000000.0
        key = jax.random.key(seed)
        k1, k2, k3 = jax.random.split(key, 3)
        B, L, C = (4, 512, 128)
        x = jax.random.normal(k1, (B, L, C), dtype=jnp.float32)
        W_in = jax.random.normal(k2, (C, N_HEADS * D_K * 3), dtype=jnp.float32) * C ** (-0.5)
        b_in = jnp.zeros((N_HEADS * D_K * 3,), dtype=jnp.float32)
        W_out = jax.random.normal(k3, (N_HEADS * D_K, C), dtype=jnp.float32) * (N_HEADS * D_K) ** (-0.5)
        b_out = jnp.zeros((C,), dtype=jnp.float32)
        return {'x': x, 'W_in': W_in, 'b_in': b_in, 'W_out': W_out, 'b_out': b_out}
    _L1_attn_all = _L1_attn_setup()
    _L1_attn_in = {k: v for k, v in _L1_attn_all.items() if k in ('W_in', 'b_in', 'W_out', 'b_out')}
    del _L1_attn_all

    def _L1_ffn_setup():
        import jax, jax.numpy as jnp
        import numpy as np
        TOP_K = 2
        key = jax.random.key(seed)
        ks = jax.random.split(key, 6)
        B, T, C, E, H = (4, 1024, 128, 8, 512)
        x = jax.random.normal(ks[0], (B, T, C), dtype=jnp.float32)
        W_router = jax.random.normal(ks[1], (C, E), dtype=jnp.float32) * 0.02
        W1 = jax.random.normal(ks[2], (E, C, H), dtype=jnp.float32) * 0.02
        b1 = jnp.zeros((E, H), dtype=jnp.float32)
        W2 = jax.random.normal(ks[3], (E, H, C), dtype=jnp.float32) * 0.02
        b2 = jnp.zeros((E, C), dtype=jnp.float32)
        return {'x': x, 'W_router': W_router, 'W1': W1, 'b1': b1, 'W2': W2, 'b2': b2}
    _L1_ffn_all = _L1_ffn_setup()
    _L1_ffn_in = {k: v for k, v in _L1_ffn_all.items() if k in ('W_router', 'W1', 'b1', 'W2', 'b2')}
    del _L1_ffn_all
    return {'x': x, 'L0_conv_learnable_q': _L0_conv_in['learnable_q'], 'L0_conv_learnable_kv': _L0_conv_in['learnable_kv'], 'L0_conv_pe1': _L0_conv_in['pe1'], 'L0_conv_pe2': _L0_conv_in['pe2'], 'L0_conv_w_q': _L0_conv_in['w_q'], 'L0_conv_b_q': _L0_conv_in['b_q'], 'L0_conv_w_kvx': _L0_conv_in['w_kvx'], 'L0_conv_b_kvx': _L0_conv_in['b_kvx'], 'L0_conv_w_kvy': _L0_conv_in['w_kvy'], 'L0_conv_b_kvy': _L0_conv_in['b_kvy'], 'L0_conv_w_q2': _L0_conv_in['w_q2'], 'L0_conv_b_q2': _L0_conv_in['b_q2'], 'L0_conv_f1w1': _L0_conv_in['f1w1'], 'L0_conv_f1b1': _L0_conv_in['f1b1'], 'L0_conv_f1w2': _L0_conv_in['f1w2'], 'L0_conv_f1b2': _L0_conv_in['f1b2'], 'L0_conv_f2w1': _L0_conv_in['f2w1'], 'L0_conv_f2b1': _L0_conv_in['f2b1'], 'L0_conv_f2w2': _L0_conv_in['f2w2'], 'L0_conv_f2b2': _L0_conv_in['f2b2'], 'L1_attn_W_in': _L1_attn_in['W_in'], 'L1_attn_b_in': _L1_attn_in['b_in'], 'L1_attn_W_out': _L1_attn_in['W_out'], 'L1_attn_b_out': _L1_attn_in['b_out'], 'L1_ffn_W_router': _L1_ffn_in['W_router'], 'L1_ffn_W1': _L1_ffn_in['W1'], 'L1_ffn_b1': _L1_ffn_in['b1'], 'L1_ffn_W2': _L1_ffn_in['W2'], 'L1_ffn_b2': _L1_ffn_in['b2']}

def reference(x, L0_conv_learnable_q, L0_conv_learnable_kv, L0_conv_pe1, L0_conv_pe2, L0_conv_w_q, L0_conv_b_q, L0_conv_w_kvx, L0_conv_b_kvx, L0_conv_w_kvy, L0_conv_b_kvy, L0_conv_w_q2, L0_conv_b_q2, L0_conv_f1w1, L0_conv_f1b1, L0_conv_f1w2, L0_conv_f1b2, L0_conv_f2w1, L0_conv_f2b1, L0_conv_f2w2, L0_conv_f2b2, L1_attn_W_in, L1_attn_b_in, L1_attn_W_out, L1_attn_b_out, L1_ffn_W_router, L1_ffn_W1, L1_ffn_b1, L1_ffn_W2, L1_ffn_b2):
    import jax
    import jax.numpy as jnp

    def _L0_conv_ref(x, learnable_q, learnable_kv, pe1, pe2, w_q, b_q, w_kvx, b_kvx, w_kvy, b_kvy, w_q2, b_q2, f1w1, f1b1, f1w2, f1b2, f2w1, f2b1, f2w2, f2b2):
        import jax, jax.numpy as jnp
        import numpy as np
        HEAD = 8
        AGENT = 16
        DIM = 128

        def _heads(t, head=HEAD):
            b, n, c = t.shape
            return t.reshape(b, n, head, c // head).transpose(0, 2, 1, 3)

        def _attn(q, k, v, pe, scale):
            s = jax.nn.softmax(jnp.einsum('bhnd,bhmd->bhnm', q, k) * scale, axis=-1) + pe
            o = jnp.einsum('bhnm,bhmd->bhnd', s, v)
            b, h, n, d = o.shape
            return o.transpose(0, 2, 1, 3).reshape(b, n, h * d)

        def _mlp(x, w1, b1, w2, b2):
            return jax.nn.silu(x @ w1 + b1) @ w2 + b2
        b, h, w, c = x.shape
        d = c // HEAD
        scale = d ** (-0.5)
        xf = x.reshape(b, h * w, c)
        q = _heads(xf @ w_q2 + b_q2)
        kv = jnp.broadcast_to(learnable_kv, (b, AGENT, c)) @ w_kvy + b_kvy
        k, v = jnp.split(kv, 2, axis=-1)
        out = _attn(q, _heads(k), _heads(v), pe1, scale)
        out = _mlp(out, f1w1, f1b1, f1w2, f1b2) + xf
        mskip = out
        q2 = _heads(jnp.broadcast_to(learnable_q, (b, AGENT, c)) @ w_q + b_q)
        kv = out @ w_kvx + b_kvx
        k, v = jnp.split(kv, 2, axis=-1)
        fin = _attn(q2, _heads(k), _heads(v), pe2, scale)
        fin = _mlp(fin, f2w1, f2b1, f2w2, f2b2)
        s = int(AGENT ** 0.5)
        fin = fin.reshape(b, s, s, c)
        fin = jnp.repeat(jnp.repeat(fin, h // s, axis=1), w // s, axis=2)
        return fin + mskip.reshape(b, h, w, c) + x

    def _L1_attn_ref(x, W_in, b_in, W_out, b_out):
        import jax, jax.numpy as jnp
        import numpy as np
        N_HEADS = 8
        D_K = 16
        NEG = 1000000000.0
        B, L, C = x.shape
        H, Dk = (N_HEADS, D_K)
        scale = Dk ** (-0.5)
        qkv = x @ W_in + b_in
        qkv = qkv.reshape(B, L, H, 3 * Dk)
        q, k, v = jnp.split(qkv, 3, axis=-1)
        attn = jnp.einsum('bihd,bjhd->bijh', q, k) * scale
        mask = jnp.tril(jnp.ones((L, L), dtype=x.dtype))[None, :, :, None]
        attn = attn * mask - NEG * (1.0 - mask)
        attn = jax.nn.softmax(attn, axis=2)
        res = jnp.einsum('bijh,bjhd->bihd', attn, v)
        res = res.reshape(B, L, H * Dk)
        res = res @ W_out + b_out
        return res + x

    def _L1_ffn_ref(x, W_router, W1, b1, W2, b2):
        import jax, jax.numpy as jnp
        import numpy as np
        TOP_K = 2
        B, T, C = x.shape
        E = W_router.shape[1]
        x_flat = x.reshape(B * T, C)
        logits = x_flat @ W_router
        probs = jax.nn.softmax(logits, axis=-1)
        topk_p, topk_i = jax.lax.top_k(probs, TOP_K)
        topk_p = topk_p / topk_p.sum(axis=-1, keepdims=True)
        combine = (jax.nn.one_hot(topk_i, E, dtype=x_flat.dtype) * topk_p[..., None]).sum(axis=1)
        out = jnp.zeros_like(x_flat)
        for e in range(E):
            h = jax.nn.relu(x_flat @ W1[e] + b1[e])
            y = h @ W2[e] + b2[e]
            out = out + combine[:, e:e + 1] * y
        return out.reshape(B, T, C)

    def _gn(v, G=32, eps=1e-05):
        B_, H_, W_, C_ = v.shape
        g = v.reshape(B_, H_, W_, G, C_ // G)
        m = jnp.mean(g, axis=(1, 2, 4), keepdims=True)
        s = jnp.var(g, axis=(1, 2, 4), keepdims=True)
        return ((g - m) / jnp.sqrt(s + eps)).reshape(v.shape)

    def _ln_c(v, eps=1e-06):
        m = jnp.mean(v, axis=-1, keepdims=True)
        s = jnp.var(v, axis=-1, keepdims=True)
        return (v - m) / jnp.sqrt(s + eps)

    def _ln_t(v, eps=1e-05):
        m = jnp.mean(v, axis=-1, keepdims=True)
        s = jnp.var(v, axis=-1, keepdims=True)
        return (v - m) / jnp.sqrt(s + eps)

    def _to_tokens(v):
        B_, H_, W_, C_ = v.shape
        return v.reshape(B_, H_ * W_, C_)

    def _from_tokens(t, like):
        return t.reshape(like.shape)
    x = x + _L0_conv_ref(_gn(x), L0_conv_learnable_q, L0_conv_learnable_kv, L0_conv_pe1, L0_conv_pe2, L0_conv_w_q, L0_conv_b_q, L0_conv_w_kvx, L0_conv_b_kvx, L0_conv_w_kvy, L0_conv_b_kvy, L0_conv_w_q2, L0_conv_b_q2, L0_conv_f1w1, L0_conv_f1b1, L0_conv_f1w2, L0_conv_f1b2, L0_conv_f2w1, L0_conv_f2b1, L0_conv_f2w2, L0_conv_f2b2)
    t = _to_tokens(x)
    t = t + _L1_attn_ref(_ln_t(t), L1_attn_W_in, L1_attn_b_in, L1_attn_W_out, L1_attn_b_out)
    t = t + _L1_ffn_ref(_ln_t(t), L1_ffn_W_router, L1_ffn_W1, L1_ffn_b1, L1_ffn_W2, L1_ffn_b2)
    x = _from_tokens(t, x)
    return x

_drawn_inputs = setup_inputs


def setup_inputs(seed=0):
    import zlib

    import numpy as np

    out = dict(_drawn_inputs(seed))
    spreads = {'L1_attn_b_in': (0.0, 2.0),
     'L1_attn_b_out': (0.0, 2.0),
     'L1_ffn_b1': (0.0, 2.0),
     'L1_ffn_b2': (0.0, 2.0)}
    factors = {'L0_conv_learnable_q': 8.0,
     'L0_conv_learnable_kv': 8.0,
     'L0_conv_pe1': 8.0,
     'L0_conv_w_q': 8.0,
     'L0_conv_b_q': 8.0,
     'L0_conv_b_kvx': 26.856,
     'L0_conv_w_kvy': 8.0,
     'L0_conv_b_kvy': 5.142,
     'L0_conv_w_q2': 8.0,
     'L0_conv_b_q2': 8.0,
     'L0_conv_f1w1': 5.454,
     'L0_conv_f1b1': 19.097,
     'L0_conv_f1w2': 3.858,
     'L0_conv_f1b2': 23.936,
     'L0_conv_f2b1': 64.0,
     'L0_conv_f2b2': 63.736,
     'L1_ffn_W_router': 9.264,
     'L1_ffn_W1': 21.937,
     'L1_ffn_W2': 12.592,
     'L1_attn_W_in': 5.345,
     'L1_attn_W_out': 5.623}
    for name, (base, spread) in spreads.items():
        noise = np.random.default_rng([zlib.crc32(name.encode()), seed]).standard_normal(out[name].shape)
        drawn = base * np.exp(spread * noise) if base else spread * noise
        out[name] = jnp.asarray(drawn.astype(out[name].dtype))
    for name, factor in factors.items():
        out[name] = (out[name] * factor).astype(out[name].dtype)
    return out
```

```python
from contextlib import ExitStack

import concourse.bass as bass
from concourse import mybir

F32 = mybir.dt.float32
F32R = mybir.dt.float32r
BF16 = mybir.dt.bfloat16
U32 = mybir.dt.uint32
ALU = mybir.AluOpType
ACT = mybir.ActivationFunctionType
AX = mybir.AxisListType

P = 128
IMAGES = 8
SIDE = 16
TOK = SIDE * SIDE
TILES = TOK // P
C = 128
HEADS = 8
DK = C // HEADS
AGENTS = 16
CELL = 4
EXPERTS = 8
HID = 512
HB = HID // P
GROUP = 4
SCALE = DK ** -0.5
SLOTS = 17
TAIL = 11
VSTEP = P + DK
LOW = 80.0

C_ID = 0
C_GRP = C_ID + P
C_CAUSAL = C_GRP + P
C_BD = C_CAUSAL + P
C_BDS = C_BD + HEADS
C_IOTA = C_BDS + HEADS
C_POW = C_IOTA + EXPERTS
C_SEL = C_POW + 2
C_N = C_SEL + EXPERTS * P

W_KVYK, W_KVYV, W_Q, W_Q2T, W_F1W1, W_KT, W_F1W2, W_V, W_F2W1, W_F2W2, W_AQ, W_AK, W_AV, W_AO = range(14)
W_N = 14
(B_KYK, B_KYV, B_Q, B_PE1, B_PE2, B_F1B1, B_F1B2, B_F2B1, B_F2B2, B_AQ, B_AK, B_Q2) = range(12)
B_N = 12
R_BV, R_BAV, R_BO = range(3)
R_N = 3


class Signal:

    def __init__(self, ctx, nc, name, per=1):
        self.sem = ctx.enter_context(nc.semaphore(name))
        self.per = per

    def nth(self, i, k=1):
        return i * self.per + k

    def before(self, i):
        return i * self.per


def first(i):
    return isinstance(i, int) and i == 0


def hybrid_block(nc, xT, consts, weights, cols, rows, agents, w_router, w1, b1, w2, b2, out):
    ctx = ExitStack()
    with ctx:
        def sb(name, shape, dt=F32):
            return ctx.enter_context(nc.sbuf_tensor(name, shape, dt))

        def sig(name, per=1):
            return Signal(ctx, nc, name, per)

        x_all = sb("x_all", [P, IMAGES * TOK])
        cst = sb("cst", [P, C_N])
        W = sb("W", [P, W_N, P])
        col = sb("col", [P, B_N])
        row = sb("row", [P, R_N, P])
        agt = sb("agt", [P, 2, AGENTS])
        wr = sb("wr", [P, EXPERTS])
        w1raw = sb("w1raw", [P, EXPERTS, HID])
        w1hi = sb("w1hi", [P, EXPERTS, HID], F32R)
        w1lo = sb("w1lo", [P, EXPERTS, HID], F32R)
        w2s = sb("w2s", [P, EXPERTS, HB, C])
        b1s = sb("b1s", [P, EXPERTS, HB])
        b2s = sb("b2s", [P, EXPERTS])
        ident = cst[:, C_ID:C_ID + P]
        grp = cst[:, C_GRP:C_GRP + P]
        bd = cst[:, C_BD:C_BD + HEADS]
        bds = cst[:, C_BDS:C_BDS + HEADS]
        iota = cst[:, C_IOTA:C_IOTA + EXPERTS]
        power = cst[:, C_POW:C_POW + 2]
        identb = sb("identb", [P, P], BF16)
        causalb = sb("causalb", [P, P], BF16)
        selr = sb("selr", [P, EXPERTS, P], F32R)

        gst = sb("gst", [P, IMAGES, 6])
        gmv = sb("gmv", [P, IMAGES, 2])
        gmean = sb("gmean", [P, IMAGES])
        gdev = sb("gdev", [P, IMAGES])
        gvar = sb("gvar", [P, IMAGES])
        gn = sb("gn", [P, IMAGES, 2])
        kvq = sb("kvq", [P, 3, AGENTS])
        kvqd = sb("kvqd", [P, 3, HEADS, AGENTS])
        bq2b = sb("bq2b", [P, P])
        fold = sb("fold", [P, 4, P])
        m1, c1, m2, mkq = (fold[:, n, :] for n in range(4))
        zb = sb("zb", [P, 1])

        gni = sb("gni", [P, 2])
        xg = sb("xg", [P, TOK])
        xx = sb("xx", [P, TOK])
        s1 = sb("s1", [P, TILES, P])
        s1m = sb("s1m", [P, TILES * HEADS])
        s1c = sb("s1c", [P, TILES, P])
        e1 = sb("e1", [P, TILES, P])
        e1s = sb("e1s", [P, TILES * HEADS])
        e1r = sb("e1r", [P, TILES * HEADS])
        p1 = sb("p1", [P, TILES, P])
        p1T = sb("p1T", [P, TOK])
        ez = sb("ez", [P, TOK])
        za = sb("za", [P, TOK])
        zr = sb("zr", [P, TOK])
        zc = sb("zc", [P, TOK])
        yc = sb("yc", [P, AGENTS])
        zs = sb("zs", [P, TOK])
        oT = sb("oT", [P, TOK])
        base = sb("base", [P, TOK])
        s2m = sb("s2m", [P, 1])
        s2s = sb("s2s", [P, 1])
        s2r = sb("s2r", [P, 1])
        e2 = sb("e2", [P, TOK])
        p2 = sb("p2", [P, TOK])
        p2T = sb("p2T", [P, TILES, P])
        vx = sb("vx", [P, TILES, P])
        fm = sb("fm", [P, HEADS, AGENTS])
        fin = sb("fin", [P, AGENTS])
        ey = sb("ey", [P, AGENTS])
        ya = sb("ya", [P, AGENTS])
        yr = sb("yr", [P, AGENTS])
        ys = sb("ys", [P, AGENTS])
        fe = sb("fe", [P, AGENTS, CELL])
        x1T = sb("x1T", [P, TOK])

        lst = sb("lst", [P, TILES, 6])
        lmv = sb("lmv", [P, TILES, 2])
        lrs = sb("lrs", [P, TILES])
        lve = sb("lve", [P, TILES])
        ln1 = sb("ln1", [P, TILES, P])
        xl = sb("xl", [P, TILES, P])
        tb = sb("tb", [P, TILES, P])
        ln1T = sb("ln1T", [P, TOK])
        qT = sb("qT", [P, TOK])
        kT = sb("kT", [P, TOK])
        kz = sb("kz", [P, HEADS, TOK])
        vz = sb("vz", [P, TILES, HEADS * VSTEP])
        nm = sb("nm", [P, 2, 2])
        rsum = sb("rsum", [P, 2, 2])
        rinv = sb("rinv", [P, 2, 2])
        pe_ = sb("pe_", [P, 2, 3 * P])
        pn = sb("pn", [P, 2, 3 * P])
        pT = sb("pT", [P, 2, 3 * P])
        aT = sb("aT", [P, TOK])
        t2 = sb("t2", [P, TILES, P])
        nst = sb("nst", [P, TILES, 6])
        nmv = sb("nmv", [P, TILES, 2])
        nve = sb("nve", [P, TILES])
        nrs = sb("nrs", [P, TILES])
        ln2 = sb("ln2", [P, TILES, P])
        ln2T = sb("ln2T", [P, TOK])
        xhi = sb("xhi", [P, TOK], F32R)
        xlo = sb("xlo", [P, TOK], F32R)
        lg = sb("lg", [P, TILES, EXPERTS])
        top = sb("top", [P, TILES, 8])
        tix = sb("tix", [P, TILES, 8], U32)
        tif = sb("tif", [P, TILES, 2])
        td = sb("td", [P, TILES])
        te = sb("te", [P, TILES])
        ta = sb("ta", [P, TILES])
        tw = sb("tw", [P, TILES, 2])
        pick = sb("pick", [P, 2, TILES, EXPERTS])
        part = sb("part", [P, 2, TILES, EXPERTS])
        comb = sb("comb", [P, TILES, EXPERTS])
        cs = sb("cs", [P, TOK], F32R)
        combB = sb("combB", [P, EXPERTS, TOK])

        hf = sb("hf", [P, 2, HB, TOK])
        yt = sb("yt", [P, 2, TOK])
        acc = sb("acc", [P, TOK])
        t2m = sb("t2m", [P, TILES, P])
        ob = sb("ob", [P, TILES, P])

        bH = [ctx.enter_context(nc.psum_tensor(f"bH{n}", [P, 2 * TOK], F32)) for n in range(2)]
        bY = ctx.enter_context(nc.psum_tensor("bY", [P, 2 * TOK], F32))
        bA = ctx.enter_context(nc.psum_tensor("bA", [P, 2 * TOK], F32))
        bS = [ctx.enter_context(nc.psum_tensor(f"bS{n}", [P, 2 * TOK], F32)) for n in range(2)]
        bT = ctx.enter_context(nc.psum_tensor("bT", [P, 2 * TOK], F32))
        bL = ctx.enter_context(nc.psum_tensor("bL", [P, 2 * TOK], F32))

        def tiles(ap):
            return ap.rearrange("p (t n) -> p t n", n=P)

        sem = lambda name: ctx.enter_context(nc.semaphore(name))
        ld_x, ld_c, ld_w, ld_1, ld_2 = (sem(n) for n in ("ld_x", "ld_c", "ld_w", "ld_1", "ld_2"))
        su_zero, su_cast, su_dve, su_pe, su_act, su_pow, su_w1 = (
            sem(n) for n in ("su_zero", "su_cast", "su_dve", "su_pe", "su_act", "su_pow", "su_w1"))
        gate = [sem(f"gate{n}") for n in range(2)]

        l0_gn, l0_xg, l0_xx = sig("l0_gn"), sig("l0_xg"), sig("l0_xx")
        l0_s1, l0_s1b, l0_m1, l0_s1c, l0_e1 = sig("l0_s1"), sig("l0_s1b"), sig("l0_m1"), sig("l0_s1c"), sig("l0_e1")
        l0_sum, l0_r1, l0_p1, l0_pt, l0_ptc = sig("l0_sum"), sig("l0_r1"), sig("l0_p1"), sig("l0_pt"), sig("l0_ptc")
        l0_zc, l0_yc = sig("l0_zc"), sig("l0_yc")
        l0_z, l0_ez, l0_za, l0_zr, l0_zs = sig("l0_z"), sig("l0_ez"), sig("l0_za"), sig("l0_zr"), sig("l0_zs")
        l0_o, l0_ot, l0_base = sig("l0_o"), sig("l0_ot"), sig("l0_base")
        l0_s2, l0_m2, l0_e2, l0_r2, l0_p2 = sig("l0_s2"), sig("l0_m2"), sig("l0_e2"), sig("l0_r2"), sig("l0_p2")
        l0_v, l0_vx, l0_qt, l0_qtc = sig("l0_v"), sig("l0_vx"), sig("l0_qt"), sig("l0_qtc")
        l0_f, l0_fm, l0_fin = sig("l0_f"), sig("l0_fm"), sig("l0_fin")
        l0_y, l0_ey, l0_ya, l0_yr, l0_ys = sig("l0_y"), sig("l0_ey"), sig("l0_ya"), sig("l0_yr"), sig("l0_ys")
        l0_w, l0_fe, l0_x1 = sig("l0_w"), sig("l0_fe"), sig("l0_x1")

        at_xt, at_st, at_mv, at_rs = sig("at_xt"), sig("at_st", 2), sig("at_mv", 3), sig("at_rs")
        at_ln, at_xl, at_tb = sig("at_ln", 2), sig("at_xl"), sig("at_tb")
        at_lt, at_ltc = sig("at_lt"), sig("at_ltc")
        at_qk, at_v, at_k, at_vz, at_kz = sig("at_qk"), sig("at_v"), sig("at_k"), sig("at_vz"), sig("at_kz", HEADS)
        at_s, at_m, at_e, at_r = sig("at_s", HEADS), sig("at_m", HEADS), sig("at_e", 2 * HEADS), sig("at_r", HEADS)
        at_p, at_t, at_tc, at_pv = sig("at_p", HEADS), sig("at_t", HEADS), sig("at_tc", HEADS), sig("at_pv", HEADS)
        at_o, at_w, at_t2 = sig("at_o"), sig("at_w"), sig("at_t2")
        at_nst, at_nmv, at_nrs, at_n2 = sig("at_nst", 2), sig("at_nmv", 3), sig("at_nrs"), sig("at_n2", 2)
        at_nt, at_ntc, at_xs = sig("at_nt"), sig("at_ntc"), sig("at_xs", 2)
        at_l, at_lg, at_top, at_tix, at_tif = sig("at_l"), sig("at_lg"), sig("at_top", 2), sig("at_tix", 2), sig("at_tif")
        at_td, at_te, at_ta, at_tw, at_pick, at_share = sig("at_td"), sig("at_te"), sig("at_ta"), sig("at_tw", 2), sig("at_pick", 2), sig("at_share", 2)
        at_comb, at_ct, at_cs, at_cb, at_cbc = sig("at_comb"), sig("at_ct"), sig("at_cs", 2), sig("at_cb", 4), sig("at_cbc", 4)

        mo_t2 = sig("mo_t2")
        mo_h, mo_r, mo_y = sig("mo_h", 2 * EXPERTS), sig("mo_r", HB * EXPERTS), sig("mo_y", EXPERTS)
        mo_yt, mo_acc = sig("mo_yt", EXPERTS), sig("mo_acc", EXPERTS)
        mo_at, mo_ob, mo_out = sig("mo_at"), sig("mo_ob"), sig("mo_out", 16)

        block = ctx.enter_context(nc.Block())

        S_SLOT = {h: h for h in range(HEADS)}
        T_SLOT = {h: S_SLOT[h] + 2 for h in range(HEADS)}
        V_SLOT = {h: S_SLOT[h] + 3 for h in range(HEADS)}

        G1_SLOT = {e: min(2 * e, 13) for e in range(EXPERTS)}
        G2_SLOT = {**{e: 2 * e + 3 for e in range(6)}, 6: 14, 7: 15}

        def heads_in(plan, s):
            return [h for h in range(HEADS) if plan[h] == s]

        def pipeline(eng, step, before_experts=lambda: None):
            step(0, None, None)
            step(1, 0, None)
            before_experts()
            with eng.Fori(0, IMAGES - 2) as i:
                step(i + 2, i + 1, i)
            step(None, IMAGES - 1, IMAGES - 2)
            step(None, None, IMAGES - 1)

        @block.sync
        def _(sp):
            sp.dma_start(x_all[:, 0:4 * TOK], xT[:, 0:4 * TOK]).then_inc(ld_x, 16)
            sp.dma_start(x_all[:, 4 * TOK:], xT[:, 4 * TOK:]).then_inc(ld_x, 16)
            sp.dma_start(cst[:, :], consts).then_inc(ld_c, 16)
            sp.dma_start(W[:, :, :], weights).then_inc(ld_w, 16)
            for e in range(EXPERTS):
                sp.dma_start(w1raw[:, e, :], w1[e]).then_inc(ld_1, 16)
                sp.dma_start(w2s[:, e, :, :], w2[e].rearrange("(k p) c -> p k c", p=P)).then_inc(ld_2, 16)

            def step(l0, at, mo):
                if mo is None:
                    return
                sp.wait_ge(mo_ob.sem, mo_ob.nth(mo))
                sp.dma_start(out[bass.ds(mo * TILES, TILES), :, :].rearrange("t p c -> p t c"), ob[:, :, :])\
                  .then_inc(mo_out.sem, 16)

            pipeline(sp, step)
            sp.wait_ge(mo_out.sem, mo_out.per * IMAGES)

        @block.gpsimd
        def _(pool):
            pool.memset(vz[:, :, :], 0.0).then_inc(su_zero, 1)
            pool.memset(cs[:, :].bitcast(F32), 0.0).then_inc(su_zero, 1)
            pool.wait_ge(ld_c, 64)
            pool.wait_ge(su_dve, 6)
            pool.tensor_tensor(gn[:, :, 0], gvar[:, :], power[:, 0:1].broadcast_to([P, IMAGES]), ALU.pow)\
                .then_inc(su_pow, 1)

            def l0_part(s, i):
                if s == 6:
                    pool.wait_ge(l0_ot.sem, l0_ot.nth(i))
                    pool.wait_ge(l0_xx.sem, l0_xx.nth(i))
                    if not first(i):
                        pool.wait_ge(l0_x1.sem, l0_x1.before(i))
                    pool.tensor_tensor(base[:, :], xx[:, :], oT[:, :], ALU.add).then_inc(l0_base.sem, 1)
                if s == 12:
                    pool.wait_ge(at_mv.sem, at_mv.nth(i, 3))
                    pool.tensor_tensor(lrs[:, :], lve[:, :], power[:, 0:1].broadcast_to([P, TILES]), ALU.pow)\
                        .then_inc(at_rs.sem, 1)
                if s == 13:
                    pool.wait_ge(at_xl.sem, at_xl.nth(i))
                    if not first(i):
                        pool.wait_ge(at_t2.sem, at_t2.before(i))
                    pool.tensor_tensor(tb[:, :, :], xl[:, :, :],
                                       row[:, R_BO, :].unsqueeze(1).broadcast_to([P, TILES, P]), ALU.add)\
                        .then_inc(at_tb.sem, 1)

            def at_part(s, i):
                for h in heads_in(S_SLOT, s - 1):
                    b = h % 2
                    pool.wait_ge(at_r.sem, at_r.nth(i, h + 1))
                    if h >= 2:
                        pool.wait_ge(at_t.sem, at_t.nth(i, h - 1))
                    elif not first(i):
                        pool.wait_ge(at_t.sem, at_t.before(i))
                    pool.tensor_tensor(pn[:, b, 0:P], pe_[:, b, 0:P],
                                       rinv[:, b, 0:1].broadcast_to([P, P]), ALU.mult)
                    pool.tensor_tensor(pn[:, b, P:3 * P], pe_[:, b, P:3 * P],
                                       rinv[:, b, 1:2].broadcast_to([P, 2 * P]), ALU.mult).then_inc(at_p.sem, 1)
                if s == 11:
                    pool.wait_ge(at_nmv.sem, at_nmv.nth(i, 3))
                    pool.tensor_tensor(nrs[:, :], nve[:, :], power[:, 0:1].broadcast_to([P, TILES]), ALU.pow)\
                        .then_inc(at_nrs.sem, 1)

            def mo_part(s, i):
                if s == 0:
                    pool.wait_ge(at_t2.sem, at_t2.nth(i))
                    if not first(i):
                        pool.wait_ge(mo_ob.sem, mo_ob.before(i))
                    pool.sem_inc(gate[1], 1)
                    pool.tensor_copy(t2m[:, :, :], t2[:, :, :]).then_inc(mo_t2.sem, 1)
                for e in heads_in(G2_SLOT, s):
                    pool.wait_ge(mo_yt.sem, mo_yt.nth(i, e + 1))
                    if e == 0:
                        if not first(i):
                            pool.wait_ge(mo_at.sem, mo_at.before(i))
                        pool.sem_inc(gate[1], 1)
                        pool.tensor_copy(acc[:, :], yt[:, 0, :]).then_inc(mo_acc.sem, 1)
                    else:
                        pool.wait_ge(mo_acc.sem, mo_acc.nth(i, e))
                        pool.tensor_tensor(acc[:, :], acc[:, :], yt[:, e % 2, :], ALU.add).then_inc(mo_acc.sem, 1)

            def step(l0, at, mo):
                for s in range(SLOTS):
                    if at is not None:
                        at_part(s, at)
                    if l0 is not None:
                        l0_part(s, l0)
                    if mo is not None:
                        mo_part(s, mo)

            pipeline(pool, step)

        @block.scalar
        def _(act):
            act.dma_start(col[:, :], cols).then_inc(ld_c, 16)
            act.dma_start(row[:, :, :].rearrange("p a b -> p (a b)"), rows.partition_broadcast(P)).then_inc(ld_c, 16)
            act.dma_start(agt[:, :, :], agents).then_inc(ld_c, 16)
            act.dma_start(wr[:, :], w_router).then_inc(ld_w, 16)
            act.dma_start(b1s[:, :, :], b1).then_inc(ld_w, 16)
            act.dma_start(b2s[:, :], b2).then_inc(ld_w, 16)
            act.wait_ge(su_pe, 4)
            act.activation(fold[:, :, :].rearrange("p a b -> p (a b)"), bS[1][:, :], ACT.Copy).then_inc(su_act, 1)

            def l0_part(s, i):
                if s == 0:
                    act.wait_ge(l0_s1c.sem, l0_s1c.nth(i))
                    if not first(i):
                        act.wait_ge(l0_p1.sem, l0_p1.before(i))
                    act.activation(e1[:, :, :], s1c[:, :, :], ACT.Exp).then_inc(l0_e1.sem, 1)
                if s == 2:
                    act.wait_ge(l0_pt.sem, l0_pt.nth(i))
                    act.activation(p1T[:, :], bL[:, 0:TOK], ACT.Copy).then_inc(l0_ptc.sem, 1)
                if s == 3:
                    act.wait_ge(l0_zc.sem, l0_zc.nth(i))
                    if not first(i):
                        act.wait_ge(l0_za.sem, l0_za.before(i))
                    act.activation(ez[:, :], zc[:, :], ACT.Exp, scale=-1.0)\
                       .then_inc(l0_ez.sem, 1)
                if s == 6:
                    act.wait_ge(l0_m2.sem, l0_m2.nth(i))
                    if not first(i):
                        act.wait_ge(l0_p2.sem, l0_p2.before(i))
                    act.activation(e2[:, :], bL[:, 0:TOK], ACT.Exp, bias=s2m[:, 0:1], accum_out=s2s[:, 0:1])\
                       .then_inc(l0_e2.sem, 1)
                if s == 8:
                    act.wait_ge(l0_qt.sem, l0_qt.nth(i))
                    act.activation(p2T[:, :, :].rearrange("p t n -> p (t n)"), bL[:, 0:TOK], ACT.Copy)\
                       .then_inc(l0_qtc.sem, 1)
                if s == 10:
                    act.wait_ge(l0_yc.sem, l0_yc.nth(i))
                    if not first(i):
                        act.wait_ge(l0_ya.sem, l0_ya.before(i))
                    act.activation(ey[:, :], yc[:, :], ACT.Exp, scale=-1.0)\
                       .then_inc(l0_ey.sem, 1)
                if s == 14:
                    act.wait_ge(at_lt.sem, at_lt.nth(i))
                    act.activation(ln1T[:, :], bL[:, 0:TOK], ACT.Copy).then_inc(at_ltc.sem, 1)

            def at_part(s, i):
                for h in heads_in(T_SLOT, s):
                    b = h % 2
                    act.wait_ge(at_t.sem, at_t.nth(i, h + 1))
                    if h >= 2:
                        act.wait_ge(at_pv.sem, at_pv.nth(i, h - 1))
                    elif not first(i):
                        act.wait_ge(at_pv.sem, at_pv.before(i))
                    act.activation(pT[:, b, :], bT[:, 0:3 * P], ACT.Copy).then_inc(at_tc.sem, 1)
                for h in heads_in(S_SLOT, s):
                    b = h % 2
                    if h >= 2:
                        act.wait_ge(at_p.sem, at_p.nth(i, h - 1))
                    elif not first(i):
                        act.wait_ge(at_p.sem, at_p.before(i))
                    act.wait_ge(at_m.sem, at_m.nth(i, h + 1))
                    act.activation(pe_[:, b, 0:P], bS[b][:, 0:P], ACT.Exp, bias=nm[:, b, 0:1],
                                   accum_out=rsum[:, b, 0:1]).then_inc(at_e.sem, 1)
                    act.activation(pe_[:, b, P:3 * P], bS[b][:, P:3 * P], ACT.Exp, bias=nm[:, b, 1:2],
                                   accum_out=rsum[:, b, 1:2]).then_inc(at_e.sem, 1)
                if s == 10:
                    act.wait_ge(at_pv.sem, at_pv.nth(i, HEADS))
                    act.activation(aT[:, :], bA[:, 0:TOK], ACT.Copy).then_inc(at_o.sem, 1)
                if s == 13:
                    act.wait_ge(at_nt.sem, at_nt.nth(i))
                    act.activation(ln2T[:, :], bA[:, 0:TOK], ACT.Copy).then_inc(at_ntc.sem, 1)
                if s == 14:
                    act.wait_ge(at_td.sem, at_td.nth(i))
                    act.activation(te[:, :], td[:, :], ACT.Exp).then_inc(at_te.sem, 1)
                if s == 16:
                    for n, bank in enumerate((bS[0], bS[1], bT, bA)):
                        act.wait_ge(at_cb.sem, at_cb.nth(i, n + 1))
                        if not first(i):
                            act.wait_ge(mo_yt.sem, mo_yt.nth(i - 1, 2 * n + 2))
                        act.activation(combB[:, 2 * n:2 * n + 2, :].rearrange("p e t -> p (e t)"), bank[:, :],
                                       ACT.Copy).then_inc(at_cbc.sem, 1)

            def mo_part(s, i):
                for e in heads_in(G1_SLOT, s):
                    for k in range(HB):
                        if k % 2 == 0:
                            act.wait_ge(mo_h.sem, mo_h.nth(i, 2 * e + k // 2 + 1))
                        if k == 0:
                            if e >= 2:
                                act.wait_ge(mo_y.sem, mo_y.nth(i, e - 1))
                            elif not first(i):
                                act.wait_ge(mo_y.sem, mo_y.before(i))
                        act.activation(hf[:, e % 2, k, :], bH[k // 2][:, (k % 2) * TOK:(k % 2 + 1) * TOK], ACT.Relu,
                                       bias=b1s[:, e, k:k + 1]).then_inc(mo_r.sem, 1)

            def step(l0, at, mo):
                for s in range(SLOTS):
                    if mo is not None and s >= TAIL:
                        mo_part(s, mo)
                    if at is not None:
                        at_part(s, at)
                    if l0 is not None:
                        l0_part(s, l0)
                    if mo is not None and s < TAIL:
                        mo_part(s, mo)

            act.wait_ge(ld_c, 64)
            act.wait_ge(ld_w, 64)
            act.wait_ge(su_dve, 13)
            pipeline(act, step)

        @block.tensor
        def _(pe):
            pe.wait_ge(ld_c, 64)
            pe.wait_ge(ld_w, 64)
            pe.wait_ge(su_cast, 4)
            for n, (w, a) in enumerate(((W_KVYK, 0), (W_KVYV, 0), (W_Q, 1))):
                mm = pe.matmul(bS[0][:, n * AGENTS:(n + 1) * AGENTS], W[:, w, :], agt[:, a, :], start=True, stop=True)
            mm.then_inc(su_pe, 1)
            pe.wait_ge(su_dve, 1)
            pe.matmul(bH[0][:, 0:2 * IMAGES], grp, gmv[:, :, :].rearrange("p i k -> p (i k)"),
                      start=True, stop=True).then_inc(su_pe, 1)
            pe.wait_ge(su_dve, 5)
            pe.matmul(bH[1][:, 0:IMAGES], grp, gdev[:, :], start=True, stop=True).then_inc(su_pe, 1)
            pe.wait_ge(su_dve, 11)
            pe.matmul(bS[1][:, 0:P], W[:, W_Q2T, :], kvqd[:, 0, :, :].rearrange("p h m -> p (h m)"), start=True, stop=True)
            pe.matmul(bS[1][:, P:2 * P], bq2b[:, :], kvqd[:, 0, :, :].rearrange("p h m -> p (h m)"), start=True, stop=True)
            pe.matmul(bS[1][:, 2 * P:3 * P], kvqd[:, 1, :, :].rearrange("p h m -> p (h m)"), W[:, W_F1W1, :], start=True, stop=True)
            pe.matmul(bS[1][:, 3 * P:4 * P], W[:, W_KT, :], kvqd[:, 2, :, :].rearrange("p h m -> p (h m)"), start=True, stop=True)\
              .then_inc(su_pe, 1)
            pe.wait_ge(su_act, 1)
            pe.matmul(bT[:, 0:1], m2, col[:, B_PE1:B_PE1 + 1], start=True, stop=True).then_inc(su_pe, 1)
            pe.wait_ge(su_dve, 13)

            def l0_part(s, i):
                if s == 0:
                    pe.wait_ge(l0_xg.sem, l0_xg.nth(i))
                    if not first(i):
                        pe.wait_ge(at_vz.sem, at_vz.before(i))
                    for t in range(TILES):
                        mm = pe.matmul(bL[:, t * P:(t + 1) * P], xg[:, t * P:(t + 1) * P], m1, start=True, stop=True)
                    mm.then_inc(l0_s1.sem, 1)
                if s == 2:
                    pe.wait_ge(l0_p1.sem, l0_p1.nth(i))
                    for t in range(TILES):
                        mm = pe.transpose(bL[:, t * P:(t + 1) * P], p1[:, t, :], ident)
                    mm.then_inc(l0_pt.sem, 1)
                if s == 3:
                    pe.wait_ge(l0_ptc.sem, l0_ptc.nth(i))
                    pe.matmul(bL[:, 0:TOK], m2, p1T[:, :], start=True, stop=True).then_inc(l0_z.sem, 1)
                if s == 5:
                    pe.wait_ge(l0_zs.sem, l0_zs.nth(i))
                    pe.matmul(bL[:, 0:TOK], W[:, W_F1W2, :], zs[:, :], start=True, stop=True).then_inc(l0_o.sem, 1)
                if s == 6:
                    pe.wait_ge(l0_ot.sem, l0_ot.nth(i))
                    pe.matmul(bL[:, 0:TOK], mkq, oT[:, :], start=True, stop=True).then_inc(l0_s2.sem, 1)
                if s == 7:
                    pe.wait_ge(l0_e2.sem, l0_e2.nth(i))
                    for t in range(TILES):
                        mm = pe.matmul(bL[:, t * P:(t + 1) * P], oT[:, t * P:(t + 1) * P], W[:, W_V, :], start=True, stop=True)
                    mm.then_inc(l0_v.sem, 1)
                if s == 8:
                    pe.wait_ge(l0_p2.sem, l0_p2.nth(i))
                    pe.wait_ge(l0_vx.sem, l0_vx.nth(i))
                    for t in range(TILES):
                        mm = pe.transpose(bL[:, t * P:(t + 1) * P], p2[:, t * P:(t + 1) * P], ident)
                    mm.then_inc(l0_qt.sem, 1)
                if s == 9:
                    pe.wait_ge(l0_qtc.sem, l0_qtc.nth(i))
                    for t in range(TILES):
                        mm = pe.matmul(bL[:, 0:P], vx[:, t, :], p2T[:, t, :], start=(t == 0), stop=(t == TILES - 1))
                    mm.then_inc(l0_f.sem, 1)
                if s == 10:
                    pe.wait_ge(l0_fin.sem, l0_fin.nth(i))
                    pe.matmul(bL[:, 0:AGENTS], W[:, W_F2W1, :], fin[:, :], start=True, stop=True).then_inc(l0_y.sem, 1)
                if s == 11:
                    pe.wait_ge(l0_ys.sem, l0_ys.nth(i))
                    pe.matmul(bL[:, 0:AGENTS], W[:, W_F2W2, :], ys[:, :], start=True, stop=True).then_inc(l0_w.sem, 1)
                if s == 12:
                    pe.wait_ge(l0_x1.sem, l0_x1.nth(i))
                    for t in range(TILES):
                        mm = pe.transpose(bL[:, t * P:(t + 1) * P], x1T[:, t * P:(t + 1) * P], ident)
                    mm.then_inc(at_xt.sem, 1)
                if s == 14:
                    pe.wait_ge(at_xl.sem, at_xl.nth(i))
                    for t in range(TILES):
                        mm = pe.transpose(bL[:, t * P:(t + 1) * P], ln1[:, t, :], ident)
                    mm.then_inc(at_lt.sem, 1)
                if s == 15:
                    pe.wait_ge(at_ltc.sem, at_ltc.nth(i))
                    pe.matmul(bL[:, 0:TOK], W[:, W_AQ, :], ln1T[:, :], start=True, stop=True)
                    pe.matmul(bL[:, TOK:2 * TOK], W[:, W_AK, :], ln1T[:, :], start=True, stop=True)\
                      .then_inc(at_qk.sem, 1)
                if s == 16:
                    pe.wait_ge(at_k.sem, at_k.nth(i))
                    for t in range(TILES):
                        mm = pe.matmul(bL[:, t * P:(t + 1) * P], ln1T[:, t * P:(t + 1) * P], W[:, W_AV, :],
                                       start=True, stop=True)
                    mm.then_inc(at_v.sem, 1)

            def at_part(s, i):
                for h in heads_in(V_SLOT, s):
                    b = h % 2
                    if h == 0:
                        pe.wait_ge(at_vz.sem, at_vz.nth(i))
                        if not first(i):
                            pe.wait_ge(at_cbc.sem, at_cbc.before(i))
                    pe.wait_ge(at_tc.sem, at_tc.nth(i, h + 1))
                    pe.matmul(bA[:, 0:TOK], vz[:, 0, h * P:(h + 1) * P], pT[:, b, 0:TOK],
                              start=(h == 0), stop=False)
                    pe.matmul(bA[:, P:TOK], vz[:, 1, h * P:(h + 1) * P], pT[:, b, TOK:3 * P],
                              start=False, stop=(h == HEADS - 1)).then_inc(at_pv.sem, 1)
                for h in heads_in(T_SLOT, s):
                    b = h % 2
                    pe.wait_ge(at_p.sem, at_p.nth(i, h + 1))
                    if h >= 1:
                        pe.wait_ge(at_tc.sem, at_tc.nth(i, h))
                    elif not first(i):
                        pe.wait_ge(at_cbc.sem, at_cbc.nth(i - 1, 3))
                    pe.transpose(bT[:, 0:P], pn[:, b, 0:P], ident)
                    pe.transpose(bT[:, P:2 * P], pn[:, b, P:2 * P], ident)
                    pe.transpose(bT[:, 2 * P:3 * P], pn[:, b, 2 * P:3 * P], ident).then_inc(at_t.sem, 1)
                for h in heads_in(S_SLOT, s):
                    b = h % 2
                    pe.wait_ge(at_kz.sem, at_kz.nth(i, h + 1))
                    if h < 2 and not first(i):
                        pe.wait_ge(at_cbc.sem, at_cbc.nth(i - 1, h + 1))
                    if h >= 2:
                        pe.wait_ge(at_e.sem, at_e.nth(i, 2 * (h - 1)))
                    pe.matmul(bS[b][:, 0:P], qT[:, 0:P], kz[:, h, 0:P], start=True, stop=False)
                    pe.matmul(bS[b][:, 0:P], identb[:, :], causalb[:, :], start=False, stop=True)
                    pe.matmul(bS[b][:, P:3 * P], qT[:, P:2 * P], kz[:, h, :], start=True, stop=False)
                    pe.matmul(bS[b][:, 2 * P:3 * P], identb[:, :], causalb[:, :], start=False, stop=True)\
                      .then_inc(at_s.sem, 1)
                if s == 11:
                    pe.wait_ge(at_o.sem, at_o.nth(i))
                    for t in range(TILES):
                        mm = pe.matmul(bA[:, t * P:(t + 1) * P], aT[:, t * P:(t + 1) * P], W[:, W_AO, :],
                                       start=True, stop=True)
                    mm.then_inc(at_w.sem, 1)
                if s == 13:
                    pe.wait_ge(at_n2.sem, at_n2.nth(i, 2))
                    for t in range(TILES):
                        mm = pe.transpose(bA[:, t * P:(t + 1) * P], ln2[:, t, :], ident)
                    mm.then_inc(at_nt.sem, 1)
                if s == 14:
                    pe.wait_ge(at_ntc.sem, at_ntc.nth(i))
                    for t in range(TILES):
                        mm = pe.matmul(bA[:, t * EXPERTS:(t + 1) * EXPERTS], ln2T[:, t * P:(t + 1) * P], wr[:, :],
                                       start=True, stop=True)
                    mm.then_inc(at_l.sem, 1)
                if s == 15:
                    pe.wait_ge(at_comb.sem, at_comb.nth(i))
                    for t in range(TILES):
                        mm = pe.transpose(bA[0:EXPERTS, t * P:(t + 1) * P], comb[:, t, :], ident)
                    mm.then_inc(at_ct.sem, 1)
                if s == 16:
                    pe.wait_ge(at_cs.sem, at_cs.nth(i, 2))
                    for n, bank in enumerate((bS[0], bS[1], bT, bA)):
                        for k in range(2):
                            mm = pe.matmul(bank[:, k * TOK:(k + 1) * TOK], selr[:, 2 * n + k, :], cs[:, :],
                                           start=True, stop=True)
                        mm.then_inc(at_cb.sem, 1)

            def mo_first(e, i):
                if e == 0:
                    pe.wait_ge(at_xs.sem, at_xs.nth(i, 2))
                for k in range(HB):
                    if k % 2 == 0:
                        if e >= 1:
                            pe.wait_ge(mo_r.sem, mo_r.nth(i, HB * (e - 1) + k + 2))
                        elif not first(i):
                            pe.wait_ge(mo_r.sem, mo_r.before(i))
                    hk = bH[k // 2][:, (k % 2) * TOK:(k % 2 + 1) * TOK]
                    wk = slice(k * P, (k + 1) * P)
                    pe.matmul(hk, w1hi[:, e, wk], xhi[:, :], start=True, stop=False)
                    pe.matmul(hk, w1hi[:, e, wk], xlo[:, :], start=False, stop=False)
                    mm = pe.matmul(hk, w1lo[:, e, wk], xhi[:, :], start=False, stop=True)
                    if k % 2 == 1:
                        mm.then_inc(mo_h.sem, 1)

            def mo_second(e, i):
                if e >= 1:
                    pe.wait_ge(mo_yt.sem, mo_yt.nth(i, e))
                elif not first(i):
                    pe.wait_ge(mo_ob.sem, mo_ob.before(i))
                pe.wait_ge(mo_r.sem, mo_r.nth(i, HB * (e + 1)))
                for k in range(HB):
                    mm = pe.matmul(bY[:, 0:TOK], w2s[:, e, k, :], hf[:, e % 2, k, :], start=(k == 0), stop=(k == HB - 1))
                mm.then_inc(mo_y.sem, 1)

            def mo_part(s, i):
                for e in heads_in(G2_SLOT, s):
                    mo_second(e, i)
                for e in heads_in(G1_SLOT, s):
                    mo_first(e, i)

            def mo_end(i):
                pe.wait_ge(mo_acc.sem, mo_acc.nth(i, EXPERTS))
                for t in range(TILES):
                    mm = pe.transpose(bY[:, t * P:(t + 1) * P], acc[:, t * P:(t + 1) * P], ident)
                mm.then_inc(mo_at.sem, 1)

            def step(l0, at, mo):
                for s in range(SLOTS):
                    if mo is not None and s >= TAIL:
                        mo_part(s, mo)
                    if l0 is not None and s == SLOTS - 1:
                        l0_part(s, l0)
                    if at is not None:
                        at_part(s, at)
                    if l0 is not None and s < SLOTS - 1:
                        l0_part(s, l0)
                    if mo is not None and s < TAIL:
                        mo_part(s, mo)
                if mo is not None:
                    mo_end(mo)

            def weights_ready():
                pe.wait_ge(ld_2, 16 * EXPERTS)
                pe.wait_ge(su_w1, 2 * EXPERTS)

            pipeline(pe, step, weights_ready)

        @block.vector
        def _(dve):
            done = [0]

            def after(ins):
                done[0] += 1
                ins.then_inc(su_dve, 1)
                dve.wait_ge(su_dve, done[0])

            dve.wait_ge(ld_x, 32)
            for n in range(IMAGES):
                last = dve.bn_stats(gst[:, n, :], x_all[:, n * TOK:(n + 1) * TOK])
            last.then_inc(su_cast, 1)
            dve.wait_ge(ld_c, 64)
            dve.tensor_copy(identb[:, :], ident).then_inc(su_cast, 1)
            dve.tensor_copy(causalb[:, :], cst[:, C_CAUSAL:C_CAUSAL + P]).then_inc(su_cast, 1)
            dve.tensor_copy(selr[:, :, :].rearrange("p e n -> p (e n)"), cst[:, C_SEL:C_N]).then_inc(su_cast, 1)
            dve.wait_ge(su_cast, 4)
            for n in range(IMAGES):
                last = dve.bn_aggr(gmv[:, n, :], gst[:, n, :])
            after(last)
            dve.wait_ge(su_pe, 2)
            after(dve.tensor_copy(gmean[:, :], bH[0][:, 0:2 * IMAGES].rearrange("p (i k) -> p i k", k=2)[:, :, 0]))
            after(dve.tensor_tensor(gdev[:, :], gmv[:, :, 0], gmean[:, :], ALU.subtract))
            after(dve.tensor_tensor(gvar[:, :], gdev[:, :], gdev[:, :], ALU.mult))
            after(dve.tensor_tensor(gdev[:, :], gvar[:, :], gmv[:, :, 1], ALU.add))
            dve.wait_ge(su_pe, 3)
            after(dve.tensor_scalar(gvar[:, :], bH[1][:, 0:IMAGES], 1e-5, None, ALU.add))
            after(dve.tensor_tensor(kvq[:, :, :], bS[0][:, 0:3 * AGENTS].rearrange("p (n m) -> p n m", n=3),
                                    col[:, B_KYK:B_Q + 1].unsqueeze(2).broadcast_to([P, 3, AGENTS]), ALU.add))
            for n, mask in enumerate((bds, bd, bds)):
                after(dve.tensor_tensor(kvqd[:, n, :, :], kvq[:, n, :].unsqueeze(1).broadcast_to([P, HEADS, AGENTS]),
                                        mask.unsqueeze(2).broadcast_to([P, HEADS, AGENTS]), ALU.mult))
            after(dve.tensor_copy(bq2b[:, :], col[:, B_Q2:B_Q2 + 1].broadcast_to([P, P])))
            dve.wait_ge(su_pow, 1)
            after(dve.scalar_tensor_tensor(out=gn[:, :, 1], in0=gmean[:, :], scalar=-1.0, in1=gn[:, :, 0],
                                           op0=ALU.mult, op1=ALU.mult))
            dve.wait_ge(su_pe, 5)
            after(dve.tensor_tensor(zb[:, :], bT[:, 0:1], col[:, B_F1B1:B_F1B1 + 1], ALU.add))

            def split_w1(e):
                dve.wait_ge(ld_1, 16 * EXPERTS)
                dve.tensor_copy(w1hi[:, e, :], w1raw[:, e, :]).then_inc(su_w1, 1)
                dve.wait_ge(su_w1, 2 * e + 1)
                dve.tensor_tensor(w1lo[:, e, :], w1raw[:, e, :], w1hi[:, e, :].bitcast(F32), ALU.subtract)\
                   .then_inc(su_w1, 1)

            def l0_late(s, i):
                if s == 0:
                    dve.tensor_copy(gni[:, :], gn[:, bass.ds(i, 1), :].rearrange("p a k -> p (a k)")).then_inc(l0_gn.sem, 1)
                    x_i = x_all[:, bass.ds(i * TOK, TOK)]
                    if not first(i):
                        dve.wait_ge(l0_s1.sem, l0_s1.before(i))
                    dve.wait_ge(l0_gn.sem, l0_gn.nth(i))
                    dve.tensor_scalar(xg[:, :], x_i, gni[:, 0:1], gni[:, 1:2], ALU.mult, ALU.add)\
                       .then_inc(l0_xg.sem, 1)
                    if not first(i):
                        dve.wait_ge(l0_base.sem, l0_base.before(i))
                    dve.wait_ge(l0_xg.sem, l0_xg.nth(i))
                    dve.tensor_tensor(xx[:, :], x_i, xg[:, :], ALU.add).then_inc(l0_xx.sem, 1)
                if s == 2:
                    egrouped = e1[:, :, :].rearrange("p t (h m) -> p (t h) m", m=AGENTS)
                    dve.wait_ge(l0_e1.sem, l0_e1.nth(i))
                    dve.tensor_reduce(e1s[:, :], egrouped, AX.X, ALU.add).then_inc(l0_sum.sem, 1)
                    dve.wait_ge(l0_sum.sem, l0_sum.nth(i))
                    dve.reciprocal(e1r[:, :], e1s[:, :]).then_inc(l0_r1.sem, 1)
                    if not first(i):
                        dve.wait_ge(l0_pt.sem, l0_pt.before(i))
                    dve.wait_ge(l0_r1.sem, l0_r1.nth(i))
                    dve.tensor_tensor(p1[:, :, :].rearrange("p t (h m) -> p (t h) m", m=AGENTS), egrouped,
                                      e1r[:, :].unsqueeze(2).broadcast_to([P, TILES * HEADS, AGENTS]),
                                      ALU.mult).then_inc(l0_p1.sem, 1)
                if s == 4:
                    dve.wait_ge(l0_ez.sem, l0_ez.nth(i))
                    dve.tensor_scalar(za[:, :], ez[:, :], 1.0, None, ALU.add).then_inc(l0_za.sem, 1)
                    dve.wait_ge(l0_za.sem, l0_za.nth(i))
                    dve.reciprocal(zr[:, :], za[:, :]).then_inc(l0_zr.sem, 1)
                    if not first(i):
                        dve.wait_ge(l0_o.sem, l0_o.before(i))
                    dve.wait_ge(l0_zr.sem, l0_zr.nth(i))
                    dve.scalar_tensor_tensor(out=zs[:, :], in0=bL[:, 0:TOK], scalar=zb[:, 0:1], in1=zr[:, :],
                                             op0=ALU.add, op1=ALU.mult).then_inc(l0_zs.sem, 1)
                if s == 7:
                    dve.wait_ge(l0_e2.sem, l0_e2.nth(i))
                    dve.reciprocal(s2r[:, :], s2s[:, :]).then_inc(l0_r2.sem, 1)
                    if not first(i):
                        dve.wait_ge(l0_qt.sem, l0_qt.before(i))
                    dve.wait_ge(l0_r2.sem, l0_r2.nth(i))
                    dve.tensor_scalar(p2[:, :], e2[:, :], s2r[:, 0:1], col[:, B_PE2:B_PE2 + 1], ALU.mult, ALU.add)\
                       .then_inc(l0_p2.sem, 1)
                if s == 11:
                    dve.wait_ge(l0_ey.sem, l0_ey.nth(i))
                    dve.tensor_scalar(ya[:, :], ey[:, :], 1.0, None, ALU.add).then_inc(l0_ya.sem, 1)
                    dve.wait_ge(l0_ya.sem, l0_ya.nth(i))
                    dve.reciprocal(yr[:, :], ya[:, :]).then_inc(l0_yr.sem, 1)
                    if not first(i):
                        dve.wait_ge(l0_w.sem, l0_w.before(i))
                    dve.wait_ge(l0_yr.sem, l0_yr.nth(i))
                    dve.scalar_tensor_tensor(out=ys[:, :], in0=bL[:, 0:AGENTS], scalar=col[:, B_F2B1:B_F2B1 + 1],
                                             in1=yr[:, :], op0=ALU.add, op1=ALU.mult).then_inc(l0_ys.sem, 1)
                if s == 13:
                    if not first(i):
                        dve.wait_ge(at_lt.sem, at_lt.before(i))
                    dve.wait_ge(at_rs.sem, at_rs.nth(i))
                    for t in range(TILES):
                        dve.tensor_scalar(ln1[:, t, :], bL[:, t * P:(t + 1) * P], lmv[:, t, 0:1], lrs[:, t:t + 1],
                                          ALU.subtract, ALU.mult).then_inc(at_ln.sem, 1)
                    if not first(i):
                        dve.wait_ge(at_tb.sem, at_tb.before(i))
                    dve.wait_ge(at_ln.sem, at_ln.nth(i, 2))
                    dve.tensor_tensor(xl[:, :, :], tiles(bL[:, 0:TOK]), ln1[:, :, :], ALU.add).then_inc(at_xl.sem, 1)

            def at_late(s, i):
                if s == 12:
                    if not first(i):
                        dve.wait_ge(at_nt.sem, at_nt.before(i))
                    dve.wait_ge(at_nrs.sem, at_nrs.nth(i))
                    for t in range(TILES):
                        dve.tensor_scalar(ln2[:, t, :], t2[:, t, :], nmv[:, t, 0:1], nrs[:, t:t + 1],
                                          ALU.subtract, ALU.mult).then_inc(at_n2.sem, 1)
                if s == 15:
                    dve.wait_ge(at_te.sem, at_te.nth(i))
                    dve.tensor_scalar(ta[:, :], te[:, :], 1.0, None, ALU.add).then_inc(at_ta.sem, 1)
                    dve.wait_ge(at_ta.sem, at_ta.nth(i))
                    dve.reciprocal(tw[:, :, 0], ta[:, :]).then_inc(at_tw.sem, 1)
                    dve.wait_ge(at_tw.sem, at_tw.nth(i, 1))
                    dve.tensor_tensor(tw[:, :, 1], te[:, :], tw[:, :, 0], ALU.mult).then_inc(at_tw.sem, 1)
                    dve.wait_ge(at_tw.sem, at_tw.nth(i, 2))
                    for k in range(2):
                        dve.tensor_tensor(part[:, k, :, :], pick[:, k, :, :],
                                          tw[:, :, k:k + 1].broadcast_to([P, TILES, EXPERTS]), ALU.mult)\
                           .then_inc(at_share.sem, 1)
                    if not first(i):
                        dve.wait_ge(at_ct.sem, at_ct.before(i))
                    dve.wait_ge(at_share.sem, at_share.nth(i, 2))
                    dve.tensor_tensor(comb[:, :, :], part[:, 0, :, :], part[:, 1, :, :], ALU.add)\
                       .then_inc(at_comb.sem, 1)

            def l0_part(s, i):
                if s == 0:
                    dve.wait_ge(l0_s1.sem, l0_s1.nth(i))
                    dve.tensor_tensor(s1[:, :, :], tiles(bL[:, 0:TOK]), c1.unsqueeze(1).broadcast_to([P, TILES, P]),
                                      ALU.add).then_inc(l0_s1b.sem, 1)
                    dve.wait_ge(l0_s1b.sem, l0_s1b.nth(i))
                    grouped = s1[:, :, :].rearrange("p t (h m) -> p (t h) m", m=AGENTS)
                    dve.tensor_reduce(s1m[:, :], grouped, AX.X, ALU.max).then_inc(l0_m1.sem, 1)
                    dve.wait_ge(l0_m1.sem, l0_m1.nth(i))
                    dve.tensor_tensor(s1c[:, :, :].rearrange("p t (h m) -> p (t h) m", m=AGENTS), grouped,
                                      s1m[:, :].unsqueeze(2).broadcast_to([P, TILES * HEADS, AGENTS]),
                                      ALU.subtract).then_inc(l0_s1c.sem, 1)
                if s == 3:
                    dve.wait_ge(l0_z.sem, l0_z.nth(i))
                    dve.tensor_scalar(zc[:, :], bL[:, 0:TOK], zb[:, 0:1], -LOW, ALU.add, ALU.max)\
                       .then_inc(l0_zc.sem, 1)
                if s == 5:
                    if not first(i):
                        dve.wait_ge(l0_v.sem, l0_v.before(i))
                    dve.wait_ge(l0_o.sem, l0_o.nth(i))
                    dve.scalar_tensor_tensor(out=oT[:, :], in0=bL[:, 0:TOK], scalar=col[:, B_F1B2:B_F1B2 + 1],
                                             in1=xg[:, :], op0=ALU.add, op1=ALU.add).then_inc(l0_ot.sem, 1)
                if s == 6:
                    dve.wait_ge(l0_s2.sem, l0_s2.nth(i))
                    dve.tensor_reduce(s2m[:, :], bL[:, 0:TOK], AX.X, ALU.max, negate=True).then_inc(l0_m2.sem, 1)
                if s == 7:
                    if not first(i):
                        dve.wait_ge(l0_f.sem, l0_f.before(i))
                    dve.wait_ge(l0_v.sem, l0_v.nth(i))
                    dve.tensor_tensor(vx[:, :, :], tiles(bL[:, 0:TOK]),
                                      row[:, R_BV, :].unsqueeze(1).broadcast_to([P, TILES, P]), ALU.add)\
                       .then_inc(l0_vx.sem, 1)
                if s == 9:
                    dve.wait_ge(l0_f.sem, l0_f.nth(i))
                    dve.tensor_tensor(fm[:, :, :], bL[:, 0:P].rearrange("p (h m) -> p h m", m=AGENTS),
                                      bd.unsqueeze(2).broadcast_to([P, HEADS, AGENTS]), ALU.mult).then_inc(l0_fm.sem, 1)
                    if not first(i):
                        dve.wait_ge(l0_y.sem, l0_y.before(i))
                    dve.wait_ge(l0_fm.sem, l0_fm.nth(i))
                    dve.tensor_reduce(fin[:, :], fm[:, :, :].rearrange("p h m -> p m h"), AX.X, ALU.add)\
                       .then_inc(l0_fin.sem, 1)
                if s == 10:
                    dve.wait_ge(l0_y.sem, l0_y.nth(i))
                    dve.tensor_scalar(yc[:, :], bL[:, 0:AGENTS], col[:, B_F2B1:B_F2B1 + 1], -LOW, ALU.add, ALU.max)\
                       .then_inc(l0_yc.sem, 1)
                if s == 11:
                    dve.wait_ge(l0_w.sem, l0_w.nth(i))
                    dve.tensor_scalar(fe[:, :, :], bL[:, 0:AGENTS].unsqueeze(2).broadcast_to([P, AGENTS, CELL]),
                                      col[:, B_F2B2:B_F2B2 + 1], None, ALU.add).then_inc(l0_fe.sem, 1)
                    if not first(i):
                        dve.wait_ge(at_xt.sem, at_xt.before(i))
                    dve.wait_ge(l0_base.sem, l0_base.nth(i))
                    dve.wait_ge(l0_fe.sem, l0_fe.nth(i))
                    dve.tensor_tensor(x1T[:, :].rearrange("p (a y x) -> p a y x", a=CELL, y=CELL),
                                      base[:, :].rearrange("p (a y x) -> p a y x", a=CELL, y=CELL),
                                      fe[:, :, :].rearrange("p (a b) x -> p a (b x)", a=CELL).unsqueeze(2)
                                      .broadcast_to([P, CELL, CELL, SIDE]), ALU.add).then_inc(l0_x1.sem, 1)
                if s == 12:
                    dve.wait_ge(at_xt.sem, at_xt.nth(i))
                    for t in range(TILES):
                        dve.bn_stats(lst[:, t, :], bL[:, t * P:(t + 1) * P]).then_inc(at_st.sem, 1)
                    dve.wait_ge(at_st.sem, at_st.nth(i, 2))
                    dve.sem_inc(gate[0], 1)
                    for t in range(TILES):
                        dve.bn_aggr(lmv[:, t, :], lst[:, t, :]).then_inc(at_mv.sem, 1)
                    dve.wait_ge(at_mv.sem, at_mv.nth(i, 2))
                    dve.tensor_scalar(lve[:, :], lmv[:, :, 1], 1e-5, None, ALU.add).then_inc(at_mv.sem, 1)
                if s == 15:
                    if not first(i):
                        dve.wait_ge(at_s.sem, at_s.before(i))
                    dve.wait_ge(at_qk.sem, at_qk.nth(i))
                    dve.tensor_scalar(kT[:, :], bL[:, TOK:2 * TOK], col[:, B_AK:B_AK + 1], None, ALU.add)
                    dve.tensor_scalar(qT[:, :], bL[:, 0:TOK], col[:, B_AQ:B_AQ + 1], SCALE, ALU.add, ALU.mult)\
                       .then_inc(at_k.sem, 1)
                    dve.wait_ge(at_k.sem, at_k.nth(i))
                    for h in range(HEADS):
                        dve.tensor_scalar(kz[:, h, :], kT[:, :], bd[:, h:h + 1], None, ALU.mult).then_inc(at_kz.sem, 1)
                if s == 16:
                    if first(i):
                        dve.wait_ge(su_zero, 2)
                    else:
                        dve.wait_ge(at_pv.sem, at_pv.before(i))
                    dve.wait_ge(at_v.sem, at_v.nth(i))
                    for t in range(TILES):
                        v = dve.tensor_tensor(vz[:, t, :].rearrange("p (h n) -> p h n", n=VSTEP)[:, :, 0:DK],
                                              bL[:, t * P:(t + 1) * P].rearrange("p (h d) -> p h d", d=DK),
                                              row[:, R_BAV, :].rearrange("p (h d) -> p h d", d=DK), ALU.add)
                    v.then_inc(at_vz.sem, 1)

            def at_part(s, i):
                for h in heads_in(S_SLOT, s - 1):
                    b = h % 2
                    if h >= 2:
                        dve.wait_ge(at_p.sem, at_p.nth(i, h - 1))
                    elif not first(i):
                        dve.wait_ge(at_p.sem, at_p.before(i))
                    dve.wait_ge(at_e.sem, at_e.nth(i, 2 * h + 2))
                    dve.reciprocal(rinv[:, b, :], rsum[:, b, :]).then_inc(at_r.sem, 1)
                for h in heads_in(S_SLOT, s):
                    b = h % 2
                    dve.wait_ge(at_s.sem, at_s.nth(i, h + 1))
                    dve.tensor_reduce(nm[:, b, 0:1], bS[b][:, 0:P], AX.X, ALU.max, negate=True)
                    dve.tensor_reduce(nm[:, b, 1:2], bS[b][:, P:3 * P], AX.X, ALU.max, negate=True)\
                       .then_inc(at_m.sem, 1)
                if s == 11:
                    if not first(i):
                        dve.wait_ge(mo_t2.sem, mo_t2.before(i))
                    dve.wait_ge(at_tb.sem, at_tb.nth(i))
                    dve.wait_ge(at_w.sem, at_w.nth(i))
                    dve.tensor_tensor(t2[:, :, :], tiles(bA[:, 0:TOK]), tb[:, :, :], ALU.add).then_inc(at_t2.sem, 1)
                    dve.wait_ge(at_t2.sem, at_t2.nth(i))
                    for t in range(TILES):
                        dve.bn_stats(nst[:, t, :], t2[:, t, :]).then_inc(at_nst.sem, 1)
                    dve.wait_ge(at_nst.sem, at_nst.nth(i, 2))
                    dve.sem_inc(gate[0], 1)
                    for t in range(TILES):
                        dve.bn_aggr(nmv[:, t, :], nst[:, t, :]).then_inc(at_nmv.sem, 1)
                    dve.wait_ge(at_nmv.sem, at_nmv.nth(i, 2))
                    dve.tensor_scalar(nve[:, :], nmv[:, :, 1], 1e-5, None, ALU.add).then_inc(at_nmv.sem, 1)
                if s == 14:
                    dve.wait_ge(at_l.sem, at_l.nth(i))
                    dve.tensor_copy(lg[:, :, :].rearrange("p t e -> p (t e)"), bA[:, 0:TILES * EXPERTS])\
                       .then_inc(at_lg.sem, 1)
                    dve.wait_ge(at_lg.sem, at_lg.nth(i))
                    dve.sem_inc(gate[0], 1)
                    for t in range(TILES):
                        dve.max(top[:, t, :], lg[:, t, :]).then_inc(at_top.sem, 1)
                    dve.wait_ge(at_top.sem, at_top.nth(i, 2))
                    dve.tensor_tensor(td[:, :], top[:, :, 1], top[:, :, 0], ALU.subtract).then_inc(at_td.sem, 1)
                    for t in range(TILES):
                        dve.max_index(tix[:, t, :], top[:, t, :], lg[:, t, :]).then_inc(at_tix.sem, 1)
                    dve.wait_ge(at_tix.sem, at_tix.nth(i, 2))
                    dve.tensor_copy(tif[:, :, :], tix[:, :, 0:2]).then_inc(at_tif.sem, 1)
                    dve.wait_ge(at_tif.sem, at_tif.nth(i))
                    for k in range(2):
                        dve.tensor_tensor(pick[:, k, :, :], iota.unsqueeze(1).broadcast_to([P, TILES, EXPERTS]),
                                          tif[:, :, k:k + 1].broadcast_to([P, TILES, EXPERTS]), ALU.is_equal)\
                           .then_inc(at_pick.sem, 1)
                if s == 15:
                    if not first(i):
                        dve.wait_ge(at_cb.sem, at_cb.before(i))
                    dve.wait_ge(at_ct.sem, at_ct.nth(i))
                    dve.tensor_copy(cs[0:EXPERTS, :], bA[0:EXPERTS, 0:TOK]).then_inc(at_cs.sem, 1)
                    dve.wait_ge(at_cs.sem, at_cs.nth(i, 1))
                    dve.tensor_tensor(cs[32:32 + EXPERTS, :], bA[0:EXPERTS, 0:TOK], cs[0:EXPERTS, :].bitcast(F32),
                                      ALU.subtract).then_inc(at_cs.sem, 1)
                    if not first(i):
                        dve.wait_ge(mo_h.sem, mo_h.before(i))
                    dve.wait_ge(at_ntc.sem, at_ntc.nth(i))
                    dve.tensor_copy(xhi[:, :], ln2T[:, :]).then_inc(at_xs.sem, 1)
                    dve.wait_ge(at_xs.sem, at_xs.nth(i, 1))
                    dve.tensor_tensor(xlo[:, :], ln2T[:, :], xhi[:, :].bitcast(F32), ALU.subtract)\
                       .then_inc(at_xs.sem, 1)

            def mo_part(s, i):
                for e in heads_in(G2_SLOT, s):
                    dve.wait_ge(at_cbc.sem, at_cbc.nth(i, e // 2 + 1))
                    if e >= 2:
                        dve.wait_ge(mo_acc.sem, mo_acc.nth(i, e - 1))
                    elif not first(i):
                        dve.wait_ge(mo_acc.sem, mo_acc.before(i))
                    dve.wait_ge(mo_y.sem, mo_y.nth(i, e + 1))
                    dve.scalar_tensor_tensor(out=yt[:, e % 2, :], in0=bY[:, 0:TOK], scalar=b2s[:, e:e + 1],
                                             in1=combB[:, e, :], op0=ALU.add, op1=ALU.mult).then_inc(mo_yt.sem, 1)

            def mo_end(i):
                if not first(i):
                    dve.wait_ge(mo_out.sem, mo_out.before(i))
                dve.wait_ge(mo_t2.sem, mo_t2.nth(i))
                dve.wait_ge(mo_at.sem, mo_at.nth(i))
                dve.tensor_tensor(ob[:, :, :], tiles(bY[:, 0:TOK]), t2m[:, :, :], ALU.add).then_inc(mo_ob.sem, 1)

            def step(l0, at, mo):
                for s in range(SLOTS):
                    if l0 is not None:
                        l0_late(s, l0)
                    if at is not None:
                        at_late(s, at)
                    if mo is not None and s >= TAIL:
                        mo_part(s, mo)
                    if at is not None:
                        at_part(s, at)
                    if l0 is not None:
                        l0_part(s, l0)
                    if mo is not None and s < TAIL:
                        mo_part(s, mo)
                    if first(at) and s < EXPERTS:
                        split_w1(s)
                if mo is not None:
                    mo_end(mo)

            pipeline(dve, step)


def kernel(**inputs):
    import numpy as np
    import concourse.bacc as bacc
    from concourse.bass_utils import run_bass_kernel_spmd

    L0 = {k[len("L0_conv_"):]: np.asarray(v) for k, v in inputs.items() if k.startswith("L0_conv_")}
    A = {k[len("L1_attn_"):]: np.asarray(v) for k, v in inputs.items() if k.startswith("L1_attn_")}
    M = {k[len("L1_ffn_"):]: np.asarray(v) for k, v in inputs.items() if k.startswith("L1_ffn_")}

    p = np.arange(P)
    consts = np.zeros((P, C_N), np.float32)
    consts[:, C_ID:C_ID + P] = np.eye(P)
    consts[:, C_GRP:C_GRP + P] = (p[:, None] // GROUP == p[None, :] // GROUP) * (1.0 / GROUP)
    consts[:, C_CAUSAL:C_CAUSAL + P] = np.where(p[None, :] > p[:, None], -1e9, 0.0)
    own = p[:, None] // DK == np.arange(HEADS)[None, :]
    consts[:, C_BD:C_BD + HEADS] = own
    consts[:, C_BDS:C_BDS + HEADS] = own * SCALE
    consts[:, C_IOTA:C_IOTA + EXPERTS] = np.arange(EXPERTS)
    consts[:, C_POW:C_POW + 2] = -0.5
    for e in range(EXPERTS):
        consts[[e, 32 + e], C_SEL + e * P:C_SEL + (e + 1) * P] = 1.0

    by_kind = A["W_in"].reshape(C, HEADS, 3, DK).transpose(2, 0, 1, 3).reshape(3, C, C)
    bias_by_kind = A["b_in"].reshape(HEADS, 3, DK).transpose(1, 0, 2).reshape(3, C)
    weights = np.stack([
        L0["w_kvy"][:, :C], L0["w_kvy"][:, C:], L0["w_q"], L0["w_q2"].T, L0["f1w1"], L0["w_kvx"][:, :C].T,
        L0["f1w2"], L0["w_kvx"][:, C:], L0["f2w1"], L0["f2w2"], by_kind[0], by_kind[1], by_kind[2], A["W_out"]],
        axis=1)
    cols = np.stack([
        L0["b_kvy"][:C], L0["b_kvy"][C:], L0["b_q"], L0["pe1"].reshape(P), L0["pe2"].reshape(P), L0["f1b1"],
        L0["f1b2"], L0["f2b1"], L0["f2b2"], bias_by_kind[0], bias_by_kind[1], L0["b_q2"]], axis=1)
    rows = np.concatenate([L0["b_kvx"][C:], bias_by_kind[2], A["b_out"]])
    agents = np.stack([L0["learnable_kv"][0].T, L0["learnable_q"][0].T], axis=1)
    arrays = {
        "xT": np.asarray(inputs["x"]).reshape(IMAGES * TOK, C).T, "consts": consts, "weights": weights,
        "cols": cols, "rows": rows, "agents": agents, "w_router": M["W_router"], "w1": M["W1"],
        "b1": M["b1"].reshape(EXPERTS, HB, P).transpose(2, 0, 1), "w2": M["W2"], "b2": M["b2"].T}

    nc = bacc.Bacc("TRN2", target_bir_lowering=False, num_devices=1)
    args = {}
    for name in arrays:
        a = arrays[name] = np.ascontiguousarray(arrays[name])
        args[name] = nc.dram_tensor(name, a.shape, mybir.dt.from_np(a.dtype), kind="ExternalInput").ap()
    out = nc.dram_tensor("out", (IMAGES * TILES, P, C), F32, kind="ExternalOutput").ap()
    hybrid_block(nc, out=out, **args)
    r = run_bass_kernel_spmd(nc, [arrays], core_ids=[0])
    return r.results[0]["out"].reshape(IMAGES, SIDE, SIDE, C)
```

```python
from contextlib import ExitStack

import concourse.bass as bass
from concourse import mybir

F32 = mybir.dt.float32
F32R = mybir.dt.float32r
BF16 = mybir.dt.bfloat16
U32 = mybir.dt.uint32
ALU = mybir.AluOpType
ACT = mybir.ActivationFunctionType
AX = mybir.AxisListType

P = 128
IMAGES = 8
SIDE = 16
TOK = SIDE * SIDE
TILES = TOK // P
C = 128
HEADS = 8
DK = C // HEADS
AGENTS = 16
CELL = 4
EXPERTS = 8
HID = 512
HB = HID // P
GROUP = 4
SCALE = DK ** -0.5
SLOTS = 17
TAIL = 11
KZ_DVE = 2
VSTEP = P + DK
LOW = 80.0

C_ID = 0
C_GRP = C_ID + P
C_CAUSAL = C_GRP + P
C_BD = C_CAUSAL + P
C_BDS = C_BD + HEADS
C_IOTA = C_BDS + HEADS
C_POW = C_IOTA + EXPERTS
C_N = C_POW + 2

W_KVYK, W_KVYV, W_Q, W_Q2T, W_F1W1, W_KT, W_F1W2, W_V, W_F2W1, W_F2W2, W_AQ, W_AK, W_AV, W_AO = range(14)
W_N = 14
(B_KYK, B_KYV, B_Q, B_PE1, B_PE2, B_F1B1, B_F1B2, B_F2B1, B_F2B2, B_AQ, B_AK, B_Q2) = range(12)
B_N = 12
R_BV, R_BAV, R_BO = range(3)
R_N = 3


class Signal:

    def __init__(self, ctx, nc, name, per=1):
        self.sem = ctx.enter_context(nc.semaphore(name))
        self.per = per

    def nth(self, i, k=1):
        return i * self.per + k

    def before(self, i):
        return i * self.per


def first(i):
    return isinstance(i, int) and i == 0


def hybrid_block(nc, xT, consts, weights, cols, rows, agents, w_router, w1, b1, w2, b2, out):
    ctx = ExitStack()
    with ctx:
        def sb(name, shape, dt=F32):
            return ctx.enter_context(nc.sbuf_tensor(name, shape, dt))

        def sig(name, per=1):
            return Signal(ctx, nc, name, per)

        x_all = sb("x_all", [P, IMAGES * TOK])
        cst = sb("cst", [P, C_N])
        W = sb("W", [P, W_N, P])
        col = sb("col", [P, B_N])
        row = sb("row", [P, R_N, P])
        agt = sb("agt", [P, 2, AGENTS])
        wr = sb("wr", [P, EXPERTS])
        w1raw = sb("w1raw", [P, EXPERTS, HID])
        w1hi = sb("w1hi", [P, EXPERTS, HID], F32R)
        w1lo = sb("w1lo", [P, EXPERTS, HID], F32R)
        w2s = sb("w2s", [P, EXPERTS, HB, C])
        b1s = sb("b1s", [P, EXPERTS, HB])
        b2s = sb("b2s", [P, C])
        ident = cst[:, C_ID:C_ID + P]
        grp = cst[:, C_GRP:C_GRP + P]
        bd = cst[:, C_BD:C_BD + HEADS]
        bds = cst[:, C_BDS:C_BDS + HEADS]
        iota = cst[:, C_IOTA:C_IOTA + EXPERTS]
        power = cst[:, C_POW:C_POW + 2]
        identb = sb("identb", [P, P], BF16)
        causalb = sb("causalb", [P, P], BF16)

        gst = sb("gst", [P, IMAGES, 6])
        gmv = sb("gmv", [P, IMAGES, 2])
        gmean = sb("gmean", [P, IMAGES])
        gdev = sb("gdev", [P, IMAGES])
        gvar = sb("gvar", [P, IMAGES])
        gn = sb("gn", [P, IMAGES, 2])
        kvq = sb("kvq", [P, 3, AGENTS])
        kvqd = sb("kvqd", [P, 3, HEADS, AGENTS])
        bq2b = sb("bq2b", [P, P])
        fold = sb("fold", [P, 4, P])
        m1, c1, m2, mkq = (fold[:, n, :] for n in range(4))
        zb = sb("zb", [P, 1])

        gni = sb("gni", [P, 2])
        xg = sb("xg", [P, TOK])
        xx = sb("xx", [P, TOK])
        s1 = sb("s1", [P, TILES, P])
        s1m = sb("s1m", [P, TILES * HEADS])
        s1c = sb("s1c", [P, TILES, P])
        e1 = sb("e1", [P, TILES, P])
        e1s = sb("e1s", [P, TILES * HEADS])
        e1r = sb("e1r", [P, TILES * HEADS])
        p1 = sb("p1", [P, TILES, P])
        p1T = sb("p1T", [P, TOK])
        ez = sb("ez", [P, TOK])
        za = sb("za", [P, TOK])
        zr = sb("zr", [P, TOK])
        zc = sb("zc", [P, TOK])
        yc = sb("yc", [P, AGENTS])
        zs = sb("zs", [P, TOK])
        oT = sb("oT", [P, TOK])
        base = sb("base", [P, TOK])
        s2m = sb("s2m", [P, 1])
        s2s = sb("s2s", [P, 1])
        s2r = sb("s2r", [P, 1])
        e2 = sb("e2", [P, TOK])
        p2 = sb("p2", [P, TOK])
        p2T = sb("p2T", [P, TILES, P])
        vx = sb("vx", [P, TILES, P])
        fm = sb("fm", [P, HEADS, AGENTS])
        fin = sb("fin", [P, AGENTS])
        ey = sb("ey", [P, AGENTS])
        ya = sb("ya", [P, AGENTS])
        yr = sb("yr", [P, AGENTS])
        ys = sb("ys", [P, AGENTS])
        fe = sb("fe", [P, AGENTS, CELL])
        x1T = sb("x1T", [P, TOK])

        lst = sb("lst", [P, TILES, 6])
        lmv = sb("lmv", [P, TILES, 2])
        lrs = sb("lrs", [P, TILES])
        lve = sb("lve", [P, TILES])
        ln1 = sb("ln1", [P, TILES, P])
        xl = sb("xl", [P, TILES, P])
        tb = sb("tb", [P, TILES, P])
        ln1T = sb("ln1T", [P, TOK])
        qT = sb("qT", [P, TOK])
        kT = sb("kT", [P, TOK])
        kz = sb("kz", [P, HEADS, TOK])
        vz = sb("vz", [P, TILES, HEADS * VSTEP])
        nm = sb("nm", [P, 2, 2])
        rsum = sb("rsum", [P, 2, 2])
        rinv = sb("rinv", [P, 2, 2])
        pe_ = sb("pe_", [P, 2, 3 * P])
        pn = sb("pn", [P, 2, 3 * P])
        pT = sb("pT", [P, 2, 3 * P])
        aT = sb("aT", [P, TOK])
        t2 = sb("t2", [P, TILES, P])
        nst = sb("nst", [P, TILES, 6])
        nmv = sb("nmv", [P, TILES, 2])
        nve = sb("nve", [P, TILES])
        nrs = sb("nrs", [P, TILES])
        ln2 = sb("ln2", [P, TILES, P])
        ln2T = sb("ln2T", [P, TOK])
        xhi = sb("xhi", [P, TOK], F32R)
        xlo = sb("xlo", [P, TOK], F32R)
        lg = sb("lg", [P, TILES, EXPERTS])
        top = sb("top", [P, TILES, 8])
        tix = sb("tix", [P, TILES, 8], U32)
        tif = sb("tif", [P, TILES, 2])
        td = sb("td", [P, TILES])
        te = sb("te", [P, TILES])
        ta = sb("ta", [P, TILES])
        tw = sb("tw", [P, TILES, 2])
        pick = sb("pick", [P, 2, TILES, EXPERTS])
        part = sb("part", [P, 2, TILES, EXPERTS])
        comb = sb("comb", [P, TILES, P])

        hf = sb("hf", [P, 2, HB, TOK])
        combT = sb("combT", [P, TOK])
        acc = sb("acc", [P, TILES, P])
        ob = sb("ob", [P, TILES, P])

        bH = [ctx.enter_context(nc.psum_tensor(f"bH{n}", [P, 2 * TOK], F32)) for n in range(2)]
        bY = ctx.enter_context(nc.psum_tensor("bY", [P, 2 * TOK], F32))
        bA = ctx.enter_context(nc.psum_tensor("bA", [P, 2 * TOK], F32))
        bS = [ctx.enter_context(nc.psum_tensor(f"bS{n}", [P, 2 * TOK], F32)) for n in range(2)]
        bT = ctx.enter_context(nc.psum_tensor("bT", [P, 2 * TOK], F32))
        bL = ctx.enter_context(nc.psum_tensor("bL", [P, 2 * TOK], F32))

        def tiles(ap):
            return ap.rearrange("p (t n) -> p t n", n=P)

        sem = lambda name: ctx.enter_context(nc.semaphore(name))
        ld_x, ld_c, ld_w, ld_1, ld_2 = (sem(n) for n in ("ld_x", "ld_c", "ld_w", "ld_1", "ld_2"))
        su_zero, su_cast, su_dve, su_pe, su_act, su_pow, su_w1 = (
            sem(n) for n in ("su_zero", "su_cast", "su_dve", "su_pe", "su_act", "su_pow", "su_w1"))
        gate = [sem(f"gate{n}") for n in range(2)]

        l0_gn, l0_xg, l0_xx = sig("l0_gn"), sig("l0_xg"), sig("l0_xx")
        l0_s1, l0_s1b, l0_m1, l0_s1c, l0_e1 = sig("l0_s1"), sig("l0_s1b"), sig("l0_m1"), sig("l0_s1c"), sig("l0_e1")
        l0_sum, l0_r1, l0_p1, l0_pt, l0_ptc = sig("l0_sum"), sig("l0_r1"), sig("l0_p1"), sig("l0_pt"), sig("l0_ptc")
        l0_zc, l0_yc = sig("l0_zc"), sig("l0_yc")
        l0_z, l0_ez, l0_za, l0_zr, l0_zs = sig("l0_z"), sig("l0_ez"), sig("l0_za"), sig("l0_zr"), sig("l0_zs")
        l0_o, l0_ot, l0_base = sig("l0_o"), sig("l0_ot"), sig("l0_base")
        l0_s2, l0_m2, l0_e2, l0_r2, l0_p2 = sig("l0_s2"), sig("l0_m2"), sig("l0_e2"), sig("l0_r2"), sig("l0_p2")
        l0_v, l0_vx, l0_qt, l0_qtc = sig("l0_v"), sig("l0_vx"), sig("l0_qt"), sig("l0_qtc")
        l0_f, l0_fm, l0_fin = sig("l0_f"), sig("l0_fm"), sig("l0_fin")
        l0_y, l0_ey, l0_ya, l0_yr, l0_ys = sig("l0_y"), sig("l0_ey"), sig("l0_ya"), sig("l0_yr"), sig("l0_ys")
        l0_w, l0_fe, l0_x1 = sig("l0_w"), sig("l0_fe"), sig("l0_x1")

        at_xt, at_st, at_mv, at_rs = sig("at_xt"), sig("at_st", 2), sig("at_mv", 3), sig("at_rs")
        at_ln, at_xl, at_tb = sig("at_ln", 2), sig("at_xl"), sig("at_tb")
        at_lt, at_ltc = sig("at_lt"), sig("at_ltc")
        at_qk, at_v, at_k, at_vz, at_kz = sig("at_qk"), sig("at_v"), sig("at_k"), sig("at_vz"), sig("at_kz", KZ_DVE)
        at_kzp = sig("at_kzp", HEADS - KZ_DVE)
        at_s, at_m, at_e, at_r = sig("at_s", HEADS), sig("at_m", HEADS), sig("at_e", 2 * HEADS), sig("at_r", HEADS)
        at_p, at_t, at_tc, at_pv = sig("at_p", HEADS), sig("at_t", HEADS), sig("at_tc", HEADS), sig("at_pv", HEADS)
        at_o, at_w, at_t2 = sig("at_o"), sig("at_w"), sig("at_t2")
        at_nst, at_nmv, at_nrs, at_n2 = sig("at_nst", 2), sig("at_nmv", 3), sig("at_nrs"), sig("at_n2", 2)
        at_nt, at_ntc, at_xs, at_xl2 = sig("at_nt"), sig("at_ntc"), sig("at_xs"), sig("at_xl2")
        at_l, at_lg, at_top, at_tix, at_tif = sig("at_l"), sig("at_lg"), sig("at_top", 2), sig("at_tix", 2), sig("at_tif")
        at_td, at_te, at_ta, at_tw, at_pick, at_share = sig("at_td"), sig("at_te"), sig("at_ta"), sig("at_tw", 2), sig("at_pick", 2), sig("at_share", 2)
        at_comb = sig("at_comb")

        mo_h, mo_r, mo_y = sig("mo_h", 2 * EXPERTS), sig("mo_r", HB * EXPERTS), sig("mo_y", EXPERTS)
        mo_ct, mo_ctc, mo_acc = sig("mo_ct"), sig("mo_ctc"), sig("mo_acc", 1 + TILES * (EXPERTS - 1))
        mo_ob, mo_out = sig("mo_ob", TILES), sig("mo_out", 16)

        block = ctx.enter_context(nc.Block())

        S_SLOT = {h: h for h in range(HEADS)}
        T_SLOT = {h: S_SLOT[h] + 2 for h in range(HEADS)}
        V_SLOT = {h: S_SLOT[h] + 3 for h in range(HEADS)}

        G1_SLOT = dict(enumerate((0, 1, 4, 6, 8, 10, 12, 13)))
        G2_SLOT = dict(enumerate((2, 5, 7, 9, 11, 13, 14, 15)))

        def y_bank(e):
            return bS[1] if e in (5, 7) else bY

        def heads_in(plan, s):
            return [h for h in range(HEADS) if plan[h] == s]

        def pipeline(eng, step, before_experts=lambda: None):
            step(0, None, None)
            step(1, 0, None)
            before_experts()
            step(2, 1, 0)
            with eng.Fori(1, IMAGES - 2) as i:
                step(i + 2, i + 1, i)
            step(None, IMAGES - 1, IMAGES - 2)
            step(None, None, IMAGES - 1)

        @block.sync
        def _(sp):
            sp.dma_start(x_all[:, 0:4 * TOK], xT[:, 0:4 * TOK]).then_inc(ld_x, 16)
            sp.dma_start(x_all[:, 4 * TOK:], xT[:, 4 * TOK:]).then_inc(ld_x, 16)
            sp.dma_start(cst[:, :], consts).then_inc(ld_c, 16)
            sp.dma_start(W[:, :, :], weights).then_inc(ld_w, 16)
            for e in range(EXPERTS):
                sp.dma_start(w1raw[:, e, :], w1[e]).then_inc(ld_1, 16)
                sp.dma_start(w2s[:, e, :, :], w2[e].rearrange("(k p) c -> p k c", p=P)).then_inc(ld_2, 16)

            def step(l0, at, mo):
                if mo is None:
                    return
                sp.wait_ge(mo_ob.sem, mo_ob.nth(mo, TILES))
                sp.dma_start(out[bass.ds(mo * TILES, TILES), :, :].rearrange("t p c -> p t c"), ob[:, :, :])\
                  .then_inc(mo_out.sem, 16)

            pipeline(sp, step)
            sp.wait_ge(mo_out.sem, mo_out.per * IMAGES)

        @block.gpsimd
        def _(pool):
            pool.memset(b2s[:, :], 0.0).then_inc(su_zero, 1)
            pool.memset(comb[:, :, :], 0.0).then_inc(su_zero, 1)
            pool.memset(vz[:, :, :], 0.0).then_inc(su_zero, 1)
            pool.wait_ge(ld_c, 64)
            pool.wait_ge(su_dve, 6)
            pool.tensor_tensor(gn[:, :, 0], gvar[:, :], power[:, 0:1].broadcast_to([P, IMAGES]), ALU.pow)\
                .then_inc(su_pow, 1)

            def l0_part(s, i):
                if s == 6:
                    pool.wait_ge(l0_ot.sem, l0_ot.nth(i))
                    pool.wait_ge(l0_xx.sem, l0_xx.nth(i))
                    if not first(i):
                        pool.wait_ge(l0_x1.sem, l0_x1.before(i))
                    pool.tensor_tensor(base[:, :], xx[:, :], oT[:, :], ALU.add).then_inc(l0_base.sem, 1)
                if s == 12:
                    pool.wait_ge(at_mv.sem, at_mv.nth(i, 3))
                    pool.tensor_tensor(lrs[:, :], lve[:, :], power[:, 0:1].broadcast_to([P, TILES]), ALU.pow)\
                        .then_inc(at_rs.sem, 1)
                if s == 13:
                    pool.wait_ge(at_xl.sem, at_xl.nth(i))
                    if not first(i):
                        pool.wait_ge(at_t2.sem, at_t2.before(i))
                    pool.tensor_tensor(tb[:, :, :], xl[:, :, :],
                                       row[:, R_BO, :].unsqueeze(1).broadcast_to([P, TILES, P]), ALU.add)\
                        .then_inc(at_tb.sem, 1)
                if s == 16:
                    if not first(i):
                        pool.wait_ge(at_s.sem, at_s.before(i))
                    pool.wait_ge(at_k.sem, at_k.nth(i))
                    for h in range(KZ_DVE, HEADS):
                        pool.tensor_tensor(kz[:, h, :], kT[:, :], bd[:, h:h + 1].broadcast_to([P, TOK]), ALU.mult)\
                            .then_inc(at_kzp.sem, 1)

            def at_part(s, i):
                for h in heads_in(S_SLOT, s - 1):
                    b = h % 2
                    pool.wait_ge(at_r.sem, at_r.nth(i, h + 1))
                    if h >= 2:
                        pool.wait_ge(at_t.sem, at_t.nth(i, h - 1))
                    elif not first(i):
                        pool.wait_ge(at_t.sem, at_t.before(i))
                    pool.tensor_tensor(pn[:, b, 0:P], pe_[:, b, 0:P],
                                       rinv[:, b, 0:1].broadcast_to([P, P]), ALU.mult)
                    pool.tensor_tensor(pn[:, b, P:3 * P], pe_[:, b, P:3 * P],
                                       rinv[:, b, 1:2].broadcast_to([P, 2 * P]), ALU.mult).then_inc(at_p.sem, 1)
                if s == 11:
                    pool.wait_ge(at_nmv.sem, at_nmv.nth(i, 3))
                    pool.tensor_tensor(nrs[:, :], nve[:, :], power[:, 0:1].broadcast_to([P, TILES]), ALU.pow)\
                        .then_inc(at_nrs.sem, 1)

                if s == 15:
                    if not first(i):
                        pool.wait_ge(mo_h.sem, mo_h.before(i))
                    pool.wait_ge(at_xs.sem, at_xs.nth(i))
                    pool.tensor_tensor(xlo[:, :], ln2T[:, :], xhi[:, :].bitcast(F32), ALU.subtract)\
                        .then_inc(at_xl2.sem, 1)

            def step(l0, at, mo):
                for s in range(SLOTS):
                    if at is not None:
                        at_part(s, at)
                    if l0 is not None:
                        l0_part(s, l0)

            pipeline(pool, step)

        @block.scalar
        def _(act):
            act.dma_start(col[:, :], cols).then_inc(ld_c, 16)
            act.dma_start(row[:, :, :].rearrange("p a b -> p (a b)"), rows.partition_broadcast(P)).then_inc(ld_c, 16)
            act.dma_start(agt[:, :, :], agents).then_inc(ld_c, 16)
            act.dma_start(wr[:, :], w_router).then_inc(ld_w, 16)
            act.dma_start(b1s[:, :, :], b1).then_inc(ld_w, 16)
            act.wait_ge(su_zero, 1)
            act.dma_start(b2s[0:EXPERTS, :], b2).then_inc(ld_w, 16)
            act.wait_ge(su_pe, 4)
            act.activation(fold[:, :, :].rearrange("p a b -> p (a b)"), bS[1][:, :], ACT.Copy).then_inc(su_act, 1)

            def l0_part(s, i):
                if s == 0:
                    act.wait_ge(l0_s1c.sem, l0_s1c.nth(i))
                    if not first(i):
                        act.wait_ge(l0_p1.sem, l0_p1.before(i))
                    act.activation(e1[:, :, :], s1c[:, :, :], ACT.Exp).then_inc(l0_e1.sem, 1)
                if s == 2:
                    act.wait_ge(l0_pt.sem, l0_pt.nth(i))
                    act.activation(p1T[:, :], bL[:, 0:TOK], ACT.Copy).then_inc(l0_ptc.sem, 1)
                if s == 3:
                    act.wait_ge(l0_zc.sem, l0_zc.nth(i))
                    if not first(i):
                        act.wait_ge(l0_za.sem, l0_za.before(i))
                    act.activation(ez[:, :], zc[:, :], ACT.Exp, scale=-1.0)\
                       .then_inc(l0_ez.sem, 1)
                if s == 6:
                    act.wait_ge(l0_m2.sem, l0_m2.nth(i))
                    if not first(i):
                        act.wait_ge(l0_p2.sem, l0_p2.before(i))
                    act.activation(e2[:, :], bL[:, 0:TOK], ACT.Exp, bias=s2m[:, 0:1], accum_out=s2s[:, 0:1])\
                       .then_inc(l0_e2.sem, 1)
                if s == 8:
                    act.wait_ge(l0_qt.sem, l0_qt.nth(i))
                    act.activation(p2T[:, :, :].rearrange("p t n -> p (t n)"), bL[:, 0:TOK], ACT.Copy)\
                       .then_inc(l0_qtc.sem, 1)
                if s == 10:
                    act.wait_ge(l0_yc.sem, l0_yc.nth(i))
                    if not first(i):
                        act.wait_ge(l0_ya.sem, l0_ya.before(i))
                    act.activation(ey[:, :], yc[:, :], ACT.Exp, scale=-1.0)\
                       .then_inc(l0_ey.sem, 1)
                if s == 14:
                    act.wait_ge(at_lt.sem, at_lt.nth(i))
                    act.activation(ln1T[:, :], bL[:, 0:TOK], ACT.Copy).then_inc(at_ltc.sem, 1)

            def at_part(s, i):
                for h in heads_in(T_SLOT, s):
                    b = h % 2
                    act.wait_ge(at_t.sem, at_t.nth(i, h + 1))
                    if h >= 2:
                        act.wait_ge(at_pv.sem, at_pv.nth(i, h - 1))
                    elif not first(i):
                        act.wait_ge(at_pv.sem, at_pv.before(i))
                    act.activation(pT[:, b, :], bT[:, 0:3 * P], ACT.Copy).then_inc(at_tc.sem, 1)
                for h in heads_in(S_SLOT, s):
                    b = h % 2
                    if h >= 2:
                        act.wait_ge(at_p.sem, at_p.nth(i, h - 1))
                    elif not first(i):
                        act.wait_ge(at_p.sem, at_p.before(i))
                    act.wait_ge(at_m.sem, at_m.nth(i, h + 1))
                    act.activation(pe_[:, b, 0:P], bS[b][:, 0:P], ACT.Exp, bias=nm[:, b, 0:1],
                                   accum_out=rsum[:, b, 0:1]).then_inc(at_e.sem, 1)
                    act.activation(pe_[:, b, P:3 * P], bS[b][:, P:3 * P], ACT.Exp, bias=nm[:, b, 1:2],
                                   accum_out=rsum[:, b, 1:2]).then_inc(at_e.sem, 1)
                if s == 10:
                    act.wait_ge(at_pv.sem, at_pv.nth(i, HEADS))
                    act.activation(aT[:, :], bA[:, 0:TOK], ACT.Copy).then_inc(at_o.sem, 1)
                if s == 13:
                    act.wait_ge(at_nt.sem, at_nt.nth(i))
                    act.activation(ln2T[:, :], bA[:, 0:TOK], ACT.Copy).then_inc(at_ntc.sem, 1)
                    act.wait_ge(at_ntc.sem, at_ntc.nth(i))
                    if not first(i):
                        act.wait_ge(mo_h.sem, mo_h.before(i))
                    act.activation(xhi[:, :], ln2T[:, :], ACT.Copy).then_inc(at_xs.sem, 1)
                if s == 14:
                    act.wait_ge(at_td.sem, at_td.nth(i))
                    act.activation(te[:, :], td[:, :], ACT.Exp).then_inc(at_te.sem, 1)

            def mo_part(s, i):
                if s == 1:
                    if not first(i):
                        act.wait_ge(mo_y.sem, mo_y.before(i))
                    act.wait_ge(mo_ct.sem, mo_ct.nth(i))
                    act.activation(combT[:, :], bY[:, 0:TOK], ACT.Copy).then_inc(mo_ctc.sem, 1)
                for e in heads_in(G1_SLOT, s):
                    for k in range(HB):
                        if k % 2 == 0:
                            act.wait_ge(mo_h.sem, mo_h.nth(i, 2 * e + k // 2 + 1))
                        if k == 0:
                            if e >= 2:
                                act.wait_ge(mo_y.sem, mo_y.nth(i, e - 1))
                            elif not first(i):
                                act.wait_ge(mo_y.sem, mo_y.before(i))
                        act.activation(hf[:, e % 2, k, :], bH[k // 2][:, (k % 2) * TOK:(k % 2 + 1) * TOK], ACT.Relu,
                                       bias=b1s[:, e, k:k + 1]).then_inc(mo_r.sem, 1)

            def step(l0, at, mo):
                for s in range(SLOTS):
                    if mo is not None and (s == 0 or s >= TAIL):
                        mo_part(s, mo)
                    if l0 is not None and s == 14:
                        l0_part(s, l0)
                    if at is not None:
                        at_part(s, at)
                    if l0 is not None and s != 14:
                        l0_part(s, l0)
                    if mo is not None and 0 < s < TAIL:
                        mo_part(s, mo)

            act.wait_ge(ld_c, 64)
            act.wait_ge(ld_w, 64)
            act.wait_ge(su_dve, 13)
            pipeline(act, step)

        @block.tensor
        def _(pe):
            pe.wait_ge(ld_c, 64)
            pe.wait_ge(ld_w, 64)
            pe.wait_ge(su_cast, 3)
            for n, (w, a) in enumerate(((W_KVYK, 0), (W_KVYV, 0), (W_Q, 1))):
                mm = pe.matmul(bS[0][:, n * AGENTS:(n + 1) * AGENTS], W[:, w, :], agt[:, a, :], start=True, stop=True)
            mm.then_inc(su_pe, 1)
            pe.wait_ge(su_dve, 1)
            pe.matmul(bH[0][:, 0:2 * IMAGES], grp, gmv[:, :, :].rearrange("p i k -> p (i k)"),
                      start=True, stop=True).then_inc(su_pe, 1)
            pe.wait_ge(su_dve, 5)
            pe.matmul(bH[1][:, 0:IMAGES], grp, gdev[:, :], start=True, stop=True).then_inc(su_pe, 1)
            pe.wait_ge(su_dve, 11)
            pe.matmul(bS[1][:, 0:P], W[:, W_Q2T, :], kvqd[:, 0, :, :].rearrange("p h m -> p (h m)"), start=True, stop=True)
            pe.matmul(bS[1][:, P:2 * P], bq2b[:, :], kvqd[:, 0, :, :].rearrange("p h m -> p (h m)"), start=True, stop=True)
            pe.matmul(bS[1][:, 2 * P:3 * P], kvqd[:, 1, :, :].rearrange("p h m -> p (h m)"), W[:, W_F1W1, :], start=True, stop=True)
            pe.matmul(bS[1][:, 3 * P:4 * P], W[:, W_KT, :], kvqd[:, 2, :, :].rearrange("p h m -> p (h m)"), start=True, stop=True)\
              .then_inc(su_pe, 1)
            pe.wait_ge(su_act, 1)
            pe.matmul(bT[:, 0:1], m2, col[:, B_PE1:B_PE1 + 1], start=True, stop=True).then_inc(su_pe, 1)
            pe.wait_ge(su_dve, 13)

            def l0_part(s, i):
                if s == 0:
                    pe.wait_ge(l0_xg.sem, l0_xg.nth(i))
                    if not first(i):
                        pe.wait_ge(at_k.sem, at_k.before(i))
                    for t in range(TILES):
                        mm = pe.matmul(bL[:, t * P:(t + 1) * P], xg[:, t * P:(t + 1) * P], m1, start=True, stop=True)
                    mm.then_inc(l0_s1.sem, 1)
                if s == 2:
                    pe.wait_ge(l0_p1.sem, l0_p1.nth(i))
                    for t in range(TILES):
                        mm = pe.transpose(bL[:, t * P:(t + 1) * P], p1[:, t, :], ident)
                    mm.then_inc(l0_pt.sem, 1)
                if s == 3:
                    pe.wait_ge(l0_ptc.sem, l0_ptc.nth(i))
                    pe.matmul(bL[:, 0:TOK], m2, p1T[:, :], start=True, stop=True).then_inc(l0_z.sem, 1)
                if s == 5:
                    pe.wait_ge(l0_zs.sem, l0_zs.nth(i))
                    pe.matmul(bL[:, 0:TOK], W[:, W_F1W2, :], zs[:, :], start=True, stop=True).then_inc(l0_o.sem, 1)
                if s == 6:
                    pe.wait_ge(l0_ot.sem, l0_ot.nth(i))
                    pe.matmul(bL[:, 0:TOK], mkq, oT[:, :], start=True, stop=True).then_inc(l0_s2.sem, 1)
                if s == 7:
                    pe.wait_ge(l0_e2.sem, l0_e2.nth(i))
                    for t in range(TILES):
                        mm = pe.matmul(bL[:, t * P:(t + 1) * P], oT[:, t * P:(t + 1) * P], W[:, W_V, :], start=True, stop=True)
                    mm.then_inc(l0_v.sem, 1)
                if s == 8:
                    pe.wait_ge(l0_p2.sem, l0_p2.nth(i))
                    pe.wait_ge(l0_vx.sem, l0_vx.nth(i))
                    for t in range(TILES):
                        mm = pe.transpose(bL[:, t * P:(t + 1) * P], p2[:, t * P:(t + 1) * P], ident)
                    mm.then_inc(l0_qt.sem, 1)
                if s == 9:
                    pe.wait_ge(l0_qtc.sem, l0_qtc.nth(i))
                    for t in range(TILES):
                        mm = pe.matmul(bL[:, 0:P], vx[:, t, :], p2T[:, t, :], start=(t == 0), stop=(t == TILES - 1))
                    mm.then_inc(l0_f.sem, 1)
                if s == 10:
                    pe.wait_ge(l0_fin.sem, l0_fin.nth(i))
                    pe.matmul(bL[:, 0:AGENTS], W[:, W_F2W1, :], fin[:, :], start=True, stop=True).then_inc(l0_y.sem, 1)
                if s == 11:
                    pe.wait_ge(l0_ys.sem, l0_ys.nth(i))
                    pe.matmul(bL[:, 0:AGENTS], W[:, W_F2W2, :], ys[:, :], start=True, stop=True).then_inc(l0_w.sem, 1)
                if s == 12:
                    pe.wait_ge(l0_x1.sem, l0_x1.nth(i))
                    for t in range(TILES):
                        mm = pe.transpose(bL[:, t * P:(t + 1) * P], x1T[:, t * P:(t + 1) * P], ident)
                    mm.then_inc(at_xt.sem, 1)
                if s == 14:
                    pe.wait_ge(at_xl.sem, at_xl.nth(i))
                    for t in range(TILES):
                        mm = pe.transpose(bL[:, t * P:(t + 1) * P], ln1[:, t, :], ident)
                    mm.then_inc(at_lt.sem, 1)
                if s == 15:
                    pe.wait_ge(at_ltc.sem, at_ltc.nth(i))
                    pe.matmul(bL[:, 0:TOK], W[:, W_AQ, :], ln1T[:, :], start=True, stop=True)
                    pe.matmul(bL[:, TOK:2 * TOK], W[:, W_AK, :], ln1T[:, :], start=True, stop=True)\
                      .then_inc(at_qk.sem, 1)
                if s == 16:
                    if not first(i):
                        pe.wait_ge(at_tc.sem, at_tc.before(i))
                    for t in range(TILES):
                        mm = pe.matmul(bT[:, t * P:(t + 1) * P], ln1T[:, t * P:(t + 1) * P], W[:, W_AV, :],
                                       start=True, stop=True)
                    mm.then_inc(at_v.sem, 1)

            def at_part(s, i):
                for h in heads_in(V_SLOT, s):
                    b = h % 2
                    if h == 0:
                        pe.wait_ge(at_vz.sem, at_vz.nth(i))
                        if not first(i):
                            pe.wait_ge(at_lg.sem, at_lg.before(i))
                    pe.wait_ge(at_tc.sem, at_tc.nth(i, h + 1))
                    pe.matmul(bA[:, 0:TOK], vz[:, 0, h * P:(h + 1) * P], pT[:, b, 0:TOK],
                              start=(h == 0), stop=False)
                    pe.matmul(bA[:, P:TOK], vz[:, 1, h * P:(h + 1) * P], pT[:, b, TOK:3 * P],
                              start=False, stop=(h == HEADS - 1)).then_inc(at_pv.sem, 1)
                for h in heads_in(T_SLOT, s):
                    b = h % 2
                    pe.wait_ge(at_p.sem, at_p.nth(i, h + 1))
                    if h >= 1:
                        pe.wait_ge(at_tc.sem, at_tc.nth(i, h))
                    else:
                        pe.wait_ge(at_vz.sem, at_vz.nth(i))
                    pe.transpose(bT[:, 0:P], pn[:, b, 0:P], ident)
                    pe.transpose(bT[:, P:2 * P], pn[:, b, P:2 * P], ident)
                    pe.transpose(bT[:, 2 * P:3 * P], pn[:, b, 2 * P:3 * P], ident).then_inc(at_t.sem, 1)
                for h in heads_in(S_SLOT, s):
                    b = h % 2
                    if h < KZ_DVE:
                        pe.wait_ge(at_kz.sem, at_kz.nth(i, h + 1))
                    else:
                        pe.wait_ge(at_kzp.sem, at_kzp.nth(i, h - KZ_DVE + 1))
                    if h < 2 and not first(i):
                        pe.wait_ge(at_e.sem, at_e.before(i))
                    if h == 1 and not (isinstance(i, int) and i < 2):
                        pe.wait_ge(mo_ob.sem, mo_ob.nth(i - 2, TILES))
                    if h >= 2:
                        pe.wait_ge(at_e.sem, at_e.nth(i, 2 * (h - 1)))
                    pe.matmul(bS[b][:, 0:P], qT[:, 0:P], kz[:, h, 0:P], start=True, stop=False)
                    pe.matmul(bS[b][:, 0:P], identb[:, :], causalb[:, :], start=False, stop=True)
                    pe.matmul(bS[b][:, P:3 * P], qT[:, P:2 * P], kz[:, h, :], start=True, stop=False)
                    pe.matmul(bS[b][:, 2 * P:3 * P], identb[:, :], causalb[:, :], start=False, stop=True)\
                      .then_inc(at_s.sem, 1)
                if s == 11:
                    pe.wait_ge(at_o.sem, at_o.nth(i))
                    for t in range(TILES):
                        mm = pe.matmul(bA[:, t * P:(t + 1) * P], aT[:, t * P:(t + 1) * P], W[:, W_AO, :],
                                       start=True, stop=True)
                    mm.then_inc(at_w.sem, 1)
                if s == 13:
                    pe.wait_ge(at_n2.sem, at_n2.nth(i, 2))
                    for t in range(TILES):
                        mm = pe.transpose(bA[:, t * P:(t + 1) * P], ln2[:, t, :], ident)
                    mm.then_inc(at_nt.sem, 1)
                if s == 14:
                    pe.wait_ge(at_ntc.sem, at_ntc.nth(i))
                    for t in range(TILES):
                        mm = pe.matmul(bA[:, t * EXPERTS:(t + 1) * EXPERTS], ln2T[:, t * P:(t + 1) * P], wr[:, :],
                                       start=True, stop=True)
                    mm.then_inc(at_l.sem, 1)

            def mo_first(e, i):
                if e == 0:
                    pe.wait_ge(at_xl2.sem, at_xl2.nth(i))
                for k in range(HB):
                    if k % 2 == 0:
                        if e >= 1:
                            pe.wait_ge(mo_r.sem, mo_r.nth(i, HB * (e - 1) + k + 2))
                        elif not first(i):
                            pe.wait_ge(mo_r.sem, mo_r.before(i))
                    hk = bH[k // 2][:, (k % 2) * TOK:(k % 2 + 1) * TOK]
                    wk = slice(k * P, (k + 1) * P)
                    pe.matmul(hk, w1hi[:, e, wk], xhi[:, :], start=True, stop=False)
                    pe.matmul(hk, w1hi[:, e, wk], xlo[:, :], start=False, stop=False)
                    mm = pe.matmul(hk, w1lo[:, e, wk], xhi[:, :], start=False, stop=True)
                    if k % 2 == 1:
                        mm.then_inc(mo_h.sem, 1)

            def mo_second(e, i, at):
                earlier = [n for n in range(e) if y_bank(n) is y_bank(e)]
                if earlier:
                    pe.wait_ge(mo_acc.sem, mo_acc.nth(i, 1 + TILES * (earlier[-1] + 1)))
                if e == 0:
                    pe.wait_ge(mo_ctc.sem, mo_ctc.nth(i))
                    for t in range(TILES):
                        pe.matmul(bY[:, TOK + t * P:TOK + (t + 1) * P], combT[:, t * P:(t + 1) * P], b2s[:, :],
                                  start=True, stop=True)
                if e == 5 and at is not None:
                    pe.wait_ge(at_e.sem, at_e.nth(at, 2 * HEADS))
                pe.wait_ge(mo_r.sem, mo_r.nth(i, HB * (e + 1)))
                for t in range(TILES):
                    for k in range(HB):
                        mm = pe.matmul(y_bank(e)[:, t * P:(t + 1) * P], hf[:, e % 2, k, t * P:(t + 1) * P], w2s[:, e, k, :],
                                       start=(k == 0), stop=(k == HB - 1))
                mm.then_inc(mo_y.sem, 1)

            def mo_part(s, i, at):
                if s == 1:
                    pe.wait_ge(at_comb.sem, at_comb.nth(i))
                    if not first(i):
                        pe.wait_ge(mo_ob.sem, mo_ob.before(i))
                    for t in range(TILES):
                        mm = pe.transpose(bY[:, t * P:(t + 1) * P], comb[:, t, :], ident)
                    mm.then_inc(mo_ct.sem, 1)
                for e in heads_in(G2_SLOT, s):
                    mo_second(e, i, at)
                for e in heads_in(G1_SLOT, s):
                    mo_first(e, i)

            def step(l0, at, mo):
                for s in range(SLOTS):
                    if l0 is not None and s == 15:
                        l0_part(s, l0)
                    if mo is not None and (s == 0 or s >= TAIL):
                        mo_part(s, mo, at)
                    if l0 is not None and s in (11, 14):
                        l0_part(s, l0)
                    if at is not None:
                        at_part(s, at)
                    if l0 is not None and s not in (11, 14, 15):
                        l0_part(s, l0)
                    if mo is not None and 0 < s < TAIL:
                        mo_part(s, mo, at)

            def weights_ready():
                pe.wait_ge(ld_2, 16 * EXPERTS)
                pe.wait_ge(su_w1, 2 * EXPERTS)

            pipeline(pe, step, weights_ready)

        @block.vector
        def _(dve):
            done = [0]

            def after(ins):
                done[0] += 1
                ins.then_inc(su_dve, 1)
                dve.wait_ge(su_dve, done[0])

            dve.wait_ge(ld_x, 32)
            for n in range(IMAGES):
                last = dve.bn_stats(gst[:, n, :], x_all[:, n * TOK:(n + 1) * TOK])
            last.then_inc(su_cast, 1)
            dve.wait_ge(ld_c, 64)
            dve.tensor_copy(identb[:, :], ident).then_inc(su_cast, 1)
            dve.tensor_copy(causalb[:, :], cst[:, C_CAUSAL:C_CAUSAL + P]).then_inc(su_cast, 1)
            dve.wait_ge(su_cast, 3)
            for n in range(IMAGES):
                last = dve.bn_aggr(gmv[:, n, :], gst[:, n, :])
            after(last)
            dve.wait_ge(su_pe, 2)
            after(dve.tensor_copy(gmean[:, :], bH[0][:, 0:2 * IMAGES].rearrange("p (i k) -> p i k", k=2)[:, :, 0]))
            after(dve.tensor_tensor(gdev[:, :], gmv[:, :, 0], gmean[:, :], ALU.subtract))
            after(dve.tensor_tensor(gvar[:, :], gdev[:, :], gdev[:, :], ALU.mult))
            after(dve.tensor_tensor(gdev[:, :], gvar[:, :], gmv[:, :, 1], ALU.add))
            dve.wait_ge(su_pe, 3)
            after(dve.tensor_scalar(gvar[:, :], bH[1][:, 0:IMAGES], 1e-5, None, ALU.add))
            after(dve.tensor_tensor(kvq[:, :, :], bS[0][:, 0:3 * AGENTS].rearrange("p (n m) -> p n m", n=3),
                                    col[:, B_KYK:B_Q + 1].unsqueeze(2).broadcast_to([P, 3, AGENTS]), ALU.add))
            for n, mask in enumerate((bds, bd, bds)):
                after(dve.tensor_tensor(kvqd[:, n, :, :], kvq[:, n, :].unsqueeze(1).broadcast_to([P, HEADS, AGENTS]),
                                        mask.unsqueeze(2).broadcast_to([P, HEADS, AGENTS]), ALU.mult))
            after(dve.tensor_copy(bq2b[:, :], col[:, B_Q2:B_Q2 + 1].broadcast_to([P, P])))
            dve.wait_ge(su_pow, 1)
            after(dve.scalar_tensor_tensor(out=gn[:, :, 1], in0=gmean[:, :], scalar=-1.0, in1=gn[:, :, 0],
                                           op0=ALU.mult, op1=ALU.mult))
            dve.wait_ge(su_pe, 5)
            after(dve.tensor_tensor(zb[:, :], bT[:, 0:1], col[:, B_F1B1:B_F1B1 + 1], ALU.add))

            def split_w1(e):
                dve.wait_ge(ld_1, 16 * EXPERTS)
                dve.tensor_copy(w1hi[:, e, :], w1raw[:, e, :]).then_inc(su_w1, 1)
                dve.wait_ge(su_w1, 2 * e + 1)
                dve.tensor_tensor(w1lo[:, e, :], w1raw[:, e, :], w1hi[:, e, :].bitcast(F32), ALU.subtract)\
                   .then_inc(su_w1, 1)

            def l0_late(s, i):
                if s == 0:
                    dve.tensor_copy(gni[:, :], gn[:, bass.ds(i, 1), :].rearrange("p a k -> p (a k)")).then_inc(l0_gn.sem, 1)
                    x_i = x_all[:, bass.ds(i * TOK, TOK)]
                    if not first(i):
                        dve.wait_ge(l0_s1.sem, l0_s1.before(i))
                    dve.wait_ge(l0_gn.sem, l0_gn.nth(i))
                    dve.tensor_scalar(xg[:, :], x_i, gni[:, 0:1], gni[:, 1:2], ALU.mult, ALU.add)\
                       .then_inc(l0_xg.sem, 1)
                if s == 2:
                    egrouped = e1[:, :, :].rearrange("p t (h m) -> p (t h) m", m=AGENTS)
                    dve.wait_ge(l0_e1.sem, l0_e1.nth(i))
                    dve.tensor_reduce(e1s[:, :], egrouped, AX.X, ALU.add).then_inc(l0_sum.sem, 1)
                    dve.wait_ge(l0_sum.sem, l0_sum.nth(i))
                    dve.reciprocal(e1r[:, :], e1s[:, :]).then_inc(l0_r1.sem, 1)
                    if not first(i):
                        dve.wait_ge(l0_pt.sem, l0_pt.before(i))
                    dve.wait_ge(l0_r1.sem, l0_r1.nth(i))
                    dve.tensor_tensor(p1[:, :, :].rearrange("p t (h m) -> p (t h) m", m=AGENTS), egrouped,
                                      e1r[:, :].unsqueeze(2).broadcast_to([P, TILES * HEADS, AGENTS]),
                                      ALU.mult).then_inc(l0_p1.sem, 1)
                if s == 3:
                    if not first(i):
                        dve.wait_ge(l0_base.sem, l0_base.before(i))
                    dve.wait_ge(l0_xg.sem, l0_xg.nth(i))
                    dve.tensor_tensor(xx[:, :], x_all[:, bass.ds(i * TOK, TOK)], xg[:, :], ALU.add).then_inc(l0_xx.sem, 1)
                if s == 4:
                    dve.wait_ge(l0_ez.sem, l0_ez.nth(i))
                    dve.tensor_scalar(za[:, :], ez[:, :], 1.0, None, ALU.add).then_inc(l0_za.sem, 1)
                    dve.wait_ge(l0_za.sem, l0_za.nth(i))
                    dve.reciprocal(zr[:, :], za[:, :]).then_inc(l0_zr.sem, 1)
                    if not first(i):
                        dve.wait_ge(l0_o.sem, l0_o.before(i))
                    dve.wait_ge(l0_zr.sem, l0_zr.nth(i))
                    dve.scalar_tensor_tensor(out=zs[:, :], in0=bL[:, 0:TOK], scalar=zb[:, 0:1], in1=zr[:, :],
                                             op0=ALU.add, op1=ALU.mult).then_inc(l0_zs.sem, 1)
                if s == 7:
                    dve.wait_ge(l0_e2.sem, l0_e2.nth(i))
                    dve.reciprocal(s2r[:, :], s2s[:, :]).then_inc(l0_r2.sem, 1)
                    if not first(i):
                        dve.wait_ge(l0_qt.sem, l0_qt.before(i))
                    dve.wait_ge(l0_r2.sem, l0_r2.nth(i))
                    dve.tensor_scalar(p2[:, :], e2[:, :], s2r[:, 0:1], col[:, B_PE2:B_PE2 + 1], ALU.mult, ALU.add)\
                       .then_inc(l0_p2.sem, 1)
                if s == 11:
                    dve.wait_ge(l0_ey.sem, l0_ey.nth(i))
                    dve.tensor_scalar(ya[:, :], ey[:, :], 1.0, None, ALU.add).then_inc(l0_ya.sem, 1)
                    dve.wait_ge(l0_ya.sem, l0_ya.nth(i))
                    dve.reciprocal(yr[:, :], ya[:, :]).then_inc(l0_yr.sem, 1)
                    if not first(i):
                        dve.wait_ge(l0_w.sem, l0_w.before(i))
                    dve.wait_ge(l0_yr.sem, l0_yr.nth(i))
                    dve.scalar_tensor_tensor(out=ys[:, :], in0=bL[:, 0:AGENTS], scalar=col[:, B_F2B1:B_F2B1 + 1],
                                             in1=yr[:, :], op0=ALU.add, op1=ALU.mult).then_inc(l0_ys.sem, 1)
                if s == 13:
                    if not first(i):
                        dve.wait_ge(at_lt.sem, at_lt.before(i))
                    dve.wait_ge(at_rs.sem, at_rs.nth(i))
                    for t in range(TILES):
                        dve.tensor_scalar(ln1[:, t, :], bL[:, t * P:(t + 1) * P], lmv[:, t, 0:1], lrs[:, t:t + 1],
                                          ALU.subtract, ALU.mult).then_inc(at_ln.sem, 1)
                    if not first(i):
                        dve.wait_ge(at_tb.sem, at_tb.before(i))
                    dve.wait_ge(at_ln.sem, at_ln.nth(i, 2))
                    dve.tensor_tensor(xl[:, :, :], tiles(bL[:, 0:TOK]), ln1[:, :, :], ALU.add).then_inc(at_xl.sem, 1)

            def at_first(s, i):
                for h in heads_in(S_SLOT, s - 1):
                    b = h % 2
                    if h >= 2:
                        dve.wait_ge(at_p.sem, at_p.nth(i, h - 1))
                    elif not first(i):
                        dve.wait_ge(at_p.sem, at_p.before(i))
                    dve.wait_ge(at_e.sem, at_e.nth(i, 2 * h + 2))
                    dve.reciprocal(rinv[:, b, :], rsum[:, b, :]).then_inc(at_r.sem, 1)
                if s == 0:
                    if first(i):
                        dve.wait_ge(su_zero, 3)
                    else:
                        dve.wait_ge(at_pv.sem, at_pv.before(i))
                    dve.wait_ge(at_v.sem, at_v.nth(i))
                    for t in range(TILES):
                        v = dve.tensor_tensor(vz[:, t, :].rearrange("p (h n) -> p h n", n=VSTEP)[:, :, 0:DK],
                                              bT[:, t * P:(t + 1) * P].rearrange("p (h d) -> p h d", d=DK),
                                              row[:, R_BAV, :].rearrange("p (h d) -> p h d", d=DK), ALU.add)
                    v.then_inc(at_vz.sem, 1)

            def at_late(s, i):
                if s == 12:
                    if not first(i):
                        dve.wait_ge(at_nt.sem, at_nt.before(i))
                    dve.wait_ge(at_nrs.sem, at_nrs.nth(i))
                    for t in range(TILES):
                        dve.tensor_scalar(ln2[:, t, :], t2[:, t, :], nmv[:, t, 0:1], nrs[:, t:t + 1],
                                          ALU.subtract, ALU.mult).then_inc(at_n2.sem, 1)

            def l0_part(s, i):
                if s == 0:
                    dve.wait_ge(l0_s1.sem, l0_s1.nth(i))
                    dve.tensor_tensor(s1[:, :, :], tiles(bL[:, 0:TOK]), c1.unsqueeze(1).broadcast_to([P, TILES, P]),
                                      ALU.add).then_inc(l0_s1b.sem, 1)
                    dve.wait_ge(l0_s1b.sem, l0_s1b.nth(i))
                    grouped = s1[:, :, :].rearrange("p t (h m) -> p (t h) m", m=AGENTS)
                    dve.tensor_reduce(s1m[:, :], grouped, AX.X, ALU.max).then_inc(l0_m1.sem, 1)
                    dve.wait_ge(l0_m1.sem, l0_m1.nth(i))
                    dve.tensor_tensor(s1c[:, :, :].rearrange("p t (h m) -> p (t h) m", m=AGENTS), grouped,
                                      s1m[:, :].unsqueeze(2).broadcast_to([P, TILES * HEADS, AGENTS]),
                                      ALU.subtract).then_inc(l0_s1c.sem, 1)
                if s == 3:
                    dve.wait_ge(l0_z.sem, l0_z.nth(i))
                    dve.tensor_scalar(zc[:, :], bL[:, 0:TOK], zb[:, 0:1], -LOW, ALU.add, ALU.max)\
                       .then_inc(l0_zc.sem, 1)
                if s == 5:
                    if not first(i):
                        dve.wait_ge(l0_v.sem, l0_v.before(i))
                    dve.wait_ge(l0_o.sem, l0_o.nth(i))
                    dve.scalar_tensor_tensor(out=oT[:, :], in0=bL[:, 0:TOK], scalar=col[:, B_F1B2:B_F1B2 + 1],
                                             in1=xg[:, :], op0=ALU.add, op1=ALU.add).then_inc(l0_ot.sem, 1)
                if s == 6:
                    dve.wait_ge(l0_s2.sem, l0_s2.nth(i))
                    dve.tensor_reduce(s2m[:, :], bL[:, 0:TOK], AX.X, ALU.max, negate=True).then_inc(l0_m2.sem, 1)
                if s == 7:
                    if not first(i):
                        dve.wait_ge(l0_f.sem, l0_f.before(i))
                    dve.wait_ge(l0_v.sem, l0_v.nth(i))
                    dve.tensor_tensor(vx[:, :, :], tiles(bL[:, 0:TOK]),
                                      row[:, R_BV, :].unsqueeze(1).broadcast_to([P, TILES, P]), ALU.add)\
                       .then_inc(l0_vx.sem, 1)
                if s == 9:
                    dve.wait_ge(l0_f.sem, l0_f.nth(i))
                    dve.tensor_tensor(fm[:, :, :], bL[:, 0:P].rearrange("p (h m) -> p h m", m=AGENTS),
                                      bd.unsqueeze(2).broadcast_to([P, HEADS, AGENTS]), ALU.mult).then_inc(l0_fm.sem, 1)
                    if not first(i):
                        dve.wait_ge(l0_y.sem, l0_y.before(i))
                    dve.wait_ge(l0_fm.sem, l0_fm.nth(i))
                    dve.tensor_reduce(fin[:, :], fm[:, :, :].rearrange("p h m -> p m h"), AX.X, ALU.add)\
                       .then_inc(l0_fin.sem, 1)
                if s == 10:
                    dve.wait_ge(l0_y.sem, l0_y.nth(i))
                    dve.tensor_scalar(yc[:, :], bL[:, 0:AGENTS], col[:, B_F2B1:B_F2B1 + 1], -LOW, ALU.add, ALU.max)\
                       .then_inc(l0_yc.sem, 1)
                if s == 11:
                    dve.wait_ge(l0_w.sem, l0_w.nth(i))
                    dve.tensor_scalar(fe[:, :, :], bL[:, 0:AGENTS].unsqueeze(2).broadcast_to([P, AGENTS, CELL]),
                                      col[:, B_F2B2:B_F2B2 + 1], None, ALU.add).then_inc(l0_fe.sem, 1)
                    if not first(i):
                        dve.wait_ge(at_xt.sem, at_xt.before(i))
                    dve.wait_ge(l0_base.sem, l0_base.nth(i))
                    dve.wait_ge(l0_fe.sem, l0_fe.nth(i))
                    dve.tensor_tensor(x1T[:, :].rearrange("p (a y x) -> p a y x", a=CELL, y=CELL),
                                      base[:, :].rearrange("p (a y x) -> p a y x", a=CELL, y=CELL),
                                      fe[:, :, :].rearrange("p (a b) x -> p a (b x)", a=CELL).unsqueeze(2)
                                      .broadcast_to([P, CELL, CELL, SIDE]), ALU.add).then_inc(l0_x1.sem, 1)
                if s == 12:
                    dve.wait_ge(at_xt.sem, at_xt.nth(i))
                    for t in range(TILES):
                        dve.bn_stats(lst[:, t, :], bL[:, t * P:(t + 1) * P]).then_inc(at_st.sem, 1)
                    dve.wait_ge(at_st.sem, at_st.nth(i, 2))
                    dve.sem_inc(gate[0], 1)
                    for t in range(TILES):
                        dve.bn_aggr(lmv[:, t, :], lst[:, t, :]).then_inc(at_mv.sem, 1)
                    dve.wait_ge(at_mv.sem, at_mv.nth(i, 2))
                    dve.tensor_scalar(lve[:, :], lmv[:, :, 1], 1e-5, None, ALU.add).then_inc(at_mv.sem, 1)
                if s == 15:
                    if not first(i):
                        dve.wait_ge(at_s.sem, at_s.before(i))
                        dve.wait_ge(at_kzp.sem, at_kzp.before(i))
                    dve.wait_ge(at_qk.sem, at_qk.nth(i))
                    dve.tensor_scalar(kT[:, :], bL[:, TOK:2 * TOK], col[:, B_AK:B_AK + 1], None, ALU.add)
                    dve.tensor_scalar(qT[:, :], bL[:, 0:TOK], col[:, B_AQ:B_AQ + 1], SCALE, ALU.add, ALU.mult)\
                       .then_inc(at_k.sem, 1)
                    dve.wait_ge(at_k.sem, at_k.nth(i))
                    for h in range(KZ_DVE):
                        dve.tensor_scalar(kz[:, h, :], kT[:, :], bd[:, h:h + 1], None, ALU.mult).then_inc(at_kz.sem, 1)

            def at_part(s, i):
                for h in heads_in(S_SLOT, s):
                    b = h % 2
                    dve.wait_ge(at_s.sem, at_s.nth(i, h + 1))
                    dve.tensor_reduce(nm[:, b, 0:1], bS[b][:, 0:P], AX.X, ALU.max, negate=True)
                    dve.tensor_reduce(nm[:, b, 1:2], bS[b][:, P:3 * P], AX.X, ALU.max, negate=True)\
                       .then_inc(at_m.sem, 1)
                if s == 11:
                    dve.wait_ge(at_tb.sem, at_tb.nth(i))
                    dve.wait_ge(at_w.sem, at_w.nth(i))
                    dve.tensor_tensor(t2[:, :, :], tiles(bA[:, 0:TOK]), tb[:, :, :], ALU.add).then_inc(at_t2.sem, 1)
                    dve.wait_ge(at_t2.sem, at_t2.nth(i))
                    for t in range(TILES):
                        dve.bn_stats(nst[:, t, :], t2[:, t, :]).then_inc(at_nst.sem, 1)
                    dve.wait_ge(at_nst.sem, at_nst.nth(i, 2))
                    dve.sem_inc(gate[0], 1)
                    for t in range(TILES):
                        dve.bn_aggr(nmv[:, t, :], nst[:, t, :]).then_inc(at_nmv.sem, 1)
                    dve.wait_ge(at_nmv.sem, at_nmv.nth(i, 2))
                    dve.tensor_scalar(nve[:, :], nmv[:, :, 1], 1e-5, None, ALU.add).then_inc(at_nmv.sem, 1)
                if s == 14:
                    dve.wait_ge(at_l.sem, at_l.nth(i))
                    dve.tensor_copy(lg[:, :, :].rearrange("p t e -> p (t e)"), bA[:, 0:TILES * EXPERTS])\
                       .then_inc(at_lg.sem, 1)
                    dve.wait_ge(at_lg.sem, at_lg.nth(i))
                    dve.sem_inc(gate[0], 1)
                    for t in range(TILES):
                        dve.max(top[:, t, :], lg[:, t, :]).then_inc(at_top.sem, 1)
                    dve.wait_ge(at_top.sem, at_top.nth(i, 2))
                    dve.tensor_tensor(td[:, :], top[:, :, 1], top[:, :, 0], ALU.subtract).then_inc(at_td.sem, 1)
                    for t in range(TILES):
                        dve.max_index(tix[:, t, :], top[:, t, :], lg[:, t, :]).then_inc(at_tix.sem, 1)
                    dve.wait_ge(at_tix.sem, at_tix.nth(i, 2))
                    dve.tensor_copy(tif[:, :, :], tix[:, :, 0:2]).then_inc(at_tif.sem, 1)
                    dve.wait_ge(at_tif.sem, at_tif.nth(i))
                    for k in range(2):
                        dve.tensor_tensor(pick[:, k, :, :], iota.unsqueeze(1).broadcast_to([P, TILES, EXPERTS]),
                                          tif[:, :, k:k + 1].broadcast_to([P, TILES, EXPERTS]), ALU.is_equal)\
                           .then_inc(at_pick.sem, 1)

            def mo_part(s, i):
                if s == 0:
                    dve.wait_ge(at_te.sem, at_te.nth(i))
                    dve.tensor_scalar(ta[:, :], te[:, :], 1.0, None, ALU.add).then_inc(at_ta.sem, 1)
                    dve.wait_ge(at_ta.sem, at_ta.nth(i))
                    dve.reciprocal(tw[:, :, 0], ta[:, :]).then_inc(at_tw.sem, 1)
                    dve.wait_ge(at_tw.sem, at_tw.nth(i, 1))
                    dve.tensor_tensor(tw[:, :, 1], te[:, :], tw[:, :, 0], ALU.mult).then_inc(at_tw.sem, 1)
                    dve.wait_ge(at_tw.sem, at_tw.nth(i, 2))
                    for k in range(2):
                        dve.tensor_tensor(part[:, k, :, :], pick[:, k, :, :],
                                          tw[:, :, k:k + 1].broadcast_to([P, TILES, EXPERTS]), ALU.mult)\
                           .then_inc(at_share.sem, 1)
                    if first(i):
                        dve.wait_ge(su_zero, 2)
                    else:
                        dve.wait_ge(mo_ct.sem, mo_ct.before(i))
                    dve.wait_ge(at_share.sem, at_share.nth(i, 2))
                    dve.tensor_tensor(comb[:, :, 0:EXPERTS], part[:, 0, :, :], part[:, 1, :, :], ALU.add)\
                       .then_inc(at_comb.sem, 1)
                for e in heads_in(G2_SLOT, s):
                    dve.wait_ge(mo_y.sem, mo_y.nth(i, e + 1))
                    if e == 0:
                        dve.wait_ge(at_t2.sem, at_t2.nth(i))
                        dve.wait_ge(at_comb.sem, at_comb.nth(i))
                        dve.tensor_tensor(acc[:, :, :], tiles(bY[:, TOK:2 * TOK]), t2[:, :, :], ALU.add)\
                           .then_inc(mo_acc.sem, 1)
                    total, done = (acc, mo_acc) if e < EXPERTS - 1 else (ob, mo_ob)
                    if e == EXPERTS - 1 and not first(i):
                        dve.wait_ge(mo_out.sem, mo_out.before(i))
                    dve.wait_ge(mo_acc.sem, mo_acc.nth(i, 1 + TILES * e))
                    for t in range(TILES):
                        dve.scalar_tensor_tensor(out=total[:, t, :], in0=y_bank(e)[:, t * P:(t + 1) * P],
                                                 scalar=comb[:, t, e:e + 1], in1=acc[:, t, :],
                                                 op0=ALU.mult, op1=ALU.add).then_inc(done.sem, 1)

            def step(l0, at, mo):
                for s in range(SLOTS):
                    if l0 is not None and s in (TAIL, 0):
                        l0_late(s, l0)
                    if l0 is not None and s == 15:
                        l0_part(s, l0)
                    if at is not None:
                        at_first(s, at)
                    if mo is not None and s >= TAIL:
                        mo_part(s, mo)
                    if l0 is not None and s in (TAIL, 12):
                        l0_part(s, l0)
                    if l0 is not None and s not in (TAIL, 0):
                        l0_late(s, l0)
                    if at is not None:
                        at_late(s, at)
                        at_part(s, at)
                    if mo is not None and s == 0:
                        mo_part(s, mo)
                    if l0 is not None and s not in (TAIL, 12, 15):
                        l0_part(s, l0)
                    if mo is not None and 0 < s < TAIL:
                        mo_part(s, mo)
                    if first(at) and s < EXPERTS:
                        split_w1(s)

            pipeline(dve, step)


def kernel(**inputs):
    import numpy as np
    import concourse.bacc as bacc
    from concourse.bass_utils import run_bass_kernel_spmd

    L0 = {k[len("L0_conv_"):]: np.asarray(v) for k, v in inputs.items() if k.startswith("L0_conv_")}
    A = {k[len("L1_attn_"):]: np.asarray(v) for k, v in inputs.items() if k.startswith("L1_attn_")}
    M = {k[len("L1_ffn_"):]: np.asarray(v) for k, v in inputs.items() if k.startswith("L1_ffn_")}

    p = np.arange(P)
    consts = np.zeros((P, C_N), np.float32)
    consts[:, C_ID:C_ID + P] = np.eye(P)
    consts[:, C_GRP:C_GRP + P] = (p[:, None] // GROUP == p[None, :] // GROUP) * (1.0 / GROUP)
    consts[:, C_CAUSAL:C_CAUSAL + P] = np.where(p[None, :] > p[:, None], -1e9, 0.0)
    own = p[:, None] // DK == np.arange(HEADS)[None, :]
    consts[:, C_BD:C_BD + HEADS] = own
    consts[:, C_BDS:C_BDS + HEADS] = own * SCALE
    consts[:, C_IOTA:C_IOTA + EXPERTS] = np.arange(EXPERTS)
    consts[:, C_POW:C_POW + 2] = -0.5

    by_kind = A["W_in"].reshape(C, HEADS, 3, DK).transpose(2, 0, 1, 3).reshape(3, C, C)
    bias_by_kind = A["b_in"].reshape(HEADS, 3, DK).transpose(1, 0, 2).reshape(3, C)
    weights = np.stack([
        L0["w_kvy"][:, :C], L0["w_kvy"][:, C:], L0["w_q"], L0["w_q2"].T, L0["f1w1"], L0["w_kvx"][:, :C].T,
        L0["f1w2"], L0["w_kvx"][:, C:], L0["f2w1"], L0["f2w2"], by_kind[0], by_kind[1], by_kind[2], A["W_out"]],
        axis=1)
    cols = np.stack([
        L0["b_kvy"][:C], L0["b_kvy"][C:], L0["b_q"], L0["pe1"].reshape(P), L0["pe2"].reshape(P), L0["f1b1"],
        L0["f1b2"], L0["f2b1"], L0["f2b2"], bias_by_kind[0], bias_by_kind[1], L0["b_q2"]], axis=1)
    rows = np.concatenate([L0["b_kvx"][C:], bias_by_kind[2], A["b_out"]])
    agents = np.stack([L0["learnable_kv"][0].T, L0["learnable_q"][0].T], axis=1)
    arrays = {
        "xT": np.asarray(inputs["x"]).reshape(IMAGES * TOK, C).T, "consts": consts, "weights": weights,
        "cols": cols, "rows": rows, "agents": agents, "w_router": M["W_router"], "w1": M["W1"],
        "b1": M["b1"].reshape(EXPERTS, HB, P).transpose(2, 0, 1), "w2": M["W2"], "b2": M["b2"]}

    nc = bacc.Bacc("TRN2", target_bir_lowering=False, num_devices=1)
    args = {}
    for name in arrays:
        a = arrays[name] = np.ascontiguousarray(arrays[name])
        args[name] = nc.dram_tensor(name, a.shape, mybir.dt.from_np(a.dtype), kind="ExternalInput").ap()
    out = nc.dram_tensor("out", (IMAGES * TILES, P, C), F32, kind="ExternalOutput").ap()
    hybrid_block(nc, out=out, **args)
    r = run_bass_kernel_spmd(nc, [arrays], core_ids=[0])
    return r.results[0]["out"].reshape(IMAGES, SIDE, SIDE, C)
```

```python
from contextlib import ExitStack

import concourse.bass as bass
from concourse import mybir

F32 = mybir.dt.float32
F32R = mybir.dt.float32r
BF16 = mybir.dt.bfloat16
U32 = mybir.dt.uint32
ALU = mybir.AluOpType
ACT = mybir.ActivationFunctionType
AX = mybir.AxisListType

P = 128
IMAGES = 8
SIDE = 16
TOK = SIDE * SIDE
TILES = TOK // P
C = 128
HEADS = 8
DK = C // HEADS
AGENTS = 16
CELL = 4
EXPERTS = 8
HID = 512
HB = HID // P
GROUP = 4
SCALE = DK ** -0.5
SLOTS = 17
TAIL = 11
KZ = 2
STACKED = 3
QHI, QLO, KHI, KLO = range(4)
RES_AT = 3
WARM_L0 = 12
WARM_AT = 6
LOW = 80.0

C_ID = 0
C_GRP = C_ID + P
C_CAUSAL = C_GRP + P
C_BD = C_CAUSAL + P
C_BDS = C_BD + HEADS
C_IOTA = C_BDS + HEADS
C_POW = C_IOTA + EXPERTS
C_N = C_POW + 2

W_KVYK, W_KVYV, W_Q, W_Q2T, W_F1W1, W_KT, W_F1W2, W_V, W_F2W1, W_F2W2, W_AQ, W_AK, W_AV, W_AO = range(14)
W_N = 14
W_SETUP = 6
(B_KYK, B_KYV, B_Q, B_PE1, B_PE2, B_F1B1, B_F1B2, B_F2B1, B_F2B2, B_AQ, B_AK, B_Q2) = range(12)
B_N = 12
R_BV, R_BAV, R_BO = range(3)
R_N = 3


class Signal:

    def __init__(self, ctx, nc, name, per=1):
        self.sem = ctx.enter_context(nc.semaphore(name))
        self.per = per

    def nth(self, i, k=1):
        return i * self.per + k

    def before(self, i):
        return i * self.per


def first(i):
    return isinstance(i, int) and i == 0


def hybrid_block(nc, xT, consts, weights, cols, rows, agents, w_router, w1, b1, w2, b2, out):
    ctx = ExitStack()
    with ctx:
        def sb(name, shape, dt=F32):
            return ctx.enter_context(nc.sbuf_tensor(name, shape, dt))

        def sig(name, per=1):
            return Signal(ctx, nc, name, per)

        x_all = sb("x_all", [P, IMAGES * TOK])
        cst = sb("cst", [P, C_N])
        W = sb("W", [P, W_N, P])
        col = sb("col", [P, B_N])
        row = sb("row", [P, R_N, P])
        agt = sb("agt", [P, 2, AGENTS])
        wr = sb("wr", [P, EXPERTS])
        w1raw = sb("w1raw", [P, EXPERTS, HID])
        w1hi = sb("w1hi", [P, EXPERTS, HID], F32R)
        w1lo = sb("w1lo", [P, EXPERTS, HID], F32R)
        w2s = sb("w2s", [P, EXPERTS, HB, C])
        b1s = sb("b1s", [P, EXPERTS, HB])
        b2r = sb("b2r", [P, EXPERTS, C])
        ident = cst[:, C_ID:C_ID + P]
        grp = cst[:, C_GRP:C_GRP + P]
        bd = cst[:, C_BD:C_BD + HEADS]
        bds = cst[:, C_BDS:C_BDS + HEADS]
        iota = cst[:, C_IOTA:C_IOTA + EXPERTS]
        power = cst[:, C_POW:C_POW + 2]
        identb = sb("identb", [P, P], BF16)
        causalb = sb("causalb", [P, P], BF16)

        gst = sb("gst", [P, IMAGES, 6])
        gmv = sb("gmv", [P, IMAGES, 2])
        gmean = sb("gmean", [P, IMAGES])
        gdev = sb("gdev", [P, IMAGES])
        gvar = sb("gvar", [P, IMAGES])
        gn = sb("gn", [P, IMAGES, 2])
        kvq = sb("kvq", [P, 3, AGENTS])
        kvqd = sb("kvqd", [P, 3, HEADS, AGENTS])
        bq2b = sb("bq2b", [P, P])
        fold = sb("fold", [P, 4, P])
        m1, c1, m2, mkq = (fold[:, n, :] for n in range(4))
        zb = sb("zb", [P, 1])

        gni = sb("gni", [P, 2])
        xg = sb("xg", [P, TOK])
        xx = sb("xx", [P, TOK])
        s1 = sb("s1", [P, TILES, P])
        s1m = sb("s1m", [P, TILES * HEADS])
        s1c = sb("s1c", [P, TILES, P])
        e1 = sb("e1", [P, TILES, P])
        e1s = sb("e1s", [P, TILES * HEADS])
        e1r = sb("e1r", [P, TILES * HEADS])
        p1 = sb("p1", [P, TILES, P])
        p1T = sb("p1T", [P, TOK])
        ez = sb("ez", [P, TOK])
        za = sb("za", [P, TOK])
        zr = sb("zr", [P, TOK])
        zc = sb("zc", [P, TOK])
        yc = sb("yc", [P, AGENTS])
        zs = sb("zs", [P, TOK])
        oT = sb("oT", [P, TOK])
        base = sb("base", [P, TOK])
        s2m = sb("s2m", [P, 1])
        s2s = sb("s2s", [P, 1])
        s2r = sb("s2r", [P, 1])
        e2 = sb("e2", [P, TOK])
        p2 = sb("p2", [P, TOK])
        p2T = sb("p2T", [P, TILES, P])
        vx = sb("vx", [P, TILES, P])
        fm = sb("fm", [P, HEADS, AGENTS])
        fin = sb("fin", [P, AGENTS])
        ey = sb("ey", [P, AGENTS])
        ya = sb("ya", [P, AGENTS])
        yr = sb("yr", [P, AGENTS])
        ys = sb("ys", [P, AGENTS])
        fe = sb("fe", [P, AGENTS, CELL])
        x1T = sb("x1T", [P, TOK])

        lst = sb("lst", [P, TILES, 6])
        lmv = sb("lmv", [P, TILES, 2])
        lrs = sb("lrs", [P, TILES])
        lve = sb("lve", [P, TILES])
        ln1 = sb("ln1", [P, TILES, P])
        xl = sb("xl", [P, TILES, P])
        tb = sb("tb", [P, TILES, P])
        ln1T = sb("ln1T", [P, TOK])
        qT = sb("qT", [P, TOK])
        kT = sb("kT", [P, TOK])
        kz = sb("kz", [P, KZ, TOK])
        split = sb("split", [P, 4, TOK], F32R)
        stack = sb("stack", [P, HEADS - KZ, 2, TOK], F32R)
        v = sb("v", [P, TILES, P])
        nm = sb("nm", [P, 2, 2])
        rsum = sb("rsum", [P, TILES, HEADS])
        rinv = sb("rinv", [P, TILES, HEADS])
        pe_ = sb("pe_", [P, 2, 3 * P])
        pT = sb("pT", [P, 2, 3 * P])
        ao = sb("ao", [P, TILES, P])
        aT = sb("aT", [P, TOK])
        t2 = sb("t2", [P, TILES, P])
        nst = sb("nst", [P, TILES, 6])
        nmv = sb("nmv", [P, TILES, 2])
        nve = sb("nve", [P, TILES])
        nrs = sb("nrs", [P, TILES])
        ln2 = sb("ln2", [P, TILES, P])
        ln2T = sb("ln2T", [P, TOK])
        xhi = sb("xhi", [P, TOK], F32R)
        xlo = sb("xlo", [P, TOK], F32R)
        lg = sb("lg", [P, TILES, EXPERTS])
        top = sb("top", [P, TILES, 8])
        tix = sb("tix", [P, TILES, 8], U32)
        tif = sb("tif", [P, TILES, 2])
        td = sb("td", [P, TILES])
        te = sb("te", [P, TILES])
        ta = sb("ta", [P, TILES])
        tw = sb("tw", [P, TILES, 2])
        pick = sb("pick", [P, 2, TILES, EXPERTS])
        part = sb("part", [P, 2, TILES, EXPERTS])
        comb = sb("comb", [P, TILES, EXPERTS])

        hf = sb("hf", [P, 2, HB, TOK])
        bw = sb("bw", [P, TILES, P])
        res = sb("res", [P, TILES, P])
        acc = sb("acc", [P, TILES, P])
        ob = sb("ob", [P, TILES, P])

        bH = [ctx.enter_context(nc.psum_tensor(f"bH{n}", [P, 2 * TOK], F32)) for n in range(2)]
        bY = ctx.enter_context(nc.psum_tensor("bY", [P, 2 * TOK], F32))
        bA = ctx.enter_context(nc.psum_tensor("bA", [P, 2 * TOK], F32))
        bS = [ctx.enter_context(nc.psum_tensor(f"bS{n}", [P, 2 * TOK], F32)) for n in range(2)]
        bT = ctx.enter_context(nc.psum_tensor("bT", [P, 2 * TOK], F32))
        bL = ctx.enter_context(nc.psum_tensor("bL", [P, 2 * TOK], F32))

        def tiles(ap):
            return ap.rearrange("p (t n) -> p t n", n=P)

        sem = lambda name: ctx.enter_context(nc.semaphore(name))
        ld_c, ld_s, ld_w, ld_1, ld_2, ld_b = (sem(n) for n in ("ld_c", "ld_s", "ld_w", "ld_1", "ld_2", "ld_b"))
        ld_x = [sem(f"ld_x{n}") for n in range(2)]
        su_zero, su_cast, su_dve, su_pe, su_act, su_pow, su_w1h, su_w1 = (
            sem(n) for n in ("su_zero", "su_cast", "su_dve", "su_pe", "su_act", "su_pow", "su_w1h", "su_w1"))
        gate = [sem(f"gate{n}") for n in range(2)]

        l0_gn, l0_xg, l0_xx = sig("l0_gn"), sig("l0_xg"), sig("l0_xx")
        l0_s1, l0_s1b, l0_m1, l0_s1c, l0_e1 = sig("l0_s1"), sig("l0_s1b"), sig("l0_m1"), sig("l0_s1c"), sig("l0_e1")
        l0_sum, l0_r1, l0_p1, l0_pt, l0_ptc = sig("l0_sum"), sig("l0_r1"), sig("l0_p1"), sig("l0_pt"), sig("l0_ptc")
        l0_zc, l0_yc = sig("l0_zc"), sig("l0_yc")
        l0_z, l0_ez, l0_za, l0_zr, l0_zs = sig("l0_z"), sig("l0_ez"), sig("l0_za"), sig("l0_zr"), sig("l0_zs")
        l0_o, l0_ot, l0_base = sig("l0_o"), sig("l0_ot"), sig("l0_base")
        l0_s2, l0_m2, l0_e2, l0_r2, l0_p2 = sig("l0_s2"), sig("l0_m2"), sig("l0_e2"), sig("l0_r2"), sig("l0_p2")
        l0_v, l0_vx, l0_qt, l0_qtc = sig("l0_v"), sig("l0_vx"), sig("l0_qt"), sig("l0_qtc")
        l0_f, l0_fm, l0_fin = sig("l0_f"), sig("l0_fm"), sig("l0_fin")
        l0_y, l0_ey, l0_ya, l0_yr, l0_ys = sig("l0_y"), sig("l0_ey"), sig("l0_ya"), sig("l0_yr"), sig("l0_ys")
        l0_w, l0_fe, l0_x1 = sig("l0_w"), sig("l0_fe"), sig("l0_x1")

        at_xt, at_st, at_mv, at_rs = sig("at_xt"), sig("at_st", 2), sig("at_mv", 3), sig("at_rs")
        at_ln, at_xl, at_tb = sig("at_ln", 2), sig("at_xl"), sig("at_tb")
        at_lt, at_ltc = sig("at_lt"), sig("at_ltc")
        at_qk, at_v, at_k, at_vb, at_kz = sig("at_qk"), sig("at_v"), sig("at_k", 2), sig("at_vb"), sig("at_kz", KZ)
        at_hi, at_lo = sig("at_hi", 2), sig("at_lo", 2)
        at_stack = [sig(f"at_stack{h}", 16 * STACKED) for h in range(HEADS - KZ)]
        at_s, at_m, at_e, at_r = sig("at_s", HEADS), sig("at_m", HEADS), sig("at_e", 2 * HEADS), sig("at_r")
        at_t, at_tc, at_pv = sig("at_t", HEADS), sig("at_tc", HEADS), sig("at_pv", HEADS)
        at_on, at_ot, at_o, at_w, at_t2 = sig("at_on"), sig("at_ot"), sig("at_o"), sig("at_w"), sig("at_t2")
        at_nst, at_nmv, at_nrs, at_n2 = sig("at_nst", 2), sig("at_nmv", 3), sig("at_nrs"), sig("at_n2", 2)
        at_nt, at_ntc, at_xs, at_xl2 = sig("at_nt"), sig("at_ntc"), sig("at_xs"), sig("at_xl2")
        at_l, at_lg, at_top, at_tix, at_tif = sig("at_l"), sig("at_lg"), sig("at_top", 2), sig("at_tix", 2), sig("at_tif")
        at_td, at_te, at_ta, at_tw, at_pick, at_share = sig("at_td"), sig("at_te"), sig("at_ta"), sig("at_tw", 2), sig("at_pick", 2), sig("at_share", 2)
        at_comb = sig("at_comb")

        mo_h, mo_r, mo_y = sig("mo_h", 2 * EXPERTS), sig("mo_r", HB * EXPERTS), sig("mo_y", EXPERTS)
        mo_bw, mo_res, mo_acc = sig("mo_bw", EXPERTS), sig("mo_res", EXPERTS), sig("mo_acc", TILES * (EXPERTS - 1) + 1)
        mo_ob, mo_out = sig("mo_ob", TILES), sig("mo_out", 16)

        block = ctx.enter_context(nc.Block())

        S_SLOT = {h: h for h in range(HEADS)}
        T_SLOT = {h: S_SLOT[h] + 2 for h in range(HEADS)}
        V_SLOT = {h: S_SLOT[h] + 3 for h in range(HEADS)}

        G1_SLOT = dict(enumerate((0, 1, 4, 6, 8, 10, 12, 13)))
        G2_SLOT = dict(enumerate((2, 5, 7, 9, 11, 13, 14, 15)))

        MIDWAY = {0: (1, 2), 6: (1, 1)}

        def y_bank(e):
            return bS[1] if e in (5, 7) else bY

        def summed(e):
            return TILES * (e + 1) + (e >= RES_AT)

        def due(plan, s):
            return [h for h in range(HEADS) if plan[h] == s]

        def pipeline(eng, step, before_experts=lambda: None):
            step(0, None, None)
            step(1, 0, None)
            before_experts()
            step(2, 1, 0)
            with eng.Fori(1, IMAGES - 2) as i:
                step(i + 2, i + 1, i)
            step(None, IMAGES - 1, IMAGES - 2)
            step(None, None, IMAGES - 1)

        @block.sync
        def _(sp):
            half = IMAGES // 2 * TOK
            sp.dma_start(x_all[:, 0:half], xT[:, 0:half]).then_inc(ld_x[0], 16)
            sp.dma_start(x_all[:, half:], xT[:, half:]).then_inc(ld_x[1], 16)
            sp.dma_start(cst[:, :], consts).then_inc(ld_c, 16)
            sp.dma_start(W[:, 0:W_SETUP, :], weights[:, 0:W_SETUP, :]).then_inc(ld_s, 16)
            sp.dma_start(W[:, W_SETUP:, :], weights[:, W_SETUP:, :]).then_inc(ld_w, 16)
            for e in range(EXPERTS):
                sp.dma_start(w1raw[:, e, :], w1[e]).then_inc(ld_1, 16)
                sp.dma_start(w2s[:, e, :, :], w2[e].rearrange("(k p) c -> p k c", p=P)).then_inc(ld_2, 16)

            def stack_heads(i):
                def send(h, n):
                    q, k = ((QHI, KHI), (QLO, KHI), (QHI, KLO))[n]
                    sp.dma_start(stack[n * DK:(n + 1) * DK, h - KZ, :, :].bitcast(F32),
                                 split[h * DK:(h + 1) * DK, q:k + 1:k - q, :].bitcast(F32))\
                      .then_inc(at_stack[h - KZ].sem, 16)

                sp.wait_ge(at_hi.sem, at_hi.nth(i, 2))
                sp.sem_inc(gate[1], 1)
                if first(i):
                    sp.wait_ge(su_zero, 1)
                else:
                    sp.wait_ge(at_s.sem, at_s.before(i))
                    sp.sem_inc(gate[1], 1)
                for h in (KZ, KZ + 1):
                    send(h, 0)
                sp.wait_ge(at_lo.sem, at_lo.nth(i, 2))
                sp.sem_inc(gate[1], 1)
                for h in range(KZ, HEADS):
                    for n in range(STACKED):
                        if n > 0 or h > KZ + 1:
                            send(h, n)

            def step(l0, at, mo):
                if l0 is not None:
                    stack_heads(l0)
                if mo is None:
                    return
                sp.sem_inc(gate[1], 1)
                sp.wait_ge(mo_ob.sem, mo_ob.nth(mo, TILES))
                sp.dma_start(out[bass.ds(mo * TILES, TILES), :, :].rearrange("t p c -> p t c"), ob[:, :, :])\
                  .then_inc(mo_out.sem, 16)

            pipeline(sp, step)
            sp.wait_ge(mo_out.sem, mo_out.per * IMAGES)

        @block.gpsimd
        def _(pool):
            pool.memset(stack[:, :, :, :].bitcast(F32), 0.0).then_inc(su_zero, 1)
            pool.wait_ge(ld_c, 64)
            pool.wait_ge(su_dve, 7)
            pool.tensor_tensor(gn[:, :, 0], gvar[:, :], power[:, 0:1].broadcast_to([P, IMAGES]), ALU.pow)\
                .then_inc(su_pow, 1)

            def l0_part(s, i):
                if s == 6:
                    pool.wait_ge(l0_ot.sem, l0_ot.nth(i))
                    pool.wait_ge(l0_xx.sem, l0_xx.nth(i))
                    if not first(i):
                        pool.wait_ge(l0_x1.sem, l0_x1.before(i))
                    pool.tensor_tensor(base[:, :], xx[:, :], oT[:, :], ALU.add).then_inc(l0_base.sem, 1)
                if s == 12:
                    pool.wait_ge(at_mv.sem, at_mv.nth(i, 3))
                    pool.tensor_tensor(lrs[:, :], lve[:, :], power[:, 0:1].broadcast_to([P, TILES]), ALU.pow)\
                        .then_inc(at_rs.sem, 1)
                if s == 13:
                    pool.wait_ge(at_xl.sem, at_xl.nth(i))
                    if not first(i):
                        pool.wait_ge(at_t2.sem, at_t2.before(i))
                    pool.tensor_tensor(tb[:, :, :], xl[:, :, :],
                                       row[:, R_BO, :].unsqueeze(1).broadcast_to([P, TILES, P]), ALU.add)\
                        .then_inc(at_tb.sem, 1)
                if s == 16:
                    if not first(i):
                        for stacked in at_stack:
                            pool.wait_ge(stacked.sem, stacked.before(i))
                    for n, (whole, hi, lo) in enumerate(((qT, QHI, QLO), (kT, KHI, KLO))):
                        pool.wait_ge(at_k.sem, at_k.nth(i, n + 1))
                        pool.wait_ge(at_hi.sem, at_hi.nth(i, n + 1))
                        pool.tensor_tensor(split[:, lo, :], whole[:, :], split[:, hi, :].bitcast(F32), ALU.subtract)\
                            .then_inc(at_lo.sem, 1)

            def at_part(s, i):
                if s == 11:
                    pool.wait_ge(at_nmv.sem, at_nmv.nth(i, 3))
                    pool.tensor_tensor(nrs[:, :], nve[:, :], power[:, 0:1].broadcast_to([P, TILES]), ALU.pow)\
                        .then_inc(at_nrs.sem, 1)

                if s == 15:
                    if not first(i):
                        pool.wait_ge(mo_h.sem, mo_h.before(i))
                    pool.wait_ge(at_xs.sem, at_xs.nth(i))
                    pool.tensor_tensor(xlo[:, :], ln2T[:, :], xhi[:, :].bitcast(F32), ALU.subtract)\
                        .then_inc(at_xl2.sem, 1)

            def mo_part(s, i):
                if s < EXPERTS:
                    e = s
                    if e == 0:
                        pool.wait_ge(at_comb.sem, at_comb.nth(i))
                        pool.wait_ge(at_t2.sem, at_t2.nth(i))
                        if not first(i):
                            pool.wait_ge(mo_acc.sem, mo_acc.before(i))
                            pool.wait_ge(mo_res.sem, mo_res.before(i))
                    else:
                        pool.wait_ge(mo_res.sem, mo_res.nth(i, e))
                    pool.tensor_tensor(bw[:, :, :], b2r[:, e, :].unsqueeze(1).broadcast_to([P, TILES, P]),
                                       comb[:, :, e:e + 1].broadcast_to([P, TILES, P]), ALU.mult)\
                        .then_inc(mo_bw.sem, 1)
                    pool.wait_ge(mo_bw.sem, mo_bw.nth(i, e + 1))
                    before = res if e >= 1 else t2
                    pool.tensor_tensor(res[:, :, :], before[:, :, :], bw[:, :, :], ALU.add).then_inc(mo_res.sem, 1)

            def step(l0, at, mo):
                for s in range(SLOTS):
                    if at is not None:
                        at_part(s, at)
                    if l0 is not None:
                        l0_part(s, l0)
                    if mo is not None:
                        mo_part(s, mo)
                    if first(l0) and 4 <= s < 4 + EXPERTS:
                        pool.wait_ge(su_w1h, s - 3)
                        pool.wait_ge(ld_1, 16 * EXPERTS)
                        pool.tensor_tensor(w1lo[:, s - 4, :], w1raw[:, s - 4, :], w1hi[:, s - 4, :].bitcast(F32),
                                           ALU.subtract).then_inc(su_w1, 1)

            pipeline(pool, step, lambda: pool.wait_ge(ld_b, 16))

        @block.scalar
        def _(act):
            act.dma_start(col[:, :], cols).then_inc(ld_c, 16)
            act.dma_start(row[:, :, :].rearrange("p a b -> p (a b)"), rows.partition_broadcast(P)).then_inc(ld_c, 16)
            act.dma_start(agt[:, :, :], agents).then_inc(ld_c, 16)
            act.dma_start(wr[:, :], w_router).then_inc(ld_w, 16)
            act.dma_start(b1s[:, :, :], b1).then_inc(ld_w, 16)
            act.dma_start(b2r[:, :, :].rearrange("p e c -> p (e c)"), b2.partition_broadcast(P)).then_inc(ld_b, 16)
            act.wait_ge(su_pe, 4)
            act.activation(fold[:, :, :].rearrange("p a b -> p (a b)"), bS[1][:, :], ACT.Copy).then_inc(su_act, 1)

            def l0_part(s, i):
                if s == 0:
                    act.wait_ge(l0_s1c.sem, l0_s1c.nth(i))
                    if not first(i):
                        act.wait_ge(l0_p1.sem, l0_p1.before(i))
                    act.activation(e1[:, :, :], s1c[:, :, :], ACT.Exp).then_inc(l0_e1.sem, 1)
                if s == 2:
                    act.wait_ge(l0_pt.sem, l0_pt.nth(i))
                    act.activation(p1T[:, :], bL[:, 0:TOK], ACT.Copy).then_inc(l0_ptc.sem, 1)
                if s == 3:
                    act.wait_ge(l0_zc.sem, l0_zc.nth(i))
                    if not first(i):
                        act.wait_ge(l0_za.sem, l0_za.before(i))
                    act.activation(ez[:, :], zc[:, :], ACT.Exp, scale=-1.0)\
                       .then_inc(l0_ez.sem, 1)
                if s == 6:
                    act.wait_ge(l0_m2.sem, l0_m2.nth(i))
                    if not first(i):
                        act.wait_ge(l0_p2.sem, l0_p2.before(i))
                    act.activation(e2[:, :], bL[:, 0:TOK], ACT.Exp, bias=s2m[:, 0:1], accum_out=s2s[:, 0:1])\
                       .then_inc(l0_e2.sem, 1)
                if s == 8:
                    act.wait_ge(l0_qt.sem, l0_qt.nth(i))
                    act.activation(p2T[:, :, :].rearrange("p t n -> p (t n)"), bL[:, 0:TOK], ACT.Copy)\
                       .then_inc(l0_qtc.sem, 1)
                if s == 10:
                    act.wait_ge(l0_yc.sem, l0_yc.nth(i))
                    if not first(i):
                        act.wait_ge(l0_ya.sem, l0_ya.before(i))
                    act.activation(ey[:, :], yc[:, :], ACT.Exp, scale=-1.0)\
                       .then_inc(l0_ey.sem, 1)
                if s == 16:
                    if not first(i):
                        for stacked in at_stack:
                            act.wait_ge(stacked.sem, stacked.before(i))
                    for n, (whole, hi) in enumerate(((qT, QHI), (kT, KHI))):
                        act.wait_ge(at_k.sem, at_k.nth(i, n + 1))
                        act.activation(split[:, hi, :], whole[:, :], ACT.Copy).then_inc(at_hi.sem, 1)
                if s == 14:
                    act.wait_ge(at_lt.sem, at_lt.nth(i))
                    act.activation(ln1T[:, :], bL[:, 0:TOK], ACT.Copy).then_inc(at_ltc.sem, 1)

            def at_turned(s, i):
                for h in due(T_SLOT, s):
                    b = h % 2
                    act.wait_ge(at_t.sem, at_t.nth(i, h + 1))
                    if h >= 2:
                        act.wait_ge(at_pv.sem, at_pv.nth(i, h - 1))
                    elif not first(i):
                        act.wait_ge(at_pv.sem, at_pv.before(i))
                    act.activation(pT[:, b, :], bT[:, 0:3 * P], ACT.Copy).then_inc(at_tc.sem, 1)

            def at_part(s, i):
                for h in due(S_SLOT, s):
                    b = h % 2
                    if h == 0 and not first(i):
                        act.wait_ge(at_r.sem, at_r.before(i))
                    if h >= 2:
                        act.wait_ge(at_t.sem, at_t.nth(i, h - 1))
                    elif not first(i):
                        act.wait_ge(at_t.sem, at_t.before(i))
                    act.wait_ge(at_m.sem, at_m.nth(i, h + 1))
                    act.activation(pe_[:, b, 0:P], bS[b][:, 0:P], ACT.Exp, bias=nm[:, b, 0:1],
                                   accum_out=rsum[:, 0, h:h + 1]).then_inc(at_e.sem, 1)
                    act.activation(pe_[:, b, P:3 * P], bS[b][:, P:3 * P], ACT.Exp, bias=nm[:, b, 1:2],
                                   accum_out=rsum[:, 1, h:h + 1]).then_inc(at_e.sem, 1)
                if s == 10:
                    act.wait_ge(at_ot.sem, at_ot.nth(i))
                    act.activation(aT[:, :], bA[:, 0:TOK], ACT.Copy).then_inc(at_o.sem, 1)
                if s == 13:
                    act.wait_ge(at_nt.sem, at_nt.nth(i))
                    act.activation(ln2T[:, :], bA[:, 0:TOK], ACT.Copy).then_inc(at_ntc.sem, 1)
                if s == 14:
                    act.wait_ge(at_ntc.sem, at_ntc.nth(i))
                    if not first(i):
                        act.wait_ge(mo_h.sem, mo_h.before(i))
                    act.activation(xhi[:, :], ln2T[:, :], ACT.Copy).then_inc(at_xs.sem, 1)
                if s == 14:
                    act.wait_ge(at_td.sem, at_td.nth(i))
                    act.activation(te[:, :], td[:, :], ACT.Exp).then_inc(at_te.sem, 1)

            def mo_part(s, i):
                late = [(1, k) for k in range(HB // 2, HB)]
                parts = [(e, k) for e in due(G1_SLOT, s) for k in range(HB) if (e, k) not in late]
                for e, k in late if s == 3 else parts:
                    if k % 2 == 0:
                        act.wait_ge(mo_h.sem, mo_h.nth(i, 2 * e + k // 2 + 1))
                    if k == 0:
                        if e >= 2:
                            act.wait_ge(mo_y.sem, mo_y.nth(i, e - 1))
                        elif not first(i):
                            act.wait_ge(mo_y.sem, mo_y.before(i))
                    act.activation(hf[:, e % 2, k, :], bH[k // 2][:, (k % 2) * TOK:(k % 2 + 1) * TOK], ACT.Relu,
                                   bias=b1s[:, e, k:k + 1]).then_inc(mo_r.sem, 1)

            def step(l0, at, mo):
                for s in range(SLOTS):
                    if mo is not None and (s == 0 or s >= TAIL):
                        mo_part(s, mo)
                    if l0 is not None and s in (2, 14):
                        l0_part(s, l0)
                    if at is not None:
                        if s != 2:
                            at_turned(s, at)
                    if mo is not None and s == 3:
                        mo_part(s, mo)
                    if at is not None:
                        at_part(s, at)
                    if l0 is not None and s not in (2, 14):
                        l0_part(s, l0)
                    if at is not None and s == 1:
                        at_turned(2, at)
                    if mo is not None and 0 < s < TAIL and s != 3:
                        mo_part(s, mo)
                    if first(l0) and 4 <= s < 4 + EXPERTS:
                        act.wait_ge(ld_1, 16 * EXPERTS)
                        act.activation(w1hi[:, s - 4, :], w1raw[:, s - 4, :], ACT.Copy).then_inc(su_w1h, 1)

            act.wait_ge(ld_c, 64)
            act.wait_ge(ld_w, 48)
            pipeline(act, step)

        @block.tensor
        def _(pe):
            pe.wait_ge(ld_c, 64)
            pe.wait_ge(su_dve, 1)
            pe.matmul(bH[0][:, 0:2 * IMAGES], grp, gmv[:, :, :].rearrange("p i k -> p (i k)"),
                      start=True, stop=True).then_inc(su_pe, 1)
            pe.wait_ge(ld_s, 16)
            for n, (w, a) in enumerate(((W_KVYK, 0), (W_KVYV, 0), (W_Q, 1))):
                mm = pe.matmul(bS[0][:, n * AGENTS:(n + 1) * AGENTS], W[:, w, :], agt[:, a, :], start=True, stop=True)
            mm.then_inc(su_pe, 1)
            pe.wait_ge(su_dve, 5)
            pe.matmul(bH[1][:, 0:IMAGES], grp, gdev[:, :], start=True, stop=True).then_inc(su_pe, 1)
            pe.wait_ge(su_cast, 4)
            pe.wait_ge(su_dve, 10)
            pe.matmul(bS[1][:, 0:P], W[:, W_Q2T, :], kvqd[:, 0, :, :].rearrange("p h m -> p (h m)"), start=True, stop=True)
            pe.matmul(bS[1][:, P:2 * P], bq2b[:, :], kvqd[:, 0, :, :].rearrange("p h m -> p (h m)"), start=True, stop=True)
            pe.matmul(bS[1][:, 2 * P:3 * P], kvqd[:, 1, :, :].rearrange("p h m -> p (h m)"), W[:, W_F1W1, :], start=True, stop=True)
            pe.matmul(bS[1][:, 3 * P:4 * P], W[:, W_KT, :], kvqd[:, 2, :, :].rearrange("p h m -> p (h m)"), start=True, stop=True)\
              .then_inc(su_pe, 1)
            pe.wait_ge(su_act, 1)
            pe.wait_ge(ld_w, 48)

            def l0_part(s, i):
                if s == 0:
                    pe.wait_ge(l0_xg.sem, l0_xg.nth(i))
                    if not first(i):
                        pe.wait_ge(at_k.sem, at_k.before(i))
                    for t in range(TILES):
                        mm = pe.matmul(bL[:, t * P:(t + 1) * P], xg[:, t * P:(t + 1) * P], m1, start=True, stop=True)
                    mm.then_inc(l0_s1.sem, 1)
                    if first(i):
                        pe.matmul(bT[:, 0:1], m2, col[:, B_PE1:B_PE1 + 1], start=True, stop=True).then_inc(su_pe, 1)
                if s == 2:
                    pe.wait_ge(l0_p1.sem, l0_p1.nth(i))
                    for t in range(TILES):
                        mm = pe.transpose(bL[:, t * P:(t + 1) * P], p1[:, t, :], ident)
                    mm.then_inc(l0_pt.sem, 1)
                if s == 3:
                    pe.wait_ge(l0_ptc.sem, l0_ptc.nth(i))
                    pe.matmul(bL[:, 0:TOK], m2, p1T[:, :], start=True, stop=True).then_inc(l0_z.sem, 1)
                if s == 5:
                    pe.wait_ge(l0_zs.sem, l0_zs.nth(i))
                    pe.matmul(bL[:, 0:TOK], W[:, W_F1W2, :], zs[:, :], start=True, stop=True).then_inc(l0_o.sem, 1)
                if s == 6:
                    pe.wait_ge(l0_ot.sem, l0_ot.nth(i))
                    pe.matmul(bL[:, 0:TOK], mkq, oT[:, :], start=True, stop=True).then_inc(l0_s2.sem, 1)
                if s == 7:
                    pe.wait_ge(l0_e2.sem, l0_e2.nth(i))
                    for t in range(TILES):
                        mm = pe.matmul(bL[:, t * P:(t + 1) * P], oT[:, t * P:(t + 1) * P], W[:, W_V, :], start=True, stop=True)
                    mm.then_inc(l0_v.sem, 1)
                if s == 8:
                    pe.wait_ge(l0_p2.sem, l0_p2.nth(i))
                    pe.wait_ge(l0_vx.sem, l0_vx.nth(i))
                    for t in range(TILES):
                        mm = pe.transpose(bL[:, t * P:(t + 1) * P], p2[:, t * P:(t + 1) * P], ident)
                    mm.then_inc(l0_qt.sem, 1)
                if s == 9:
                    pe.wait_ge(l0_qtc.sem, l0_qtc.nth(i))
                    for t in range(TILES):
                        mm = pe.matmul(bL[:, 0:P], vx[:, t, :], p2T[:, t, :], start=(t == 0), stop=(t == TILES - 1))
                    mm.then_inc(l0_f.sem, 1)
                if s == 10:
                    pe.wait_ge(l0_fin.sem, l0_fin.nth(i))
                    pe.matmul(bL[:, 0:AGENTS], W[:, W_F2W1, :], fin[:, :], start=True, stop=True).then_inc(l0_y.sem, 1)
                if s == 11:
                    pe.wait_ge(l0_ys.sem, l0_ys.nth(i))
                    pe.matmul(bL[:, 0:AGENTS], W[:, W_F2W2, :], ys[:, :], start=True, stop=True).then_inc(l0_w.sem, 1)
                if s == 12:
                    pe.wait_ge(l0_x1.sem, l0_x1.nth(i))
                    for t in range(TILES):
                        mm = pe.transpose(bL[:, t * P:(t + 1) * P], x1T[:, t * P:(t + 1) * P], ident)
                    mm.then_inc(at_xt.sem, 1)
                if s == 14:
                    pe.wait_ge(at_xl.sem, at_xl.nth(i))
                    for t in range(TILES):
                        mm = pe.transpose(bL[:, t * P:(t + 1) * P], ln1[:, t, :], ident)
                    mm.then_inc(at_lt.sem, 1)
                if s == 15:
                    pe.wait_ge(at_ltc.sem, at_ltc.nth(i))
                    pe.matmul(bL[:, 0:TOK], W[:, W_AQ, :], ln1T[:, :], start=True, stop=True)
                    pe.matmul(bL[:, TOK:2 * TOK], W[:, W_AK, :], ln1T[:, :], start=True, stop=True)\
                      .then_inc(at_qk.sem, 1)
                if s == 16:
                    if not first(i):
                        pe.wait_ge(at_tc.sem, at_tc.before(i))
                    for t in range(TILES):
                        mm = pe.matmul(bT[:, t * P:(t + 1) * P], ln1T[:, t * P:(t + 1) * P], W[:, W_AV, :],
                                       start=True, stop=True)
                    mm.then_inc(at_v.sem, 1)

            def at_part(s, i):
                for h in due(T_SLOT, s):
                    b = h % 2
                    pe.wait_ge(at_e.sem, at_e.nth(i, 2 * (h + 1)))
                    if h >= 1:
                        pe.wait_ge(at_tc.sem, at_tc.nth(i, h))
                    else:
                        pe.wait_ge(at_vb.sem, at_vb.nth(i))
                    pe.transpose(bT[:, 0:P], pe_[:, b, 0:P], ident)
                    pe.transpose(bT[:, P:2 * P], pe_[:, b, P:2 * P], ident)
                    pe.transpose(bT[:, 2 * P:3 * P], pe_[:, b, 2 * P:3 * P], ident).then_inc(at_t.sem, 1)
                for h in due(S_SLOT, s):
                    b = h % 2
                    if h < KZ:
                        pe.wait_ge(at_kz.sem, at_kz.nth(i, h + 1))
                    else:
                        pe.wait_ge(at_stack[h - KZ].sem, at_stack[h - KZ].nth(i, 16 * STACKED))
                    if h < 2 and not first(i):
                        pe.wait_ge(at_e.sem, at_e.before(i))
                    if h == 1 and not (isinstance(i, int) and i < 2):
                        pe.wait_ge(mo_ob.sem, mo_ob.nth(i - 2, TILES))
                    if h >= 2:
                        pe.wait_ge(at_e.sem, at_e.nth(i, 2 * (h - 1)))
                    if h < KZ:
                        queries, keys = qT[:, :], kz[:, h, :]
                    else:
                        queries, keys = stack[:, h - KZ, 0, :], stack[:, h - KZ, 1, :]
                    pe.matmul(bS[b][:, 0:P], queries[:, 0:P], keys[:, 0:P], start=True, stop=False)
                    pe.matmul(bS[b][:, 0:P], identb[:, :], causalb[:, :], start=False, stop=True)
                    pe.matmul(bS[b][:, P:3 * P], queries[:, P:2 * P], keys, start=True, stop=False)
                    pe.matmul(bS[b][:, 2 * P:3 * P], identb[:, :], causalb[:, :], start=False, stop=True)\
                      .then_inc(at_s.sem, 1)
                if s == 11:
                    pe.wait_ge(at_o.sem, at_o.nth(i))
                    for t in range(TILES):
                        mm = pe.matmul(bA[:, t * P:(t + 1) * P], aT[:, t * P:(t + 1) * P], W[:, W_AO, :],
                                       start=True, stop=True)
                    mm.then_inc(at_w.sem, 1)
                if s == 13:
                    pe.wait_ge(at_n2.sem, at_n2.nth(i, 2))
                    for t in range(TILES):
                        mm = pe.transpose(bA[:, t * P:(t + 1) * P], ln2[:, t, :], ident)
                    mm.then_inc(at_nt.sem, 1)
                if s == 14:
                    pe.wait_ge(at_ntc.sem, at_ntc.nth(i))
                    for t in range(TILES):
                        mm = pe.matmul(bA[:, t * EXPERTS:(t + 1) * EXPERTS], ln2T[:, t * P:(t + 1) * P], wr[:, :],
                                       start=True, stop=True)
                    mm.then_inc(at_l.sem, 1)

            def at_values(s, i):
                for h in due(V_SLOT, s):
                    b = h % 2
                    own = slice(h * DK, (h + 1) * DK)
                    if h == 0:
                        pe.wait_ge(at_vb.sem, at_vb.nth(i))
                        if not first(i):
                            pe.wait_ge(at_lg.sem, at_lg.before(i))
                    pe.wait_ge(at_tc.sem, at_tc.nth(i, h + 1))
                    pe.matmul(bA[:, 0:P][:, own], pT[:, b, 0:P], v[:, 0, own], start=True, stop=True)
                    pe.matmul(bA[:, P:TOK][:, own], pT[:, b, P:TOK], v[:, 0, own], start=True, stop=False)
                    pe.matmul(bA[:, P:TOK][:, own], pT[:, b, TOK:3 * P], v[:, 1, own], start=False, stop=True)\
                      .then_inc(at_pv.sem, 1)

            def at_turn(s, i):
                if s == 10:
                    pe.wait_ge(at_on.sem, at_on.nth(i))
                    for t in range(TILES):
                        mm = pe.transpose(bA[:, t * P:(t + 1) * P], ao[:, t, :], ident)
                    mm.then_inc(at_ot.sem, 1)

            def mo_first(e, i):
                if e == 0:
                    pe.wait_ge(at_xl2.sem, at_xl2.nth(i))
                for k in range(HB):
                    if k % 2 == 0:
                        if e >= 1:
                            pe.wait_ge(mo_r.sem, mo_r.nth(i, HB * (e - 1) + k + 2))
                        elif not first(i):
                            pe.wait_ge(mo_r.sem, mo_r.before(i))
                    hk = bH[k // 2][:, (k % 2) * TOK:(k % 2 + 1) * TOK]
                    wk = slice(k * P, (k + 1) * P)
                    pe.matmul(hk, w1hi[:, e, wk], xhi[:, :], start=True, stop=False)
                    pe.matmul(hk, w1hi[:, e, wk], xlo[:, :], start=False, stop=False)
                    mm = pe.matmul(hk, w1lo[:, e, wk], xhi[:, :], start=False, stop=True)
                    if k % 2 == 1:
                        mm.then_inc(mo_h.sem, 1)

            def mo_second(e, i, at, l0):
                earlier = [n for n in range(e) if y_bank(n) is y_bank(e)]
                if earlier:
                    pe.wait_ge(mo_acc.sem, mo_acc.nth(i, summed(earlier[-1])))
                elif e == 0 and not first(i):
                    pe.wait_ge(mo_acc.sem, mo_acc.before(i))
                if e == 5 and at is not None:
                    pe.wait_ge(at_e.sem, at_e.nth(at, 2 * HEADS))
                pe.wait_ge(mo_r.sem, mo_r.nth(i, HB * (e + 1)))
                for t in range(TILES):
                    for k in range(HB):
                        if l0 is not None and MIDWAY.get(e) == (t, k):
                            l0_part(G2_SLOT[e], l0)
                        mm = pe.matmul(y_bank(e)[:, t * P:(t + 1) * P], hf[:, e % 2, k, t * P:(t + 1) * P], w2s[:, e, k, :],
                                       start=(k == 0), stop=(k == HB - 1))
                mm.then_inc(mo_y.sem, 1)

            def mo_part(s, i, at, l0):
                for e in due(G2_SLOT, s):
                    mo_second(e, i, at, l0)
                for e in due(G1_SLOT, s):
                    mo_first(e, i)

            def keep_warm(n):
                for _ in range(n):
                    pe.matmul(bH[1][:, 0:P], identb[:, :], causalb[:, :], start=True, stop=True)

            def step(l0, at, mo):
                for s in range(SLOTS):
                    if mo is None:
                        keep_warm(WARM_L0 if at is None else WARM_AT)
                    if l0 is not None and s == 15:
                        l0_part(s, l0)
                    if mo is not None and (s == 0 or s >= TAIL):
                        mo_part(s, mo, at, l0)
                    if l0 is not None and (s == 11 or s == 14 and mo is None):
                        l0_part(s, l0)
                    if at is not None:
                        at_values(s, at)
                        at_part(s, at)
                    if l0 is not None and s not in (2, 5, 11, 14, 15):
                        l0_part(s, l0)
                    if mo is not None and 0 < s < TAIL:
                        mo_part(s, mo, at, l0)
                    if l0 is not None and (s == 5 or s == 2 and mo is None):
                        l0_part(s, l0)
                    if at is not None:
                        at_turn(s, at)

            def weights_ready():
                pe.wait_ge(ld_2, 16 * EXPERTS)
                pe.wait_ge(su_w1, EXPERTS)

            pipeline(pe, step, weights_ready)

        @block.vector
        def _(dve):
            done = [0]

            def after(ins):
                done[0] += 1
                ins.then_inc(su_dve, 1)
                dve.wait_ge(su_dve, done[0])

            for n in range(IMAGES):
                if n % (IMAGES // 2) == 0:
                    dve.wait_ge(ld_x[n // (IMAGES // 2)], 16)
                last = dve.bn_stats(gst[:, n, :], x_all[:, n * TOK:(n + 1) * TOK])
            last.then_inc(su_cast, 1)
            dve.wait_ge(ld_c, 64)
            dve.tensor_copy(identb[:, :], ident).then_inc(su_cast, 1)
            dve.tensor_copy(causalb[:, :], cst[:, C_CAUSAL:C_CAUSAL + P]).then_inc(su_cast, 1)
            dve.wait_ge(su_cast, 3)
            dve.tensor_copy(bq2b[:, :], col[:, B_Q2:B_Q2 + 1].broadcast_to([P, P])).then_inc(su_cast, 1)
            for n in range(IMAGES):
                last = dve.bn_aggr(gmv[:, n, :], gst[:, n, :])
            after(last)
            dve.wait_ge(su_pe, 1)
            after(dve.tensor_copy(gmean[:, :], bH[0][:, 0:2 * IMAGES].rearrange("p (i k) -> p i k", k=2)[:, :, 0]))
            after(dve.tensor_tensor(gdev[:, :], gmv[:, :, 0], gmean[:, :], ALU.subtract))
            after(dve.tensor_tensor(gvar[:, :], gdev[:, :], gdev[:, :], ALU.mult))
            after(dve.tensor_tensor(gdev[:, :], gvar[:, :], gmv[:, :, 1], ALU.add))
            dve.wait_ge(su_pe, 2)
            after(dve.tensor_tensor(kvq[:, :, :], bS[0][:, 0:3 * AGENTS].rearrange("p (n m) -> p n m", n=3),
                                    col[:, B_KYK:B_Q + 1].unsqueeze(2).broadcast_to([P, 3, AGENTS]), ALU.add))
            dve.wait_ge(su_pe, 3)
            after(dve.tensor_scalar(gvar[:, :], bH[1][:, 0:IMAGES], 1e-5, None, ALU.add))
            for n, mask in enumerate((bds, bd, bds)):
                after(dve.tensor_tensor(kvqd[:, n, :, :], kvq[:, n, :].unsqueeze(1).broadcast_to([P, HEADS, AGENTS]),
                                        mask.unsqueeze(2).broadcast_to([P, HEADS, AGENTS]), ALU.mult))
            dve.wait_ge(su_pow, 1)
            after(dve.scalar_tensor_tensor(out=gn[:, :, 1], in0=gmean[:, :], scalar=-1.0, in1=gn[:, :, 0],
                                           op0=ALU.mult, op1=ALU.mult))

            def mlp_bias():
                dve.wait_ge(su_pe, 5)
                after(dve.tensor_tensor(zb[:, :], bT[:, 0:1], col[:, B_F1B1:B_F1B1 + 1], ALU.add))

            def l0_late(s, i):
                if s == 0:
                    dve.tensor_copy(gni[:, :], gn[:, bass.ds(i, 1), :].rearrange("p a k -> p (a k)")).then_inc(l0_gn.sem, 1)
                    x_i = x_all[:, bass.ds(i * TOK, TOK)]
                    if not first(i):
                        dve.wait_ge(l0_s1.sem, l0_s1.before(i))
                    dve.wait_ge(l0_gn.sem, l0_gn.nth(i))
                    dve.tensor_scalar(xg[:, :], x_i, gni[:, 0:1], gni[:, 1:2], ALU.mult, ALU.add)\
                       .then_inc(l0_xg.sem, 1)
                if s == 2:
                    egrouped = e1[:, :, :].rearrange("p t (h m) -> p (t h) m", m=AGENTS)
                    dve.wait_ge(l0_e1.sem, l0_e1.nth(i))
                    dve.tensor_reduce(e1s[:, :], egrouped, AX.X, ALU.add).then_inc(l0_sum.sem, 1)
                    dve.wait_ge(l0_sum.sem, l0_sum.nth(i))
                    dve.reciprocal(e1r[:, :], e1s[:, :]).then_inc(l0_r1.sem, 1)
                    if not first(i):
                        dve.wait_ge(l0_pt.sem, l0_pt.before(i))
                    dve.wait_ge(l0_r1.sem, l0_r1.nth(i))
                    dve.tensor_tensor(p1[:, :, :].rearrange("p t (h m) -> p (t h) m", m=AGENTS), egrouped,
                                      e1r[:, :].unsqueeze(2).broadcast_to([P, TILES * HEADS, AGENTS]),
                                      ALU.mult).then_inc(l0_p1.sem, 1)
                if s == 3:
                    if not first(i):
                        dve.wait_ge(l0_base.sem, l0_base.before(i))
                    dve.wait_ge(l0_xg.sem, l0_xg.nth(i))
                    dve.tensor_tensor(xx[:, :], x_all[:, bass.ds(i * TOK, TOK)], xg[:, :], ALU.add).then_inc(l0_xx.sem, 1)
                if s == 4:
                    dve.wait_ge(l0_ez.sem, l0_ez.nth(i))
                    dve.tensor_scalar(za[:, :], ez[:, :], 1.0, None, ALU.add).then_inc(l0_za.sem, 1)
                    dve.wait_ge(l0_za.sem, l0_za.nth(i))
                    dve.reciprocal(zr[:, :], za[:, :]).then_inc(l0_zr.sem, 1)
                    if not first(i):
                        dve.wait_ge(l0_o.sem, l0_o.before(i))
                    dve.wait_ge(l0_zr.sem, l0_zr.nth(i))
                    dve.scalar_tensor_tensor(out=zs[:, :], in0=bL[:, 0:TOK], scalar=zb[:, 0:1], in1=zr[:, :],
                                             op0=ALU.add, op1=ALU.mult).then_inc(l0_zs.sem, 1)
                if s == 7:
                    dve.wait_ge(l0_e2.sem, l0_e2.nth(i))
                    dve.reciprocal(s2r[:, :], s2s[:, :]).then_inc(l0_r2.sem, 1)
                    if not first(i):
                        dve.wait_ge(l0_qt.sem, l0_qt.before(i))
                    dve.wait_ge(l0_r2.sem, l0_r2.nth(i))
                    dve.tensor_scalar(p2[:, :], e2[:, :], s2r[:, 0:1], col[:, B_PE2:B_PE2 + 1], ALU.mult, ALU.add)\
                       .then_inc(l0_p2.sem, 1)
                if s == 11:
                    dve.wait_ge(l0_ey.sem, l0_ey.nth(i))
                    dve.tensor_scalar(ya[:, :], ey[:, :], 1.0, None, ALU.add).then_inc(l0_ya.sem, 1)
                    dve.wait_ge(l0_ya.sem, l0_ya.nth(i))
                    dve.reciprocal(yr[:, :], ya[:, :]).then_inc(l0_yr.sem, 1)
                    if not first(i):
                        dve.wait_ge(l0_w.sem, l0_w.before(i))
                    dve.wait_ge(l0_yr.sem, l0_yr.nth(i))
                    dve.scalar_tensor_tensor(out=ys[:, :], in0=bL[:, 0:AGENTS], scalar=col[:, B_F2B1:B_F2B1 + 1],
                                             in1=yr[:, :], op0=ALU.add, op1=ALU.mult).then_inc(l0_ys.sem, 1)
                if s == 13:
                    if not first(i):
                        dve.wait_ge(at_lt.sem, at_lt.before(i))
                    dve.wait_ge(at_rs.sem, at_rs.nth(i))
                    for t in range(TILES):
                        dve.tensor_scalar(ln1[:, t, :], bL[:, t * P:(t + 1) * P], lmv[:, t, 0:1], lrs[:, t:t + 1],
                                          ALU.subtract, ALU.mult).then_inc(at_ln.sem, 1)
                    if not first(i):
                        dve.wait_ge(at_tb.sem, at_tb.before(i))
                    dve.wait_ge(at_ln.sem, at_ln.nth(i, 2))
                    dve.tensor_tensor(xl[:, :, :], tiles(bL[:, 0:TOK]), ln1[:, :, :], ALU.add).then_inc(at_xl.sem, 1)

            def at_first(s, i):
                if s == 0:
                    if not first(i):
                        dve.wait_ge(at_pv.sem, at_pv.before(i))
                    dve.wait_ge(at_v.sem, at_v.nth(i))
                    dve.tensor_tensor(v[:, :, :], tiles(bT[:, 0:TOK]),
                                      row[:, R_BAV, :].unsqueeze(1).broadcast_to([P, TILES, P]), ALU.add)\
                       .then_inc(at_vb.sem, 1)
                if s == 9:
                    dve.wait_ge(at_e.sem, at_e.nth(i, 2 * HEADS))
                    dve.reciprocal(rinv[:, :, :], rsum[:, :, :]).then_inc(at_r.sem, 1)
                if s == 10:
                    if not first(i):
                        dve.wait_ge(at_ot.sem, at_ot.before(i))
                    dve.wait_ge(at_r.sem, at_r.nth(i))
                    dve.wait_ge(at_pv.sem, at_pv.nth(i, HEADS))
                    dve.tensor_tensor(ao[:, :, :].rearrange("p t (h d) -> p (t h) d", d=DK),
                                      bA[:, 0:TOK].rearrange("p (n d) -> p n d", d=DK),
                                      rinv[:, :, :].rearrange("p t h -> p (t h)").unsqueeze(2)
                                      .broadcast_to([P, TILES * HEADS, DK]), ALU.mult).then_inc(at_on.sem, 1)

            def at_late(s, i):
                if s == 12:
                    if not first(i):
                        dve.wait_ge(at_nt.sem, at_nt.before(i))
                    dve.wait_ge(at_nrs.sem, at_nrs.nth(i))
                    for t in range(TILES):
                        dve.tensor_scalar(ln2[:, t, :], t2[:, t, :], nmv[:, t, 0:1], nrs[:, t:t + 1],
                                          ALU.subtract, ALU.mult).then_inc(at_n2.sem, 1)

            def l0_part(s, i):
                if s == 0:
                    dve.wait_ge(l0_s1.sem, l0_s1.nth(i))
                    dve.tensor_tensor(s1[:, :, :], tiles(bL[:, 0:TOK]), c1.unsqueeze(1).broadcast_to([P, TILES, P]),
                                      ALU.add).then_inc(l0_s1b.sem, 1)
                    dve.wait_ge(l0_s1b.sem, l0_s1b.nth(i))
                    grouped = s1[:, :, :].rearrange("p t (h m) -> p (t h) m", m=AGENTS)
                    dve.tensor_reduce(s1m[:, :], grouped, AX.X, ALU.max).then_inc(l0_m1.sem, 1)
                    dve.wait_ge(l0_m1.sem, l0_m1.nth(i))
                    dve.tensor_tensor(s1c[:, :, :].rearrange("p t (h m) -> p (t h) m", m=AGENTS), grouped,
                                      s1m[:, :].unsqueeze(2).broadcast_to([P, TILES * HEADS, AGENTS]),
                                      ALU.subtract).then_inc(l0_s1c.sem, 1)
                if s == 3:
                    dve.wait_ge(l0_z.sem, l0_z.nth(i))
                    dve.tensor_scalar(zc[:, :], bL[:, 0:TOK], zb[:, 0:1], -LOW, ALU.add, ALU.max)\
                       .then_inc(l0_zc.sem, 1)
                if s == 5:
                    if not first(i):
                        dve.wait_ge(l0_v.sem, l0_v.before(i))
                    dve.wait_ge(l0_o.sem, l0_o.nth(i))
                    dve.scalar_tensor_tensor(out=oT[:, :], in0=bL[:, 0:TOK], scalar=col[:, B_F1B2:B_F1B2 + 1],
                                             in1=xg[:, :], op0=ALU.add, op1=ALU.add).then_inc(l0_ot.sem, 1)
                if s == 6:
                    dve.wait_ge(l0_s2.sem, l0_s2.nth(i))
                    dve.tensor_reduce(s2m[:, :], bL[:, 0:TOK], AX.X, ALU.max, negate=True).then_inc(l0_m2.sem, 1)
                if s == 7:
                    if not first(i):
                        dve.wait_ge(l0_f.sem, l0_f.before(i))
                    dve.wait_ge(l0_v.sem, l0_v.nth(i))
                    dve.tensor_tensor(vx[:, :, :], tiles(bL[:, 0:TOK]),
                                      row[:, R_BV, :].unsqueeze(1).broadcast_to([P, TILES, P]), ALU.add)\
                       .then_inc(l0_vx.sem, 1)
                if s == 9:
                    dve.wait_ge(l0_f.sem, l0_f.nth(i))
                    dve.tensor_tensor(fm[:, :, :], bL[:, 0:P].rearrange("p (h m) -> p h m", m=AGENTS),
                                      bd.unsqueeze(2).broadcast_to([P, HEADS, AGENTS]), ALU.mult).then_inc(l0_fm.sem, 1)
                    if not first(i):
                        dve.wait_ge(l0_y.sem, l0_y.before(i))
                    dve.wait_ge(l0_fm.sem, l0_fm.nth(i))
                    dve.tensor_reduce(fin[:, :], fm[:, :, :].rearrange("p h m -> p m h"), AX.X, ALU.add)\
                       .then_inc(l0_fin.sem, 1)
                if s == 10:
                    dve.wait_ge(l0_y.sem, l0_y.nth(i))
                    dve.tensor_scalar(yc[:, :], bL[:, 0:AGENTS], col[:, B_F2B1:B_F2B1 + 1], -LOW, ALU.add, ALU.max)\
                       .then_inc(l0_yc.sem, 1)
                if s == 11:
                    dve.wait_ge(l0_w.sem, l0_w.nth(i))
                    dve.tensor_scalar(fe[:, :, :], bL[:, 0:AGENTS].unsqueeze(2).broadcast_to([P, AGENTS, CELL]),
                                      col[:, B_F2B2:B_F2B2 + 1], None, ALU.add).then_inc(l0_fe.sem, 1)
                    if not first(i):
                        dve.wait_ge(at_xt.sem, at_xt.before(i))
                    dve.wait_ge(l0_base.sem, l0_base.nth(i))
                    dve.wait_ge(l0_fe.sem, l0_fe.nth(i))
                    dve.tensor_tensor(x1T[:, :].rearrange("p (a y x) -> p a y x", a=CELL, y=CELL),
                                      base[:, :].rearrange("p (a y x) -> p a y x", a=CELL, y=CELL),
                                      fe[:, :, :].rearrange("p (a b) x -> p a (b x)", a=CELL).unsqueeze(2)
                                      .broadcast_to([P, CELL, CELL, SIDE]), ALU.add).then_inc(l0_x1.sem, 1)
                if s == 12:
                    dve.wait_ge(at_xt.sem, at_xt.nth(i))
                    for t in range(TILES):
                        dve.bn_stats(lst[:, t, :], bL[:, t * P:(t + 1) * P]).then_inc(at_st.sem, 1)
                    dve.wait_ge(at_st.sem, at_st.nth(i, 2))
                    dve.sem_inc(gate[0], 1)
                    for t in range(TILES):
                        dve.bn_aggr(lmv[:, t, :], lst[:, t, :]).then_inc(at_mv.sem, 1)
                    dve.wait_ge(at_mv.sem, at_mv.nth(i, 2))
                    dve.tensor_scalar(lve[:, :], lmv[:, :, 1], 1e-5, None, ALU.add).then_inc(at_mv.sem, 1)
                if s == 15:
                    if not first(i):
                        dve.wait_ge(at_s.sem, at_s.before(i))
                        dve.wait_ge(at_lo.sem, at_lo.before(i))
                    dve.wait_ge(at_qk.sem, at_qk.nth(i))
                    dve.tensor_scalar(qT[:, :], bL[:, 0:TOK], col[:, B_AQ:B_AQ + 1], SCALE, ALU.add, ALU.mult)\
                       .then_inc(at_k.sem, 1)
                    dve.tensor_scalar(kT[:, :], bL[:, TOK:2 * TOK], col[:, B_AK:B_AK + 1], None, ALU.add)\
                       .then_inc(at_k.sem, 1)
                    dve.wait_ge(at_k.sem, at_k.nth(i, 2))
                    for h in range(KZ):
                        dve.tensor_scalar(kz[:, h, :], kT[:, :], bd[:, h:h + 1], None, ALU.mult).then_inc(at_kz.sem, 1)

            def at_part(s, i):
                for h in due(S_SLOT, s):
                    b = h % 2
                    dve.wait_ge(at_s.sem, at_s.nth(i, h + 1))
                    dve.tensor_reduce(nm[:, b, 0:1], bS[b][:, 0:P], AX.X, ALU.max, negate=True)
                    dve.tensor_reduce(nm[:, b, 1:2], bS[b][:, P:3 * P], AX.X, ALU.max, negate=True)\
                       .then_inc(at_m.sem, 1)
                if s == 11:
                    if not first(i):
                        dve.wait_ge(mo_res.sem, mo_res.nth(i - 1, 1))
                    dve.wait_ge(at_tb.sem, at_tb.nth(i))
                    dve.wait_ge(at_w.sem, at_w.nth(i))
                    dve.tensor_tensor(t2[:, :, :], tiles(bA[:, 0:TOK]), tb[:, :, :], ALU.add).then_inc(at_t2.sem, 1)
                    dve.wait_ge(at_t2.sem, at_t2.nth(i))
                    for t in range(TILES):
                        dve.bn_stats(nst[:, t, :], t2[:, t, :]).then_inc(at_nst.sem, 1)
                    dve.wait_ge(at_nst.sem, at_nst.nth(i, 2))
                    dve.sem_inc(gate[0], 1)
                    for t in range(TILES):
                        dve.bn_aggr(nmv[:, t, :], nst[:, t, :]).then_inc(at_nmv.sem, 1)
                    dve.wait_ge(at_nmv.sem, at_nmv.nth(i, 2))
                    dve.tensor_scalar(nve[:, :], nmv[:, :, 1], 1e-5, None, ALU.add).then_inc(at_nmv.sem, 1)
                if s == 14:
                    dve.wait_ge(at_l.sem, at_l.nth(i))
                    dve.tensor_copy(lg[:, :, :].rearrange("p t e -> p (t e)"), bA[:, 0:TILES * EXPERTS])\
                       .then_inc(at_lg.sem, 1)
                    dve.wait_ge(at_lg.sem, at_lg.nth(i))
                    dve.sem_inc(gate[0], 1)
                    for t in range(TILES):
                        dve.max(top[:, t, :], lg[:, t, :]).then_inc(at_top.sem, 1)
                    dve.wait_ge(at_top.sem, at_top.nth(i, 2))
                    dve.tensor_tensor(td[:, :], top[:, :, 1], top[:, :, 0], ALU.subtract).then_inc(at_td.sem, 1)
                    for t in range(TILES):
                        dve.max_index(tix[:, t, :], top[:, t, :], lg[:, t, :]).then_inc(at_tix.sem, 1)
                    dve.wait_ge(at_tix.sem, at_tix.nth(i, 2))
                    dve.tensor_copy(tif[:, :, :], tix[:, :, 0:2]).then_inc(at_tif.sem, 1)
                    dve.wait_ge(at_tif.sem, at_tif.nth(i))
                    for k in range(2):
                        dve.tensor_tensor(pick[:, k, :, :], iota.unsqueeze(1).broadcast_to([P, TILES, EXPERTS]),
                                          tif[:, :, k:k + 1].broadcast_to([P, TILES, EXPERTS]), ALU.is_equal)\
                           .then_inc(at_pick.sem, 1)

            def mo_part(s, i):
                if s == 0:
                    dve.wait_ge(at_te.sem, at_te.nth(i))
                    dve.tensor_scalar(ta[:, :], te[:, :], 1.0, None, ALU.add).then_inc(at_ta.sem, 1)
                    dve.wait_ge(at_ta.sem, at_ta.nth(i))
                    dve.reciprocal(tw[:, :, 0], ta[:, :]).then_inc(at_tw.sem, 1)
                    dve.wait_ge(at_tw.sem, at_tw.nth(i, 1))
                    dve.tensor_tensor(tw[:, :, 1], te[:, :], tw[:, :, 0], ALU.mult).then_inc(at_tw.sem, 1)
                    dve.wait_ge(at_tw.sem, at_tw.nth(i, 2))
                    for k in range(2):
                        dve.tensor_tensor(part[:, k, :, :], pick[:, k, :, :],
                                          tw[:, :, k:k + 1].broadcast_to([P, TILES, EXPERTS]), ALU.mult)\
                           .then_inc(at_share.sem, 1)
                    if not first(i):
                        dve.wait_ge(mo_res.sem, mo_res.before(i))
                    dve.wait_ge(at_share.sem, at_share.nth(i, 2))
                    dve.tensor_tensor(comb[:, :, :], part[:, 0, :, :], part[:, 1, :, :], ALU.add)\
                       .then_inc(at_comb.sem, 1)
                for e in due(G2_SLOT, s):
                    dve.wait_ge(mo_y.sem, mo_y.nth(i, e + 1))
                    total, done = (acc, mo_acc) if e < EXPERTS - 1 else (ob, mo_ob)
                    if e == 0:
                        dve.wait_ge(at_comb.sem, at_comb.nth(i))
                        for t in range(TILES):
                            dve.tensor_scalar(acc[:, t, :], y_bank(e)[:, t * P:(t + 1) * P], comb[:, t, e:e + 1], None,
                                              ALU.mult).then_inc(mo_acc.sem, 1)
                        continue
                    if e == EXPERTS - 1 and not first(i):
                        dve.wait_ge(mo_out.sem, mo_out.before(i))
                    dve.wait_ge(mo_acc.sem, mo_acc.nth(i, summed(e - 1)))
                    for t in range(TILES):
                        dve.scalar_tensor_tensor(out=total[:, t, :], in0=y_bank(e)[:, t * P:(t + 1) * P],
                                                 scalar=comb[:, t, e:e + 1], in1=acc[:, t, :],
                                                 op0=ALU.mult, op1=ALU.add).then_inc(done.sem, 1)
                    if e == RES_AT:
                        dve.wait_ge(mo_res.sem, mo_res.nth(i, EXPERTS))
                        dve.wait_ge(mo_acc.sem, mo_acc.nth(i, summed(e) - 1))
                        dve.tensor_tensor(acc[:, :, :], acc[:, :, :], res[:, :, :], ALU.add).then_inc(mo_acc.sem, 1)

            def step(l0, at, mo):
                for s in range(SLOTS):
                    if l0 is not None and s in (TAIL, 0):
                        l0_late(s, l0)
                    if l0 is not None and s == 15:
                        l0_part(s, l0)
                    if at is not None:
                        at_first(s, at)
                    if mo is not None and s >= TAIL:
                        mo_part(s, mo)
                    if l0 is not None and s in (TAIL, 12):
                        l0_part(s, l0)
                    if l0 is not None and s not in (TAIL, 0, 4):
                        l0_late(s, l0)
                    if mo is not None and s == 0:
                        mo_part(s, mo)
                    if at is not None:
                        at_late(s, at)
                        at_part(s, at)
                    if l0 is not None and s == 4:
                        l0_late(s, l0)
                    if l0 is not None and s not in (TAIL, 12, 15):
                        l0_part(s, l0)
                    if mo is not None and 0 < s < TAIL:
                        mo_part(s, mo)
                    if first(l0) and s == 0:
                        mlp_bias()

            pipeline(dve, step)


def kernel(**inputs):
    import numpy as np
    import concourse.bacc as bacc
    from concourse.bass_utils import run_bass_kernel_spmd

    L0 = {k[len("L0_conv_"):]: np.asarray(v) for k, v in inputs.items() if k.startswith("L0_conv_")}
    A = {k[len("L1_attn_"):]: np.asarray(v) for k, v in inputs.items() if k.startswith("L1_attn_")}
    M = {k[len("L1_ffn_"):]: np.asarray(v) for k, v in inputs.items() if k.startswith("L1_ffn_")}

    p = np.arange(P)
    consts = np.zeros((P, C_N), np.float32)
    consts[:, C_ID:C_ID + P] = np.eye(P)
    consts[:, C_GRP:C_GRP + P] = (p[:, None] // GROUP == p[None, :] // GROUP) * (1.0 / GROUP)
    consts[:, C_CAUSAL:C_CAUSAL + P] = np.where(p[None, :] > p[:, None], -1e9, 0.0)
    own = p[:, None] // DK == np.arange(HEADS)[None, :]
    consts[:, C_BD:C_BD + HEADS] = own
    consts[:, C_BDS:C_BDS + HEADS] = own * SCALE
    consts[:, C_IOTA:C_IOTA + EXPERTS] = np.arange(EXPERTS)
    consts[:, C_POW:C_POW + 2] = -0.5

    by_kind = A["W_in"].reshape(C, HEADS, 3, DK).transpose(2, 0, 1, 3).reshape(3, C, C)
    bias_by_kind = A["b_in"].reshape(HEADS, 3, DK).transpose(1, 0, 2).reshape(3, C)
    weights = np.stack([
        L0["w_kvy"][:, :C], L0["w_kvy"][:, C:], L0["w_q"], L0["w_q2"].T, L0["f1w1"], L0["w_kvx"][:, :C].T,
        L0["f1w2"], L0["w_kvx"][:, C:], L0["f2w1"], L0["f2w2"], by_kind[0], by_kind[1], by_kind[2], A["W_out"]],
        axis=1)
    cols = np.stack([
        L0["b_kvy"][:C], L0["b_kvy"][C:], L0["b_q"], L0["pe1"].reshape(P), L0["pe2"].reshape(P), L0["f1b1"],
        L0["f1b2"], L0["f2b1"], L0["f2b2"], bias_by_kind[0], bias_by_kind[1], L0["b_q2"]], axis=1)
    rows = np.concatenate([L0["b_kvx"][C:], bias_by_kind[2], A["b_out"]])
    agents = np.stack([L0["learnable_kv"][0].T, L0["learnable_q"][0].T], axis=1)
    arrays = {
        "xT": np.asarray(inputs["x"]).reshape(IMAGES * TOK, C).T, "consts": consts, "weights": weights,
        "cols": cols, "rows": rows, "agents": agents, "w_router": M["W_router"], "w1": M["W1"],
        "b1": M["b1"].reshape(EXPERTS, HB, P).transpose(2, 0, 1), "w2": M["W2"], "b2": M["b2"].reshape(-1)}

    nc = bacc.Bacc("TRN2", target_bir_lowering=False, num_devices=1)
    args = {}
    for name in arrays:
        a = arrays[name] = np.ascontiguousarray(arrays[name])
        args[name] = nc.dram_tensor(name, a.shape, mybir.dt.from_np(a.dtype), kind="ExternalInput").ap()
    out = nc.dram_tensor("out", (IMAGES * TILES, P, C), F32, kind="ExternalOutput").ap()
    hybrid_block(nc, out=out, **args)
    r = run_bass_kernel_spmd(nc, [arrays], core_ids=[0])
    return r.results[0]["out"].reshape(IMAGES, SIDE, SIDE, C)
```
